# Optimizing a Trainium2 kernel written in Bass

```python
import numpy as np
import jax
import jax.numpy as jnp

def _softmax(x, axis=-1):
    return jax.nn.softmax(x, axis=axis)

def _gelu(x):
    return jax.nn.gelu(x, approximate=True)

def _silu(x):
    return jax.nn.silu(x)

def _sigmoid(x):
    return jax.nn.sigmoid(x)

def _layernorm(x, axis=-1, eps=1e-05):
    m = jnp.mean(x, axis=axis, keepdims=True)
    v = jnp.var(x, axis=axis, keepdims=True)
    return (x - m) / jnp.sqrt(v + eps)

def _scatter_add(tgt, idx, src, axis=0):
    return tgt.at[idx].add(src)

def _segment_sum(src, seg, n):
    return jax.ops.segment_sum(src, seg, n)
kernel_name = 'mk_recurrent_d1_jaxref_r8_98e8c6'

def setup_inputs(seed: int=0):
    np.random.seed(seed)
    _w = jnp.asarray

    def _L0_attn_setup():
        import jax, jax.numpy as jnp
        import numpy as np
        B, L, H, I, K, G = (2, 512, 128, 256, 4, 8)
        EPS = 1e-05

        def _layernorm(x, g, b):
            m = x.mean(-1, keepdims=True)
            v = jnp.var(x, axis=-1, keepdims=True)
            return (x - m) * jax.lax.rsqrt(v + EPS) * g + b
        key = jax.random.key(seed)
        ks = jax.random.split(key, 8)
        s = 0.02
        return {'hidden_states': jax.random.normal(ks[0], (B, L, H), jnp.float32), 'in_proj_w': jax.random.normal(ks[1], (2 * I, H), jnp.float32) * s, 'conv_w': jax.random.normal(ks[2], (I, I // G, K), jnp.float32) * s, 'conv_b': jax.random.normal(ks[3], (I,), jnp.float32) * s, 'ln_g': jnp.ones((I,), jnp.float32), 'ln_b': jnp.zeros((I,), jnp.float32), 'fc_w': jax.random.normal(ks[4], (H, I), jnp.float32) * s, 'fc_b': jnp.zeros((H,), jnp.float32), 'cproj_w': jax.random.normal(ks[5], (I, H), jnp.float32) * s, 'cproj_b': jnp.zeros((I,), jnp.float32), 'out_w': jax.random.normal(ks[6], (H, I), jnp.float32) * s}
    _L0_attn_in = _L0_attn_setup()

    def _L0_ffn_setup():
        import jax, jax.numpy as jnp
        import numpy as np
        B, N, D, H, E = (4, 128, 128, 16, 8)
        DK = D // H
        HID = 4 * D
        EPS = 1e-05

        def _layernorm(x, w, b):
            m = jnp.mean(x, axis=-1, keepdims=True)
            v = jnp.mean(jnp.square(x - m), axis=-1, keepdims=True)
            return (x - m) * jax.lax.rsqrt(v + EPS) * w + b

        def _msa(x, w_qkv, w_proj):
            b, n, d = x.shape
            qkv = (x @ w_qkv).reshape(b, n, 3, H, DK)
            q = qkv[:, :, 0].transpose(0, 2, 1, 3)
            k = qkv[:, :, 1].transpose(0, 2, 1, 3)
            v = qkv[:, :, 2].transpose(0, 2, 1, 3)
            attn = jnp.einsum('bhnd,bhmd->bhnm', q, k) * (1.0 / np.sqrt(DK))
            attn = jax.nn.softmax(attn, axis=-1)
            y = jnp.einsum('bhnm,bhmd->bhnd', attn, v)
            y = y.transpose(0, 2, 1, 3).reshape(b, n, d)
            return y @ w_proj

        def _moe_mlp(x, gate_w, gate_b, w1, w2):
            b, n, d = x.shape
            xf = x.reshape(b * n, d)
            logits = xf @ gate_w + gate_b
            one_hot = jax.nn.one_hot(jnp.argmax(logits, axis=-1), E, dtype=xf.dtype)
            h = jax.nn.gelu(jnp.einsum('td,edh->teh', xf, w1), approximate=True)
            y = jnp.einsum('teh,ehd->ted', h, w2)
            out = jnp.einsum('te,ted->td', one_hot, y)
            return out.reshape(b, n, d)
        key = jax.random.key(seed)
        ks = jax.random.split(key, 8)
        s = 0.02
        return {'x': jax.random.normal(ks[0], (B, N, D), jnp.float32), 'ln1_w': jnp.ones((D,), jnp.float32), 'ln1_b': jnp.zeros((D,), jnp.float32), 'w_qkv': jax.random.normal(ks[1], (D, 3 * D), jnp.float32) * s, 'w_proj': jax.random.normal(ks[2], (D, D), jnp.float32) * s, 'ln2_w': jnp.ones((D,), jnp.float32), 'ln2_b': jnp.zeros((D,), jnp.float32), 'gate_w': jax.random.normal(ks[3], (D, E), jnp.float32) * s, 'gate_b': jnp.zeros((E,), jnp.float32), 'w1': jax.random.normal(ks[4], (E, D, HID), jnp.float32) * s, 'w2': jax.random.normal(ks[5], (E, HID, D), jnp.float32) * s}
    _L0_ffn_in = _L0_ffn_setup()
    _d = {'L0_attn_hidden_states': _L0_attn_in['hidden_states'], 'L0_attn_in_proj_w': _L0_attn_in['in_proj_w'], 'L0_attn_conv_w': _L0_attn_in['conv_w'], 'L0_attn_conv_b': _L0_attn_in['conv_b'], 'L0_attn_ln_g': _L0_attn_in['ln_g'], 'L0_attn_ln_b': _L0_attn_in['ln_b'], 'L0_attn_fc_w': _L0_attn_in['fc_w'], 'L0_attn_fc_b': _L0_attn_in['fc_b'], 'L0_attn_cproj_w': _L0_attn_in['cproj_w'], 'L0_attn_cproj_b': _L0_attn_in['cproj_b'], 'L0_attn_out_w': _L0_attn_in['out_w'], 'L0_ffn_ln1_w': _L0_ffn_in['ln1_w'], 'L0_ffn_ln1_b': _L0_ffn_in['ln1_b'], 'L0_ffn_w_qkv': _L0_ffn_in['w_qkv'], 'L0_ffn_w_proj': _L0_ffn_in['w_proj'], 'L0_ffn_ln2_w': _L0_ffn_in['ln2_w'], 'L0_ffn_ln2_b': _L0_ffn_in['ln2_b'], 'L0_ffn_gate_w': _L0_ffn_in['gate_w'], 'L0_ffn_gate_b': _L0_ffn_in['gate_b'], 'L0_ffn_w1': _L0_ffn_in['w1'], 'L0_ffn_w2': _L0_ffn_in['w2']}
    _x0 = _d['L0_attn_hidden_states']
    _d['L0_attn_hidden_states'] = jax.random.normal(jax.random.fold_in(jax.random.key(seed), 1), (8, 512, 128), dtype=_x0.dtype)
    del _x0
    return _d

def reference(L0_attn_hidden_states, L0_attn_in_proj_w, L0_attn_conv_w, L0_attn_conv_b, L0_attn_ln_g, L0_attn_ln_b, L0_attn_fc_w, L0_attn_fc_b, L0_attn_cproj_w, L0_attn_cproj_b, L0_attn_out_w, L0_ffn_ln1_w, L0_ffn_ln1_b, L0_ffn_w_qkv, L0_ffn_w_proj, L0_ffn_ln2_w, L0_ffn_ln2_b, L0_ffn_gate_w, L0_ffn_gate_b, L0_ffn_w1, L0_ffn_w2):

    def _L0_attn_ref(hidden_states, in_proj_w, conv_w, conv_b, ln_g, ln_b, fc_w, fc_b, cproj_w, cproj_b, out_w):
        import jax, jax.numpy as jnp
        import numpy as np
        B, L, H, I, K, G = (2, 512, 128, 256, 4, 8)
        EPS = 1e-05

        def _layernorm(x, g, b):
            m = x.mean(-1, keepdims=True)
            v = jnp.var(x, axis=-1, keepdims=True)
            return (x - m) * jax.lax.rsqrt(v + EPS) * g + b
        p = hidden_states @ in_proj_w.T
        h, gate = (p[..., :I], p[..., I:])
        gate = jax.nn.silu(gate)
        hc = jnp.transpose(h, (0, 2, 1))
        conv = jax.lax.conv_general_dilated(hc, conv_w, window_strides=(1,), padding=[(K - 1, 0)], feature_group_count=G, dimension_numbers=('NCH', 'OIH', 'NCH'))
        conv = conv + conv_b[None, :, None]
        h = jnp.transpose(conv, (0, 2, 1)) * gate
        residual = h
        hn = _layernorm(h, ln_g, ln_b)
        m = jax.nn.silu(hn @ fc_w.T + fc_b) @ cproj_w.T + cproj_b
        h = m + residual
        return h @ out_w.T

    def _L0_ffn_ref(x, ln1_w, ln1_b, w_qkv, w_proj, ln2_w, ln2_b, gate_w, gate_b, w1, w2):
        import jax, jax.numpy as jnp
        import numpy as np
        B, N, D, H, E = (4, 128, 128, 16, 8)
        DK = D // H
        HID = 4 * D
        EPS = 1e-05

        def _layernorm(x, w, b):
            m = jnp.mean(x, axis=-1, keepdims=True)
            v = jnp.mean(jnp.square(x - m), axis=-1, keepdims=True)
            return (x - m) * jax.lax.rsqrt(v + EPS) * w + b

        def _msa(x, w_qkv, w_proj):
            b, n, d = x.shape
            qkv = (x @ w_qkv).reshape(b, n, 3, H, DK)
            q = qkv[:, :, 0].transpose(0, 2, 1, 3)
            k = qkv[:, :, 1].transpose(0, 2, 1, 3)
            v = qkv[:, :, 2].transpose(0, 2, 1, 3)
            attn = jnp.einsum('bhnd,bhmd->bhnm', q, k) * (1.0 / np.sqrt(DK))
            attn = jax.nn.softmax(attn, axis=-1)
            y = jnp.einsum('bhnm,bhmd->bhnd', attn, v)
            y = y.transpose(0, 2, 1, 3).reshape(b, n, d)
            return y @ w_proj

        def _moe_mlp(x, gate_w, gate_b, w1, w2):
            b, n, d = x.shape
            xf = x.reshape(b * n, d)
            logits = xf @ gate_w + gate_b
            one_hot = jax.nn.one_hot(jnp.argmax(logits, axis=-1), E, dtype=xf.dtype)
            h = jax.nn.gelu(jnp.einsum('td,edh->teh', xf, w1), approximate=True)
            y = jnp.einsum('teh,ehd->ted', h, w2)
            out = jnp.einsum('te,ted->td', one_hot, y)
            return out.reshape(b, n, d)
        x = x + _msa(_layernorm(x, ln1_w, ln1_b), w_qkv, w_proj)
        x = x + _moe_mlp(_layernorm(x, ln2_w, ln2_b), gate_w, gate_b, w1, w2)
        return x
    x = L0_attn_hidden_states
    xn = _layernorm(x, axis=-1)
    s = _L0_attn_ref(xn, L0_attn_in_proj_w, L0_attn_conv_w, L0_attn_conv_b, L0_attn_ln_g, L0_attn_ln_b, L0_attn_fc_w, L0_attn_fc_b, L0_attn_cproj_w, L0_attn_cproj_b, L0_attn_out_w)
    g = _silu(_L0_ffn_ref(xn, L0_ffn_ln1_w, L0_ffn_ln1_b, L0_ffn_w_qkv, L0_ffn_w_proj, L0_ffn_ln2_w, L0_ffn_ln2_b, L0_ffn_gate_w, L0_ffn_gate_b, L0_ffn_w1, L0_ffn_w2))
    x = x + s * g
    return x

_drawn_inputs = setup_inputs


def setup_inputs(seed=0):
    import zlib

    import numpy as np

    out = dict(_drawn_inputs(seed))
    spreads = {'L0_attn_ln_g': (1.0, 0.6),
     'L0_attn_ln_b': (0.0, 0.8),
     'L0_attn_fc_b': (0.0, 0.8),
     'L0_attn_cproj_b': (0.0, 0.429),
     'L0_ffn_ln1_w': (1.0, 0.6),
     'L0_ffn_ln1_b': (0.0, 0.8),
     'L0_ffn_ln2_w': (1.0, 0.6),
     'L0_ffn_ln2_b': (0.0, 0.8),
     'L0_ffn_gate_b': (0.0, 0.8)}
    factors = {'L0_attn_in_proj_w': 8.0,
     'L0_attn_conv_w': 8.0,
     'L0_attn_conv_b': 8.0,
     'L0_attn_fc_w': 8.0,
     'L0_attn_cproj_w': 7.669,
     'L0_attn_out_w': 2.725,
     'L0_ffn_w_qkv': 8.0,
     'L0_ffn_w_proj': 8.0,
     'L0_ffn_gate_w': 8.0,
     'L0_ffn_w1': 8.0,
     'L0_ffn_w2': 8.0}
    for name, (base, spread) in spreads.items():
        noise = np.random.default_rng([zlib.crc32(name.encode()), seed]).standard_normal(out[name].shape)
        drawn = base * np.exp(spread * noise) if base else spread * noise
        out[name] = jnp.asarray(drawn.astype(out[name].dtype))
    for name, factor in factors.items():
        out[name] = (out[name] * factor).astype(out[name].dtype)
    return out
```

```python
from contextlib import ExitStack

import numpy as np

import concourse.bass as bass
from concourse import mybir

F32 = mybir.dt.float32
FR = mybir.dt.float32r
BF16 = mybir.dt.bfloat16
I32 = mybir.dt.int32
U32 = mybir.dt.uint32
ALU = mybir.AluOpType
ACT = mybir.ActivationFunctionType
AX = mybir.AxisListType

P = 128
EPS = 1e-5
NB, L, D = 8, 512, 128
NT = L // P
CI = 256
NC = CI // P
TAPS = 4
H = 16
DK = D // H
HG = 4
NG = H // HG
PADL = TAPS - 1
NE = 8
HID = 512
NHC = HID // P
SCALE = float(DK) ** -0.5
ROW = 4 * D + 1
SEG = NB * L + 2 * P
TILE = 2 * P
N_TILES = NB * L // TILE + NE
BUFS = 4
PASSES = N_TILES // BUFS
NO_TOKEN = 2.0 ** 20
C_ROW = 96


def fused_block(nc, ins, out):
    (x, w_h, w_gT, conv_blk, conv_b, ln_g, ln_b, fcT, fc_b, cproj, cproj_b, outT,
     ln1_w, ln1_b, w_qkv, w_proj, ln2_w, ln2_b, gate_w, gate_b, w_exp,
     ident_in, ones_pattern, expert_rank, segment_start, token_no, before, tile_no, tile_edges) = ins

    x_v = x.rearrange("b (t p) d -> b p t d", p=P)
    out_v = out.rearrange("b (t p) d -> b p t d", p=P)
    qk_dram = nc.dram_tensor("qk_dram", [P, 4, L], F32, kind="Internal").ap()
    rows_dram = nc.dram_tensor("rows_dram", [NE * SEG + TILE, ROW], F32, kind="Internal").ap()
    out_rows = out.rearrange("b t d -> (b t) d")

    with ExitStack() as ctx:
        def sb(name, shape, dt=F32):
            return ctx.enter_context(nc.sbuf_tensor(name, shape, dt))

        def sem(name):
            return ctx.enter_context(nc.semaphore(name))

        ps = ctx.enter_context(nc.psum_tensor("ps", [P, 8, 512], F32))

        prob = sb("prob", [P, 2 * HG, NT, L])
        blk_sb = prob[:, 7, 0:2, :].rearrange("p a n -> p (a n)").rearrange("p (j c n) -> p j c n", j=TAPS, c=NC)
        w_h_sb = prob[:, 7, 2, 0:NC * D].rearrange("p (c d) -> p c d", c=NC)
        cproj_sb = prob[:, 7, 2, NC * D:2 * NC * D].rearrange("p (c d) -> p c d", c=NC)
        fcg = prob[:, 7, 3, 0:NC * D].rearrange("p (c d) -> p c d", c=NC)
        ident = sb("ident", [P, P])
        w_gT_sb = sb("w_gT_sb", [P, CI])
        cb_sb = sb("cb_sb", [P, NC])
        lng_sb = sb("lng_sb", [P, NC])
        lnb_sb = sb("lnb_sb", [P, NC])
        fcT_sb = sb("fcT_sb", [P, NC, D])
        fcb_sb = sb("fcb_sb", [P, 1])
        cpb_sb = sb("cpb_sb", [P, NC])
        outT_sb = sb("outT_sb", [P, NC, D])
        ln1w_sb = sb("ln1w_sb", [P, 1])
        ln1b_sb = sb("ln1b_sb", [P, 1])
        wqkv_sb = sb("wqkv_sb", [P, 3 * D])
        wproj_sb = sb("wproj_sb", [P, D])
        ln2w_sb = sb("ln2w_sb", [P, 1])
        ln2b_sb = sb("ln2b_sb", [P, 1])
        gw_sb = sb("gw_sb", [P, NE])
        gb_sb = sb("gb_sb", [P, NE])
        pat_sb = sb("pat_sb", [P, HG])
        erank_sb = sb("erank_sb", [P, NE])
        seg_sb = sb("seg_sb", [P, NE])
        tok_sb = sb("tok_sb", [P, NT])
        before_sb = sb("before_sb", [P, P])
        tno_sb = sb("tno_sb", [P, N_TILES])
        edge_sb = sb("edge_sb", [P, N_TILES - NE])
        before_bf = sb("before_bf", [P, P], BF16)
        ones_bf = sb("ones_bf", [P, P], BF16)
        ones = sb("ones", [P, P])
        mean_w = sb("mean_w", [P, P])
        neg_half = sb("neg_half", [P, NT])
        wc = sb("wc", [P, TAPS, CI])
        half_cb = sb("half_cb", [P, NC])
        fcc = sb("fcc", [P, NC, D])
        fc_bias = sb("fc_bias", [P, 1])
        w_so = sb("w_so", [P, D])
        s_bias = sb("s_bias", [P, 1])
        x_tok = sb("x_tok", [P, NT, D])
        x_st = sb("x_st", [P, NT, 6])
        x_mv = sb("x_mv", [P, NT, 2])
        x_ve = sb("x_ve", [P, NT])
        x_rs = sb("x_rs", [P, NT])
        x_tmp = sb("x_tmp", [P, 3, NT])
        x_r1 = sb("x_r1", [P, NT])
        xn = sb("xn", [P, NT, D])
        xn1 = sb("xn1", [P, NT, D])
        xnT = sb("xnT", [P, PADL + L])
        xn1T = sb("xn1T", [P, L])
        qk_hl = sb("qk_hl", [P, 4, L], FR)
        q_max = sb("q_max", [P, NG, L], FR)
        q_exp = sb("q_exp", [P, NG, L], FR)
        k_one = sb("k_one", [P, H, L], FR)
        v_sb = sb("v_sb", [P, NT, H, 32])
        th = sb("th", [P, NC, L])
        u = sb("u", [P, NC, L])
        hm = sb("hm", [P, NC, L])
        sq = sb("sq", [P, NC, L])
        srow = sb("srow", [64, L])
        h_mean = sb("h_mean", [P, NT])
        h_msq = sb("h_msq", [P, NT])
        h_var = sb("h_var", [P, NT])
        h_ve = sb("h_ve", [P, NT])
        h_rs = sb("h_rs", [P, NT])
        diag = sb("diag", [P, NT, P])
        rbc = sb("rbc", [P, L])
        zr = sb("zr", [P, L])
        zb = sb("zb", [P, L])
        tz = sb("tz", [P, L])
        s1 = sb("s1", [P, L])
        sT = sb("sT", [P, L])
        mx = sb("mx", [P, NG, NT, HG])
        negc = sb("negc", [P, NG, NT, 2 * HG], FR)
        crow = sb("crow", [2 * HG, L], FR)
        yraw = sb("yraw", [P, L])
        rden = sb("rden", [P, NT, HG])
        ytok = sb("ytok", [P, NT, NG, HG, DK])
        xres = sb("xres", [P, NT, D])
        yTs = sb("yTs", [P, L])
        row = sb("row", [P, NT, ROW])
        xn2 = row[:, :, 0:D]
        x2 = row[:, :, D:2 * D]
        s_tok = row[:, :, 2 * D:3 * D]
        x_row = row[:, :, 3 * D:4 * D]
        no_row = row[:, :, 4 * D]
        no_now = sb("no_now", [P, NT])
        f_st = sb("f_st", [P, NT, 6])
        f_mv = sb("f_mv", [P, NT, 2])
        f_ve = sb("f_ve", [P, NT])
        f_rs = sb("f_rs", [P, NT])
        x3T = sb("x3T", [P, L])
        lg = sb("lg", [P, NT, NE])
        lg_top = sb("lg_top", [P, NT])
        lg_eq = sb("lg_eq", [P, NT, NE])
        lg_sc = sb("lg_sc", [P, NT, NE])
        lg_first = sb("lg_first", [P, NT])
        hot = sb("hot", [P, NT, NE], BF16)
        base = sb("base", [P, NE])
        place = sb("place", [P, NT, NE])
        place_hot = sb("place_hot", [P, NT, NE])
        slot_f = sb("slot_f", [P, NT])
        slot = sb("slot", [P, NT], U32)
        count = sb("count", [P, NE])
        tiles = sb("tiles", [P, NE])
        upto = sb("upto", [P, NE])
        zeros8 = sb("zeros8", [P, NE])
        t_exp = sb("t_exp", [P, N_TILES])
        t_off = sb("t_off", [P, N_TILES])
        t_row = sb("t_row", [P, N_TILES])
        t_row2 = sb("t_row2", [P, N_TILES])
        tile_row = sb("tile_row", [P, N_TILES], I32)
        tile_exp = sb("tile_exp", [P, N_TILES], I32)
        pad_row = sb("pad_row", [P, NE], I32)
        room = prob[:].rearrange("p a t n -> p (a t n)")
        used = 0
        def carve(shape):
            nonlocal used
            size = int(np.prod(shape))
            got = room[:, used:used + size]
            used += size
            if len(shape) == 2:
                got = got.rearrange("p (a b) -> p a b", a=shape[0])
            if len(shape) == 3:
                got = got.rearrange("p (a b c) -> p a b c", a=shape[0], b=shape[1])
            return got
        rt = [carve([2, ROW]) for _ in range(BUFS)]
        wt = [carve([2 * HID]) for _ in range(BUFS)]
        x3s = [carve([TILE]) for _ in range(2)]
        hT = carve([NHC, TILE])
        yTe = carve([TILE])
        fe = carve([2, D])
        te = carve([2, D])
        ge = carve([2, D])
        sg = carve([2, D])
        oo = [carve([2, D]) for _ in range(BUFS)]
        pad = carve([2, ROW])
        over = carve([NE, N_TILES - NE])
        past = carve([N_TILES, NE])
        past_n = carve([N_TILES, NE])
        out_no = [sb(f"out_no{r}", [P, 2], U32) for r in range(BUFS)]

        names = """parted wts_loaded setup_dve setup_pe setup_act ones_set
            x_loaded x_aggr x_var xp_chain x_r1 xn_part xn_ready xT_done xnT_ready xn1T_ready qk_done qk_high qk_split qk_spilled
            q_stacked k_stacked v_done v_ready
            gate_done tanh_ready u_ready conv_done hm_ready sq_ready sums_done srow_ready statT_done h_chain h_var_ready
            h_rs_ready diag_ready rbc_done rbc_ready z_done zr_ready zb_ready tz_ready s1_ready sT_done sT_ready
            stok_done stok_ready xrow_loaded norow_ready no_next
            m_done max_done negh_ready negc_ready cT_done crow_ready e_done exp_done pv_done yraw_ready yT_done
            rden_ready ynorm_ready
            xres_ready ytT_done yTs_ready proj_done x2_ready f_chain f_var_ready f_rs_ready xn2_ready
            xn2T_done x3T_ready lg_done r_chain hot_ready rank_done slotf_ready slot_ready base_ready scattered
            pad_set tile_chain tiles_ready padded et_done x3s_ready hid_done hid_ready
            ye_done yTe_ready yt_done fe_ready te_ready ge_ready sg_ready oo_ready outno_ready""".split()
        S = {n: sem(n) for n in names}
        rt_loaded = [sem(f"rt_loaded{r}") for r in range(BUFS)]
        wt_loaded = [sem(f"wt_loaded{r}") for r in range(BUFS)]
        out_stored = [sem(f"out_stored{r}") for r in range(BUFS)]
        c_placed = [sem(f"c_placed{g}") for g in range(NG)]

        weights = [(ident[:], ident_in), (w_h_sb, w_h), (w_gT_sb[:], w_gT), (blk_sb, conv_blk), (cb_sb[:], conv_b),
                   (lng_sb[:], ln_g), (lnb_sb[:], ln_b), (fcT_sb[:], fcT), (fcb_sb[:], fc_b), (cproj_sb, cproj),
                   (cpb_sb[:], cproj_b), (outT_sb[:], outT), (ln1w_sb[:], ln1_w), (ln1b_sb[:], ln1_b), (wqkv_sb[:], w_qkv),
                   (wproj_sb[:], w_proj), (ln2w_sb[:], ln2_w), (ln2b_sb[:], ln2_b), (gw_sb[:], gate_w), (gb_sb[:], gate_b),
                   (pat_sb[:], ones_pattern),
                   (erank_sb[:], expert_rank), (seg_sb[:], segment_start), (tok_sb[:], token_no),
                   (before_sb[:], before), (tno_sb[:], tile_no), (edge_sb[:], tile_edges)]

        def part(eng):
            eng.sem_inc(S["parted"])

        def expert_tiles(eng, step):
            for r in range(BUFS):
                step(r, r, True, False)
            with eng.Fori(1, PASSES - 1) as n:
                for r in range(BUFS):
                    step(n * BUFS + r, r, False, False)
            for r in range(BUFS):
                step((PASSES - 1) * BUFS + r, r, False, True)

        def loads_of(i, r):
            return 16 // BUFS * (i - r) + 16

        def batches(eng, body):
            body(0, True, False)
            with eng.Fori(1, NB - 1) as b:
                body(b, False, False)
            body(NB - 1, False, True)

        with nc.Block() as block:

            @block.sync
            def _(sp):
                for dst, src in weights:
                    sp.dma_start(dst, src).then_inc(S["wts_loaded"], 16)

                def load_x(b, first):
                    if not first:
                        sp.wait_ge(S["xn_ready"], b)
                    sp.dma_start(x_tok[:], x_v[b]).then_inc(S["x_loaded"], 16)

                def spill_qk(b, first):
                    sp.wait_ge(S["qk_split"], 2 * b + 2)
                    sp.dma_start(qk_dram, qk_hl[:].bitcast(F32)).then_inc(S["qk_spilled"], 16)

                def stack_qk(b, first):
                    sp.wait_ge(S["qk_spilled"], 16 * b + 16)
                    if first:
                        sp.wait_ge(S["ones_set"], 6)
                    else:
                        part(sp)
                        sp.wait_ge(S["e_done"], H * NT * b)
                    for copy, piece in enumerate((0, 1, 0)):
                        rows = slice(32 * copy, 32 * copy + 32)
                        src = qk_dram[:, piece, :].rearrange("(g r) n -> r g n", g=NG)
                        sp.dma_start(q_max[rows].bitcast(F32), src).then_inc(S["q_stacked"], 16)
                        sp.dma_start(q_exp[rows].bitcast(F32), src).then_inc(S["q_stacked"], 16)
                    for copy, piece in enumerate((2, 2, 3)):
                        for j in range(HG):
                            row = 32 * copy + DK * j
                            src = qk_dram[:, piece, :].rearrange("(g r) n -> r g n", g=NG)[DK * j:DK * j + DK]
                            dst = k_one[row:row + DK].rearrange("p (g j) n -> p g j n", g=NG)[:, :, j, :]
                            sp.dma_start(dst.bitcast(F32), src).then_inc(S["k_stacked"], 16)

                load_x(0, True)
                spill_qk(0, True)
                stack_qk(0, True)

                def body(b, first, last):
                    if not first:
                        sp.wait_ge(S["scattered"], 64 * b)
                    sp.dma_start(x_row, x_v[b]).then_inc(S["xrow_loaded"], 16)
                    if not last:
                        load_x(b + 1, False)
                    for g in range(NG):
                        sp.wait_ge(S["crow_ready"], NG * b + g + 1)
                        sp.dma_start(q_exp[C_ROW:C_ROW + 2 * HG, g, :].bitcast(F32),
                                     crow[:].bitcast(F32)).then_inc(c_placed[g], 16)
                    if not last:
                        sp.wait_ge(S["q_stacked"], 96 * b + 96)
                        sp.wait_ge(S["k_stacked"], 192 * b + 192)
                        spill_qk(b + 1, False)
                        stack_qk(b + 1, False)

                batches(sp, body)

                sp.wait_ge(S["scattered"], 64 * NB)
                sp.wait_ge(S["tiles_ready"], 3)
                sp.wait_ge(S["pad_set"], 2)
                for e in range(NE):
                    at = sp.value_load(pad_row[0:1, e:e + 1], min_val=0, max_val=NE * SEG - TILE)
                    sp.dma_start(rows_dram[bass.ds(at, TILE), :].rearrange("(h p) r -> p h r", p=P),
                                 pad).then_inc(S["padded"], 16)
                sp.dma_start(rows_dram[NE * SEG:NE * SEG + TILE, :].rearrange("(h p) r -> p h r", p=P),
                             pad).then_inc(S["padded"], 16)
                sp.wait_ge(S["padded"], 16 * (NE + 1))

                def load_tile(i, r, start, end):
                    row_at = sp.value_load(tile_row[0:1, bass.ds(i, 1)], min_val=0, max_val=NE * SEG)
                    exp_at = sp.value_load(tile_exp[0:1, bass.ds(i, 1)], min_val=0, max_val=NE - 1)
                    if not start:
                        sp.wait_ge(S["oo_ready"], i - BUFS + 1)
                    sp.dma_start(rt[r], rows_dram[bass.ds(row_at, TILE), :].rearrange("(h p) r -> p h r", p=P))\
                        .then_inc(rt_loaded[r], 16)
                    if not start:
                        sp.wait_ge(S["ye_done"], i - BUFS + 1)
                    sp.dma_start(wt[r], w_exp[exp_at]).then_inc(wt_loaded[r], 16)

                expert_tiles(sp, load_tile)

            @block.tensor
            def _(pe):
                mm = nc.tensor.matmul
                tr = nc.tensor.transpose
                pe.wait_ge(S["wts_loaded"], 16 * len(weights))
                pe.wait_ge(S["setup_dve"], 3)
                for j in range(TAPS):
                    for c in range(NC):
                        last = mm(ps[:, j // 2, (j % 2) * CI + c * P:(j % 2) * CI + (c + 1) * P], w_h_sb[:, c, :],
                                  blk_sb[:, j, c, :], start=True, stop=True, skip_group_check=True)
                last.then_inc(S["setup_pe"], 1)
                for c in range(NC):
                    last = mm(ps[:, 2, 0:D], mean_w[:], fcg[:, c, :], start=(c == 0), stop=(c == NC - 1))
                last.then_inc(S["setup_pe"], 1)
                for c in range(NC):
                    mm(ps[:, 3, 0:1], fcT_sb[:, c, :], lnb_sb[:, c:c + 1], start=(c == 0), stop=(c == NC - 1))
                for c in range(NC):
                    mm(ps[:, 4, 0:1], outT_sb[:, c, :], cpb_sb[:, c:c + 1], start=(c == 0), stop=(c == NC - 1))
                for c in range(NC):
                    last = mm(ps[:, 5, 0:D], cproj_sb[:, c, :], outT_sb[:, c, :], start=(c == 0), stop=(c == NC - 1))
                last.then_inc(S["setup_pe"], 1)

                def p_transpose(b):
                    pe.wait_ge(S["xn_ready"], b + 1)
                    for t in range(NT):
                        last = tr(ps[:, 0, t * P:(t + 1) * P], xn[:, t, :], ident[:])
                    last.then_inc(S["xT_done"], 1)
                    for t in range(NT):
                        last = tr(ps[:, 1, t * P:(t + 1) * P], xn1[:, t, :], ident[:])
                    last.then_inc(S["xT_done"], 1)

                def p_qk(b):
                    pe.wait_ge(S["xn1T_ready"], b + 1)
                    mm(ps[:, 2, :], wqkv_sb[:, 0:D], xn1T[:], start=True, stop=True).then_inc(S["qk_done"], 1)
                    mm(ps[:, 3, :], wqkv_sb[:, D:2 * D], xn1T[:], start=True, stop=True).then_inc(S["qk_done"], 1)

                def p_v(b):
                    pe.wait_ge(S["xnT_ready"], b + 1)
                    pe.wait_ge(S["xn1T_ready"], b + 1)
                    for t in range(NT):
                        last = mm(ps[:, 0, t * D:(t + 1) * D], xn1T[:, t * P:(t + 1) * P], wqkv_sb[:, 2 * D:3 * D],
                                  start=True, stop=True, skip_group_check=True)
                    last.then_inc(S["v_done"], 1)

                def a_gate_conv(b):
                    pe.wait_ge(S["xnT_ready"], b + 1)
                    for c in range(NC):
                        mm(ps[:, 4 + c, :], w_gT_sb[:, c * P:(c + 1) * P], xnT[:, PADL:PADL + L],
                           start=True, stop=True).then_inc(S["gate_done"], 1)
                    for c in range(NC):
                        for j in range(TAPS):
                            last = mm(ps[:, 6 + c, :], wc[:, j, c * P:(c + 1) * P], xnT[:, j:j + L],
                                      start=(j == 0), stop=(j == TAPS - 1))
                        last.then_inc(S["conv_done"], 1)

                def a_sums(b):
                    pe.wait_ge(S["hm_ready"], 2 * b + 2)
                    pe.wait_ge(S["u_ready"], 2 * b + 2)
                    pe.wait_ge(S["sq_ready"], 2 * b + 2)
                    for c in range(NC):
                        mm(ps[0:32, 4, :], ones[:, 0:32], hm[:, c, :], start=(c == 0), stop=(c == NC - 1),
                           skip_group_check=True)
                        last = mm(ps[32:64, 4, :], ones[:, 0:32], sq[:, c, :], start=(c == 0), stop=(c == NC - 1),
                                  skip_group_check=True)
                    last.then_inc(S["sums_done"], 1)

                def a_stat_transpose(b):
                    pe.wait_ge(S["srow_ready"], b + 1)
                    part(pe)
                    for t in range(NT):
                        last = tr(ps[:, 5, t * 64:(t + 1) * 64], srow[:, t * P:(t + 1) * P], ident[0:64, 0:64])
                    last.then_inc(S["statT_done"], 1)

                def a_z(b):
                    for c in range(NC):
                        last = mm(ps[:, 6, :], fcc[:, c, :], hm[:, c, :], start=(c == 0), stop=(c == NC - 1))
                    last.then_inc(S["z_done"], 1)

                def a_rbc(b):
                    pe.wait_ge(S["diag_ready"], b + 1)
                    mm(ps[:, 5, :], ones[:], diag[:].rearrange("p t n -> p (t n)"), start=True,
                       stop=True).then_inc(S["rbc_done"], 1)

                def a_out(b):
                    for c in range(NC):
                        mm(ps[:, 7, :], outT_sb[:, c, :], hm[:, c, :], start=(c == 0), stop=False)
                    pe.wait_ge(S["s1_ready"], b + 1)
                    mm(ps[:, 7, :], w_so[:], s1[:], start=False, stop=True).then_inc(S["sT_done"], 1)

                def a_s_transpose(b):
                    pe.wait_ge(S["sT_ready"], b + 1)
                    pe.wait_ge(S["zr_ready"], b + 1)
                    for t in range(NT):
                        last = tr(ps[:, 6, t * P:(t + 1) * P], sT[:, t * P:(t + 1) * P], ident[:])
                    last.then_inc(S["stok_done"], 1)

                def m_pair(b, first, n):
                    head, pair = n // 2, n % 2
                    slot = n % 2
                    if not (first and n < 2):
                        pe.wait_ge(S["max_done"], H * 2 * b + n - 1)
                    for i in range(2):
                        t = 2 * pair + i
                        last = mm(ps[:, 2 * slot + i, :], q_max[:, head // HG, t * P:(t + 1) * P], k_one[:, head, :],
                                  start=True, stop=True)
                    last.then_inc(S["m_done"], 1)

                def c_transpose(b, g):
                    pe.wait_ge(S["negc_ready"], NG * b + g + 1)
                    for t in range(NT):
                        last = tr(ps[0:2 * HG, 7, t * P:(t + 1) * P], negc[:, g, t, :].bitcast(F32), ident[:])
                    last.then_inc(S["cT_done"], 1)

                def e_step(b, first, g, k):
                    n = g * HG * NT + k
                    if not (first and n < 2):
                        pe.wait_ge(S["exp_done"], H * NT * b + n - 1)
                    mt = k % NT
                    mm(ps[:, 4 + n % 2, :], k_one[:, g * HG + k // NT, mt * P:(mt + 1) * P], q_exp[:, g, :],
                       start=True, stop=True).then_inc(S["e_done"], 1)

                def pv(b, g, mt):
                    if mt == 0:
                        pe.wait_ge(S["exp_done"], H * NT * b + HG * NT * (g + 1))
                        if g > 0:
                            pe.wait_ge(S["yraw_ready"], NG * b + g)
                    for j in range(HG):
                        last = mm(ps[32 * j:32 * j + 32, 6, :], v_sb[:, mt, g * HG + j, :],
                                  prob[:, (g % 2) * HG + j, mt, :], start=(mt == 0), stop=(mt == NT - 1),
                                  skip_group_check=True)
                    if mt == NT - 1:
                        last.then_inc(S["pv_done"], 1)

                def y_transpose(b, g):
                    pe.wait_ge(S["yraw_ready"], NG * b + g + 1)
                    if g > 0:
                        pe.wait_ge(S["ynorm_ready"], NG * b + g)
                    for t in range(NT):
                        last = tr(ps[:, 7, t * P:(t + 1) * P], yraw[:, t * P:(t + 1) * P], ident[:])
                    last.then_inc(S["yT_done"], 1)

                def f_stage(b):
                    pe.wait_ge(S["ynorm_ready"], NG * b + NG)
                    pe.wait_ge(S["exp_done"], H * NT * b + H * NT)
                    for t in range(NT):
                        last = tr(ps[:, 4, t * P:(t + 1) * P], ytok[:, t].rearrange("p g j d -> p (g j d)"), ident[:])
                    last.then_inc(S["ytT_done"], 1)
                    pe.wait_ge(S["yTs_ready"], b + 1)
                    for t in range(NT):
                        last = mm(ps[:, 5, t * D:(t + 1) * D], yTs[:, t * P:(t + 1) * P], wproj_sb[:], start=True,
                                  stop=True, skip_group_check=True)
                    last.then_inc(S["proj_done"], 1)
                    pe.wait_ge(S["xn2_ready"], b + 1)
                    for t in range(NT):
                        last = tr(ps[:, 4, t * P:(t + 1) * P], xn2[:, t, :], ident[:])
                    last.then_inc(S["xn2T_done"], 1)

                def r_stage(b):
                    pe.wait_ge(S["x3T_ready"], b + 1)
                    pe.wait_ge(S["x2_ready"], b + 1)
                    for t in range(NT):
                        last = mm(ps[:, 5, t * NE:(t + 1) * NE], x3T[:, t * P:(t + 1) * P], gw_sb[:], start=True,
                                  stop=True, skip_group_check=True)
                    last.then_inc(S["lg_done"], 1)
                    pe.wait_ge(S["hot_ready"], b + 1)
                    for t in range(NT):
                        for earlier in range(t):
                            mm(ps[:, 4, t * NE:(t + 1) * NE], ones_bf[:], hot[:, earlier, :], start=(earlier == 0),
                               stop=False, skip_group_check=True)
                        mm(ps[:, 4, t * NE:(t + 1) * NE], before_bf[:], hot[:, t, :], start=(t == 0), stop=True,
                           skip_group_check=True)
                    for t in range(NT):
                        last = mm(ps[:, 6, 0:NE], ones_bf[:], hot[:, t, :], start=(t == 0), stop=(t == NT - 1))
                    last.then_inc(S["rank_done"], 1)

                pe.wait_ge(S["setup_dve"], 8)
                pe.wait_ge(S["setup_act"], 2)
                p_transpose(0)
                p_qk(0)
                p_v(0)

                def body(b, first, last):
                    if not first:
                        pe.wait_ge(S["x3T_ready"], b)
                        pe.wait_ge(S["x2_ready"], b)
                        pe.wait_ge(S["slot_ready"], b)
                        pe.wait_ge(S["base_ready"], b + 1)
                        pe.wait_ge(S["ynorm_ready"], NG * b)
                    a_gate_conv(b)
                    pe.wait_ge(S["qk_split"], 2 * b + 2)
                    pe.wait_ge(S["v_ready"], b + 1)
                    pe.wait_ge(S["q_stacked"], 96 * b + 96)
                    pe.wait_ge(S["k_stacked"], 192 * b + 192)
                    for n in range(4):
                        m_pair(b, first, n)
                    a_sums(b)
                    for n in range(4, 6):
                        m_pair(b, first, n)
                    a_stat_transpose(b)
                    a_z(b)
                    for n in range(6, 9):
                        m_pair(b, first, n)
                    a_rbc(b)
                    for n in range(9, 13):
                        m_pair(b, first, n)
                    c_transpose(b, 0)
                    for n in range(13, 16):
                        m_pair(b, first, n)
                    pe.wait_ge(S["crow_ready"], NG * b + 1)
                    a_out(b)
                    a_s_transpose(b)
                    pe.wait_ge(S["stok_ready"], b + 1)
                    pe.wait_ge(S["rbc_ready"], b + 1)
                    for g in range(NG):
                        pe.wait_ge(c_placed[g], 16 * b + 16)
                        for k in range(HG * NT):
                            e_step(b, first, g, k)
                            if g < 2 and k % 2 == 0:
                                m_pair(b, first, (g + 2) * 8 + k // 2)
                            if g > 0 and k % 4 == 1:
                                pv(b, g - 1, k // 4)
                            if k == 3 and g < NG - 1:
                                c_transpose(b, g + 1)
                            if g == 2 and k == 6 and not last:
                                pe.wait_ge(S["max_done"], H * 2 * (b + 1))
                                p_transpose(b + 1)
                            if g == 2 and k == 14 and not last:
                                p_qk(b + 1)
                            if g > 1 and k == 8:
                                if g == 2:
                                    pe.wait_ge(S["crow_ready"], NG * b + NG)
                                y_transpose(b, g - 2)
                    for mt in range(NT):
                        pv(b, NG - 1, mt)
                    if not last:
                        p_v(b + 1)
                    y_transpose(b, NG - 2)
                    y_transpose(b, NG - 1)
                    f_stage(b)
                    r_stage(b)

                batches(pe, body)

                def e_transpose(i, r, start):
                    q = r % 2
                    pe.wait_ge(rt_loaded[r], loads_of(i, r))
                    if not (start and r < 2):
                        pe.wait_ge(S["x3s_ready"], i - 1)
                    for h in range(2):
                        last = tr(ps[:, q, h * P:(h + 1) * P], rt[r][:, h, 0:D], ident[:])
                    last.then_inc(S["et_done"], 1)

                def e_hidden(i, r, start):
                    pe.wait_ge(wt_loaded[r], loads_of(i, r))
                    pe.wait_ge(S["x3s_ready"], i + 1)
                    for k in range(NHC):
                        if k % 2 == 0 and not (start and r == 0):
                            pe.wait_ge(S["hid_ready"], 2 * i + k // 2 - 1)
                        last = mm(ps[:, 2 + k // 2, (k % 2) * TILE:(k % 2 + 1) * TILE], wt[r][:, k * P:(k + 1) * P],
                                  x3s[r % 2], start=True, stop=True, skip_group_check=True)
                        if k % 2:
                            last.then_inc(S["hid_done"], 1)

                def e_second(i, r, start):
                    if not (start and r < 2):
                        pe.wait_ge(S["yTe_ready"], i - 1)
                    for k in range(NHC):
                        if k % 2 == 0:
                            pe.wait_ge(S["hid_ready"], 2 * i + k // 2 + 1)
                        last = mm(ps[:, 4 + r % 2, 0:TILE], wt[r][:, HID + k * D:HID + (k + 1) * D], hT[:, k, :],
                                  start=(k == 0), stop=(k == NHC - 1))
                    last.then_inc(S["ye_done"], 1)

                def e_back(i, r, start):
                    pe.wait_ge(S["yTe_ready"], i + 1)
                    if not (start and r < 2):
                        pe.wait_ge(S["fe_ready"], i - 1)
                    part(pe)
                    for h in range(2):
                        last = tr(ps[:, 6 + r % 2, h * P:(h + 1) * P], yTe[:, h * P:(h + 1) * P], ident[:])
                    last.then_inc(S["yt_done"], 1)

                def tile(i, r, start, end):
                    e_hidden(i, r, start)
                    if not (start and r == 0):
                        e_back(i - 1, (r - 1) % BUFS, start)
                    if not (end and r == BUFS - 1):
                        e_transpose(i + 1, (r + 1) % BUFS, start and r + 1 < BUFS)
                    e_second(i, r, start)

                pe.wait_ge(S["base_ready"], NB + 1)
                pe.wait_ge(S["slot_ready"], NB)
                e_transpose(0, 0, True)
                expert_tiles(pe, tile)
                e_back(N_TILES - 1, BUFS - 1, False)

            @block.scalar
            def _(act):
                A = nc.scalar.activation
                act.preload_act_table(ACT.Exp)
                act.wait_ge(S["setup_pe"], 1)
                A(wc[:].rearrange("p j c -> p (j c)"), ps[:, 0:2, :].rearrange("p k n -> p (k n)"), ACT.Copy,
                  scale=0.5).then_inc(S["setup_act"], 1)
                act.wait_ge(S["setup_pe"], 3)
                A(w_so[:], ps[:, 5, 0:D], ACT.Copy, scale=0.5).then_inc(S["setup_act"], 1)

                def p_xT(b, first):
                    act.wait_ge(S["xT_done"], 2 * b + 1)
                    if not first:
                        act.wait_ge(S["conv_done"], 2 * b)
                    A(xnT[:, PADL:PADL + L], ps[:, 0, :], ACT.Copy).then_inc(S["xnT_ready"], 1)
                    act.wait_ge(S["xT_done"], 2 * b + 2)
                    if not first:
                        act.wait_ge(S["v_done"], b)
                    A(xn1T[:], ps[:, 1, :], ACT.Identity, bias=ln1b_sb[:], scale=ln1w_sb[:]).then_inc(S["xn1T_ready"], 1)

                def p_v(b, first):
                    act.wait_ge(S["v_done"], b + 1)
                    if first:
                        act.wait_ge(S["ones_set"], 6)
                    else:
                        act.wait_ge(S["pv_done"], NG * b)
                    for t in range(NT):
                        last = A(v_sb[:, t, :, 0:DK], ps[:, 0, t * D:(t + 1) * D].rearrange("p (h d) -> p h d", h=H),
                                 ACT.Copy)
                    last.then_inc(S["v_ready"], 1)

                p_xT(0, True)
                p_v(0, True)

                def exp_step(b, first, g, k):
                    n = g * HG * NT + k
                    act.wait_ge(S["e_done"], H * NT * b + n + 1)
                    if k == 0:
                        if g >= 2:
                            act.wait_ge(S["pv_done"], NG * b + g - 1)
                        elif not first:
                            act.wait_ge(S["pv_done"], NG * b + g - 1)
                    A(prob[:, (g % 2) * HG + k // NT, k % NT, :], ps[:, 4 + n % 2, :], ACT.Exp,
                      scale=SCALE).then_inc(S["exp_done"], 1)

                def y_copy(b, g, first):
                    act.wait_ge(S["pv_done"], NG * b + g + 1)
                    if not (first and g == 0):
                        act.wait_ge(S["yT_done"], NG * b + g)
                    A(yraw[:], ps[:, 6, :], ACT.Copy).then_inc(S["yraw_ready"], 1)

                def body(b, first, last):
                    for c in range(NC):
                        act.wait_ge(S["gate_done"], 2 * b + c + 1)
                        if not first:
                            act.wait_ge(S["u_ready"], 2 * b)
                        A(th[:, c, :], ps[:, 4 + c, :], ACT.Tanh, scale=0.5).then_inc(S["tanh_ready"], 1)
                    for c in range(NC):
                        act.wait_ge(S["hm_ready"], 2 * b + c + 1)
                        if not first:
                            act.wait_ge(S["sums_done"], b)
                        A(sq[:, c, :], hm[:, c, :], ACT.Square).then_inc(S["sq_ready"], 1)
                    act.wait_ge(S["sums_done"], b + 1)
                    if not first:
                        act.wait_ge(S["statT_done"], b)
                    A(srow[:], ps[0:64, 4, :], ACT.Copy).then_inc(S["srow_ready"], 1)
                    act.wait_ge(S["rbc_done"], b + 1)
                    if not first:
                        act.wait_ge(S["zr_ready"], b)
                    A(rbc[:], ps[:, 5, :], ACT.Copy).then_inc(S["rbc_ready"], 1)
                    act.wait_ge(S["zb_ready"], b + 1)
                    if not first:
                        act.wait_ge(S["s1_ready"], b)
                    A(tz[:], zb[:], ACT.Tanh, scale=0.5).then_inc(S["tz_ready"], 1)
                    act.wait_ge(S["sT_done"], b + 1)
                    act.wait_ge(S["setup_dve"], 8)
                    if not first:
                        act.wait_ge(S["stok_done"], b)
                    A(sT[:], ps[:, 7, :], ACT.Identity, bias=s_bias[:]).then_inc(S["sT_ready"], 1)
                    act.wait_ge(S["stok_done"], b + 1)
                    if not first:
                        act.wait_ge(S["scattered"], 64 * b)
                    A(s_tok, ps[:, 6, :].rearrange("p (t d) -> p t d", t=NT), ACT.Copy).then_inc(S["stok_ready"], 1)
                    for g in range(NG):
                        for k in range(HG * NT):
                            exp_step(b, first, g, k)
                            if g > 0 and k == HG * NT - 1:
                                y_copy(b, g - 1, first)
                            if g == 2 and k == 10 and not last:
                                p_xT(b + 1, False)
                    y_copy(b, NG - 1, first)
                    if not last:
                        p_v(b + 1, False)
                    act.wait_ge(S["ytT_done"], b + 1)
                    if not first:
                        act.wait_ge(S["proj_done"], b)
                    A(yTs[:], ps[:, 4, :], ACT.Copy).then_inc(S["yTs_ready"], 1)
                    act.wait_ge(S["xn2T_done"], b + 1)
                    if not first:
                        act.wait_ge(S["lg_done"], b)
                    A(x3T[:], ps[:, 4, :], ACT.Identity, bias=ln2b_sb[:], scale=ln2w_sb[:]).then_inc(S["x3T_ready"], 1)

                batches(act, body)

                act.preload_act_table(ACT.Gelu_apprx_tanh)

                def x3_scale(i, r, start):
                    act.wait_ge(S["et_done"], i + 1)
                    if not (start and r < 2):
                        act.wait_ge(S["hid_done"], 2 * (i - 1))
                    A(x3s[r % 2], ps[:, r % 2, 0:TILE], ACT.Identity, bias=ln2b_sb[:], scale=ln2w_sb[:])\
                        .then_inc(S["x3s_ready"], 1)

                def gelu(i, r, start):
                    for half in range(2):
                        act.wait_ge(S["hid_done"], 2 * i + half + 1)
                        if half == 0 and not (start and r == 0):
                            act.wait_ge(S["ye_done"], i)
                        A(hT[:, 2 * half:2 * half + 2, :], ps[:, 2 + half, :].rearrange("p (k n) -> p k n", k=2),
                          ACT.Gelu_apprx_tanh).then_inc(S["hid_ready"], 1)

                def y_out(i, r, start):
                    act.wait_ge(S["ye_done"], i + 1)
                    if not (start and r == 0):
                        act.wait_ge(S["yt_done"], i)
                    A(yTe, ps[:, 4 + r % 2, 0:TILE], ACT.Copy).then_inc(S["yTe_ready"], 1)

                def tanh_half(i, r, start):
                    act.wait_ge(S["fe_ready"], i + 1)
                    if not (start and r == 0):
                        act.wait_ge(S["ge_ready"], i)
                    A(te, fe, ACT.Tanh, scale=0.5).then_inc(S["te_ready"], 1)

                def tile(i, r, start, end):
                    gelu(i, r, start)
                    if not (end and r == BUFS - 1):
                        x3_scale(i + 1, (r + 1) % BUFS, start and r + 1 < BUFS)
                    if not (start and r == 0):
                        tanh_half(i - 1, (r - 1) % BUFS, start and r > 0)
                    y_out(i, r, start)

                x3_scale(0, 0, True)
                expert_tiles(act, tile)
                tanh_half(N_TILES - 1, BUFS - 1, False)

            @block.gpsimd
            def _(pool):
                G = nc.gpsimd

                def p_norm(b, first):
                    chain = 4 * b
                    pool.wait_ge(S["x_var"], b + 1)
                    if not first:
                        pool.wait_ge(S["xT_done"], 2 * b)
                        pool.wait_ge(S["xn_ready"], b)
                        pool.wait_ge(S["xres_ready"], b)
                    G.tensor_tensor(x_rs[:], x_ve[:], neg_half[:], ALU.pow).then_inc(S["xp_chain"], 1)
                    pool.wait_ge(S["xp_chain"], chain + 1)
                    G.tensor_tensor(x_tmp[:, 0, :], x_mv[:, :, 1], x_rs[:], ALU.mult).then_inc(S["xp_chain"], 1)
                    pool.wait_ge(S["xp_chain"], chain + 2)
                    G.tensor_tensor(x_tmp[:, 1, :], x_tmp[:, 0, :], x_rs[:], ALU.mult).then_inc(S["xp_chain"], 1)
                    pool.wait_ge(S["xp_chain"], chain + 3)
                    part(pool)
                    G.tensor_scalar(x_tmp[:, 2, :], x_tmp[:, 1, :], EPS, None, ALU.add).then_inc(S["xp_chain"], 1)
                    pool.wait_ge(S["xp_chain"], chain + 4)
                    G.tensor_tensor(x_r1[:], x_tmp[:, 2, :], neg_half[:], ALU.pow).then_inc(S["x_r1"], 1)
                    for t in range(NT):
                        G.tensor_scalar(xn[:, t, :], x_tok[:, t, :], x_mv[:, t, 0:1], x_rs[:, t:t + 1],
                                        ALU.subtract, ALU.mult).then_inc(S["xn_part"], 1)
                    pool.wait_ge(S["x_r1"], b + 1)
                    pool.wait_ge(S["xn_part"], NT * b + NT)
                    part(pool)
                    for t in range(NT):
                        last = G.tensor_scalar(xn1[:, t, :], xn[:, t, :], x_r1[:, t:t + 1], None, ALU.mult)
                    last.then_inc(S["xn_ready"], 1)

                def scatter_rows(b):
                    pool.wait_ge(S["slot_ready"], b + 1)
                    pool.wait_ge(S["stok_ready"], b + 1)
                    pool.wait_ge(S["xrow_loaded"], 16 * b + 16)
                    pool.wait_ge(S["xn2_ready"], b + 1)
                    pool.wait_ge(S["norow_ready"], b + 1)
                    part(pool)
                    for t in range(NT):
                        G.indirect_dma_start(rows_dram, bass.IndirectOffsetOnAxis(slot[:, t:t + 1], 0), row[:, t, :],
                                             None, bounds_check=NE * SEG - 1, oob_is_err=False)\
                            .then_inc(S["scattered"], 16)

                pool.wait_ge(S["ones_set"], 8)
                p_norm(0, True)

                def body(b, first, last):
                    pool.wait_ge(S["xn_ready"], b + 1)
                    if not first:
                        pool.wait_ge(S["x2_ready"], b)
                        part(pool)
                    G.tensor_scalar(xres[:].rearrange("p t d -> p (t d)"), xn[:].rearrange("p t d -> p (t d)"), 1.0,
                                    None, ALU.mult).then_inc(S["xres_ready"], 1)
                    pool.wait_ge(S["h_var_ready"], b + 1)
                    if not first:
                        pool.wait_ge(S["diag_ready"], b)
                    G.tensor_tensor(h_rs[:], h_ve[:], neg_half[:], ALU.pow).then_inc(S["h_rs_ready"], 1)
                    pool.wait_ge(S["zr_ready"], b + 1)
                    if not first:
                        pool.wait_ge(S["s1_ready"], b)
                        part(pool)
                    G.tensor_scalar(zb[:], zr[:], fc_bias[:, 0:1], None, ALU.add).then_inc(S["zb_ready"], 1)
                    if not last:
                        p_norm(b + 1, False)
                    pool.wait_ge(S["f_var_ready"], b + 1)
                    if not first:
                        pool.wait_ge(S["xn2_ready"], b)
                        pool.wait_ge(S["xn2T_done"], b)
                    G.tensor_tensor(f_rs[:], f_ve[:], neg_half[:], ALU.pow).then_inc(S["f_rs_ready"], 1)
                    if not first:
                        pool.wait_ge(S["scattered"], 64 * b)
                        pool.wait_ge(S["no_next"], b + 1)
                    pool.wait_ge(S["f_rs_ready"], b + 1)
                    part(pool)
                    for t in range(NT):
                        last = G.tensor_scalar(xn2[:, t, :], x2[:, t, :], f_mv[:, t, 0:1], f_rs[:, t:t + 1],
                                               ALU.subtract, ALU.mult)
                    last.then_inc(S["xn2_ready"], 1)
                    G.tensor_scalar(no_row, no_now[:], 1.0, None, ALU.mult).then_inc(S["norow_ready"], 1)
                    pool.wait_ge(S["norow_ready"], b + 1)
                    part(pool)
                    G.tensor_scalar(no_now[:], no_now[:], float(L), None, ALU.add).then_inc(S["no_next"], 1)
                    scatter_rows(b)

                G.tensor_scalar(no_now[:], tok_sb[:], 1.0, None, ALU.mult).then_inc(S["no_next"], 1)
                batches(pool, body)

                G.memset(pad.rearrange("p h r -> p (h r)"), 0.0).then_inc(S["pad_set"], 1)
                pool.wait_ge(S["pad_set"], 1)
                G.memset(pad[:, :, 4 * D:4 * D + 1], NO_TOKEN).then_inc(S["pad_set"], 1)

                def weigh_store(i, r, start, end):
                    pool.wait_ge(S["ge_ready"], i + 1)
                    if not (start and r == 0):
                        pool.wait_ge(S["oo_ready"], i)
                    G.tensor_tensor(sg, rt[r][:, :, 2 * D:3 * D], ge, ALU.mult).then_inc(S["sg_ready"], 1)
                    pool.wait_ge(S["oo_ready"], i + 1)
                    pool.wait_ge(S["outno_ready"], i + 1)
                    part(pool)
                    for h in range(2):
                        G.indirect_dma_start(out_rows, bass.IndirectOffsetOnAxis(out_no[r][:, h:h + 1], 0), oo[r][:, h, :],
                                             None, bounds_check=NB * L - 1, oob_is_err=False)\
                            .then_inc(out_stored[r], 16)

                expert_tiles(pool, weigh_store)
                for r in range(BUFS):
                    pool.wait_ge(out_stored[r], 32 * PASSES)

            @block.vector
            def _(dve):
                V = nc.vector
                V.memset(ones[:], 1.0).then_inc(S["ones_set"], 1)
                V.memset(neg_half[:], -0.5).then_inc(S["ones_set"], 1)
                V.memset(mean_w[:], 1.0 / CI).then_inc(S["setup_dve"], 1)
                V.memset(xnT[:, 0:PADL], 0.0).then_inc(S["setup_dve"], 1)
                V.memset(v_sb[:].rearrange("p t h d -> p (t h d)"), 0.0).then_inc(S["ones_set"], 1)
                dve.wait_ge(S["wts_loaded"], 16 * len(weights))
                dve.wait_ge(S["ones_set"], 3)
                V.memset(v_sb[:, :, :, DK:DK + 1], 1.0).then_inc(S["ones_set"], 1)
                V.tensor_tensor(fcg, fcT_sb[:], lng_sb[:].rearrange("p (c o) -> p c o", o=1).to_broadcast([P, NC, D]),
                                ALU.mult).then_inc(S["setup_dve"], 1)
                for g in range(NG):
                    ins = V.tensor_copy(k_one[:, g * HG:(g + 1) * HG, :],
                                        pat_sb[:].rearrange("p (j o) -> p j o", o=1).to_broadcast([P, HG, L]))
                ins.then_inc(S["ones_set"], 1)
                zero = prob[:, 0, :, :]
                V.memset(zero, 0.0).then_inc(S["h_chain"], 1)
                dve.wait_ge(S["h_chain"], 1)
                V.tensor_copy(q_max[:], zero)
                V.tensor_copy(q_exp[:], zero).then_inc(S["ones_set"], 1)
                V.tensor_copy(before_bf[:], before_sb[:])
                V.tensor_copy(ones_bf[:], ones[:]).then_inc(S["ones_set"], 1)
                V.tensor_copy(base[:], seg_sb[:]).then_inc(S["base_ready"], 1)
                V.memset(zeros8[:], 0.0).then_inc(S["ones_set"], 1)
                V.tensor_scalar(half_cb[:], cb_sb[:], 0.5, None, ALU.mult).then_inc(S["setup_dve"], 1)

                def p_stats(b, first):
                    dve.wait_ge(S["x_loaded"], 16 * b + 16)
                    if not first:
                        dve.wait_ge(S["xn_ready"], b)
                    for t in range(NT):
                        last = V.bn_stats(x_st[:, t, :], x_tok[:, t, :])
                    last.then_inc(S["x_aggr"], 1)
                    dve.wait_ge(S["x_aggr"], 2 * b + 1)
                    part(dve)
                    for t in range(NT):
                        last = V.bn_aggr(x_mv[:, t, :], x_st[:, t, :])
                    last.then_inc(S["x_aggr"], 1)
                    dve.wait_ge(S["x_aggr"], 2 * b + 2)
                    V.tensor_scalar(x_ve[:], x_mv[:, :, 1], EPS, None, ALU.add).then_inc(S["x_var"], 1)

                def p_split(b, first):
                    for i in range(2):
                        dve.wait_ge(S["qk_done"], 2 * b + i + 1)
                        if not first:
                            dve.wait_ge(S["qk_spilled"], 16 * b)
                        V.tensor_copy(qk_hl[:, 2 * i, :], ps[:, 2 + i, :]).then_inc(S["qk_high"], 1)
                        dve.wait_ge(S["qk_high"], 2 * b + i + 1)
                        V.tensor_tensor(qk_hl[:, 2 * i + 1, :], ps[:, 2 + i, :], qk_hl[:, 2 * i, :].bitcast(F32),
                                        ALU.subtract).then_inc(S["qk_split"], 1)

                p_stats(0, True)
                dve.wait_ge(S["setup_pe"], 3)
                V.tensor_tensor(fcc[:], fcg, ps[:, 2, 0:D].rearrange("p (o d) -> p o d", o=1).to_broadcast([P, NC, D]),
                                ALU.subtract).then_inc(S["setup_dve"], 1)
                V.tensor_tensor(fc_bias[:], ps[:, 3, 0:1], fcb_sb[:], ALU.add).then_inc(S["setup_dve"], 1)
                V.tensor_copy(s_bias[:], ps[:, 4, 0:1]).then_inc(S["setup_dve"], 1)
                V.tensor_scalar(h_mean[:], ones[:, 0:NT], 0.0, None, ALU.mult).then_inc(S["setup_dve"], 1)
                dve.wait_ge(S["setup_dve"], 8)
                p_split(0, True)

                def reduce_max(b, first, n):
                    head, pair = n // 2, n % 2
                    g, j = head // HG, head % HG
                    dve.wait_ge(S["m_done"], H * 2 * b + n + 1)
                    if n % 8 == 0 and not first:
                        dve.wait_ge(S["negc_ready"], NG * b)
                    V.tensor_reduce(mx[:, g, 2 * pair:2 * pair + 2, j], ps[:, 2 * (n % 2):2 * (n % 2) + 2, :], AX.X,
                                    ALU.max).then_inc(S["max_done"], 1)

                def split_max(b, first, g):
                    dve.wait_ge(S["max_done"], H * 2 * b + 8 * (g + 1))
                    if not first:
                        dve.wait_ge(S["cT_done"], NG * b)
                    V.tensor_scalar(negc[:, g, :, 0:HG], mx[:, g, :, :], -1.0, None, ALU.mult).then_inc(S["negh_ready"], 1)
                    dve.wait_ge(S["negh_ready"], NG * b + g + 1)
                    V.scalar_tensor_tensor(negc[:, g, :, HG:2 * HG], mx[:, g, :, :], -1.0,
                                           negc[:, g, :, 0:HG].bitcast(F32), ALU.mult, ALU.subtract)\
                        .then_inc(S["negc_ready"], 1)

                def c_row(b, first, g):
                    dve.wait_ge(S["cT_done"], NG * b + g + 1)
                    if g > 0:
                        dve.wait_ge(c_placed[g - 1], 16 * b + 16)
                    elif not first:
                        dve.wait_ge(c_placed[NG - 1], 16 * b)
                    V.tensor_copy(crow[:], ps[0:2 * HG, 7, :]).then_inc(S["crow_ready"], 1)

                def y_norm(b, first, g):
                    dve.wait_ge(S["yT_done"], NG * b + g + 1)
                    if not (first and g == 0):
                        dve.wait_ge(S["ynorm_ready"], NG * b + g)
                    if g == 0 and not first:
                        dve.wait_ge(S["ytT_done"], b)
                    yv = ps[:, 7, :].rearrange("p (t j r) -> p t j r", t=NT, j=HG)
                    V.reciprocal(rden[:], yv[:, :, :, DK]).then_inc(S["rden_ready"], 1)
                    dve.wait_ge(S["rden_ready"], NG * b + g + 1)
                    V.tensor_tensor(ytok[:, :, g, :, :], yv[:, :, :, 0:DK],
                                    rden[:].rearrange("p t (j o) -> p t j o", o=1).to_broadcast([P, NT, HG, DK]),
                                    ALU.mult).then_inc(S["ynorm_ready"], 1)

                def body(b, first, last):
                    chain = 3 * b + 1
                    for c in range(NC):
                        dve.wait_ge(S["tanh_ready"], 2 * b + c + 1)
                        if not first:
                            dve.wait_ge(S["hm_ready"], 2 * b)
                        V.scalar_tensor_tensor(u[:, c, :], th[:, c, :], 1.0, ps[:, 4 + c, :], ALU.add,
                                               ALU.mult).then_inc(S["u_ready"], 1)
                    for c in range(NC):
                        dve.wait_ge(S["conv_done"], 2 * b + c + 1)
                        dve.wait_ge(S["u_ready"], 2 * b + c + 1)
                        if not first:
                            dve.wait_ge(S["sT_done"], b)
                            dve.wait_ge(S["sq_ready"], 2 * b)
                        V.scalar_tensor_tensor(hm[:, c, :], ps[:, 6 + c, :], half_cb[:, c:c + 1], u[:, c, :], ALU.add,
                                               ALU.mult).then_inc(S["hm_ready"], 1)
                    for n in range(6):
                        reduce_max(b, first, n)
                    dve.wait_ge(S["statT_done"], b + 1)
                    if not first:
                        dve.wait_ge(S["h_rs_ready"], b)
                    sums = ps[:, 5, 0:4 * 64].rearrange("p (t r) -> p t r", t=NT)
                    V.tensor_scalar(h_mean[:], sums[:, :, 0], 1.0 / CI, None, ALU.mult).then_inc(S["h_chain"], 1)
                    dve.wait_ge(S["h_chain"], chain + 1)
                    V.tensor_tensor(h_msq[:], h_mean[:], h_mean[:], ALU.mult).then_inc(S["h_chain"], 1)
                    dve.wait_ge(S["h_chain"], chain + 2)
                    V.scalar_tensor_tensor(h_var[:], sums[:, :, 32], 1.0 / CI, h_msq[:], ALU.mult,
                                           ALU.subtract).then_inc(S["h_chain"], 1)
                    dve.wait_ge(S["h_chain"], chain + 3)
                    V.tensor_scalar(h_ve[:], h_var[:], 0.0, EPS, ALU.max, ALU.add).then_inc(S["h_var_ready"], 1)
                    for n in range(6, 8):
                        reduce_max(b, first, n)
                    split_max(b, first, 0)
                    dve.wait_ge(S["h_rs_ready"], b + 1)
                    if not first:
                        dve.wait_ge(S["rbc_done"], b)
                    V.tensor_tensor(diag[:], ident[:].rearrange("p (o n) -> p o n", o=1).to_broadcast([P, NT, P]),
                                    h_rs[:].rearrange("p (t o) -> p t o", o=1).to_broadcast([P, NT, P]),
                                    ALU.mult).then_inc(S["diag_ready"], 1)
                    for n in range(8, 11):
                        reduce_max(b, first, n)
                    dve.wait_ge(S["z_done"], b + 1)
                    dve.wait_ge(S["rbc_ready"], b + 1)
                    if not first:
                        dve.wait_ge(S["zb_ready"], b)
                    V.tensor_tensor(zr[:], ps[:, 6, :], rbc[:], ALU.mult).then_inc(S["zr_ready"], 1)
                    for n in range(11, 13):
                        reduce_max(b, first, n)
                    c_row(b, first, 0)
                    dve.wait_ge(S["tz_ready"], b + 1)
                    if not first:
                        dve.wait_ge(S["sT_done"], b)
                    V.scalar_tensor_tensor(s1[:], tz[:], 1.0, zb[:], ALU.add, ALU.mult).then_inc(S["s1_ready"], 1)
                    for n in range(13, 16):
                        reduce_max(b, first, n)
                    split_max(b, first, 1)
                    reduce_max(b, first, 16)
                    reduce_max(b, first, 17)
                    c_row(b, first, 1)
                    for n in range(18, 24):
                        reduce_max(b, first, n)
                    split_max(b, first, 2)
                    reduce_max(b, first, 24)
                    reduce_max(b, first, 25)
                    c_row(b, first, 2)
                    for n in range(26, 32):
                        reduce_max(b, first, n)
                    split_max(b, first, 3)
                    if not last:
                        p_stats(b + 1, False)
                    c_row(b, first, 3)
                    y_norm(b, first, 0)
                    if not last:
                        p_split(b + 1, False)
                    for g in range(1, NG):
                        y_norm(b, first, g)
                    dve.wait_ge(S["proj_done"], b + 1)
                    dve.wait_ge(S["xres_ready"], b + 1)
                    if not first:
                        dve.wait_ge(S["scattered"], 64 * b)
                    V.tensor_tensor(x2, ps[:, 5, :].rearrange("p (t d) -> p t d", t=NT), xres[:],
                                    ALU.add).then_inc(S["x2_ready"], 1)
                    dve.wait_ge(S["x2_ready"], b + 1)
                    for t in range(NT):
                        ins = V.bn_stats(f_st[:, t, :], x2[:, t, :])
                    ins.then_inc(S["f_chain"], 1)
                    dve.wait_ge(S["f_chain"], 2 * b + 1)
                    part(dve)
                    for t in range(NT):
                        ins = V.bn_aggr(f_mv[:, t, :], f_st[:, t, :])
                    ins.then_inc(S["f_chain"], 1)
                    dve.wait_ge(S["f_chain"], 2 * b + 2)
                    V.tensor_scalar(f_ve[:], f_mv[:, :, 1], EPS, None, ALU.add).then_inc(S["f_var_ready"], 1)
                    route(b, first)

                def step(ins, name, count):
                    ins.then_inc(S[name], 1)
                    dve.wait_ge(S[name], count)

                def wide(a):
                    return a.rearrange("p (t o) -> p t o", o=1).to_broadcast([P, NT, NE])

                def over_tiles(a):
                    return a.rearrange("p (o e) -> p o e", o=1).to_broadcast([P, NT, NE])

                def route(b, first):
                    c = 7 * b
                    dve.wait_ge(S["lg_done"], b + 1)
                    step(V.tensor_tensor(lg[:], ps[:, 5, 0:NT * NE].rearrange("p (t e) -> p t e", t=NT),
                                         over_tiles(gb_sb[:]), ALU.add), "r_chain", c + 1)
                    step(V.tensor_reduce(lg_top[:], lg[:], AX.X, ALU.max), "r_chain", c + 2)
                    step(V.tensor_tensor(lg_eq[:], lg[:], wide(lg_top[:]), ALU.is_equal), "r_chain", c + 3)
                    step(V.tensor_tensor(lg_sc[:], lg_eq[:], over_tiles(erank_sb[:]), ALU.mult), "r_chain", c + 4)
                    step(V.tensor_reduce(lg_first[:], lg_sc[:], AX.X, ALU.max), "r_chain", c + 5)
                    if not first:
                        dve.wait_ge(S["rank_done"], b)
                    V.tensor_tensor(hot[:], lg_sc[:], wide(lg_first[:]), ALU.is_equal).then_inc(S["hot_ready"], 1)
                    dve.wait_ge(S["hot_ready"], b + 1)
                    dve.wait_ge(S["rank_done"], b + 1)
                    dve.wait_ge(S["base_ready"], b + 1)
                    V.tensor_tensor(place[:], ps[:, 4, 0:NT * NE].rearrange("p (t e) -> p t e", t=NT),
                                    over_tiles(base[:]), ALU.add).then_inc(S["r_chain"], 1)
                    dve.wait_ge(S["r_chain"], c + 6)
                    V.tensor_tensor(base[:], base[:], ps[:, 6, 0:NE], ALU.add).then_inc(S["base_ready"], 1)
                    V.tensor_tensor(place_hot[:], place[:], hot[:], ALU.mult).then_inc(S["r_chain"], 1)
                    dve.wait_ge(S["r_chain"], c + 7)
                    V.tensor_reduce(slot_f[:], place_hot[:], AX.X, ALU.add).then_inc(S["slotf_ready"], 1)
                    dve.wait_ge(S["slotf_ready"], b + 1)
                    if not first:
                        dve.wait_ge(S["scattered"], 64 * b)
                    V.tensor_copy(slot[:], slot_f[:]).then_inc(S["slot_ready"], 1)

                batches(dve, body)

                dve.wait_ge(S["base_ready"], NB + 1)
                step(V.tensor_tensor(count[:], base[:], seg_sb[:], ALU.subtract), "tile_chain", 1)
                step(V.tensor_tensor(over, count[:].rearrange("p (e o) -> p e o", o=1).to_broadcast([P, NE, N_TILES - NE]),
                                     edge_sb[:].rearrange("p (o k) -> p o k", o=1).to_broadcast([P, NE, N_TILES - NE]),
                                     ALU.is_gt), "tile_chain", 2)
                step(V.tensor_reduce(tiles[:], over, AX.X, ALU.add), "tile_chain", 3)
                step(V.tensor_tensor_scan(upto[:], tiles[:], zeros8[:], 0.0, ALU.add, ALU.add), "tile_chain", 4)
                step(V.tensor_tensor(past, tno_sb[:].rearrange("p (i o) -> p i o", o=1).to_broadcast([P, N_TILES, NE]),
                                     upto[:].rearrange("p (o e) -> p o e", o=1).to_broadcast([P, N_TILES, NE]), ALU.is_ge), "tile_chain", 5)
                step(V.tensor_reduce(t_exp[:], past, AX.X, ALU.add), "tile_chain", 6)
                step(V.tensor_tensor(past_n, past,
                                     tiles[:].rearrange("p (o e) -> p o e", o=1).to_broadcast([P, N_TILES, NE]), ALU.mult), "tile_chain", 7)
                step(V.tensor_reduce(t_off[:], past_n, AX.X, ALU.add), "tile_chain", 8)
                step(V.tensor_tensor(t_row[:], tno_sb[:], t_off[:], ALU.subtract), "tile_chain", 9)
                step(V.tensor_scalar(t_row2[:], t_row[:], float(TILE), None, ALU.mult), "tile_chain", 10)
                step(V.scalar_tensor_tensor(t_row[:], t_exp[:], float(SEG), t_row2[:], ALU.mult, ALU.add), "tile_chain", 11)
                V.tensor_scalar(tile_row[:], t_row[:], float(NE * SEG), None, ALU.min).then_inc(S["tiles_ready"], 1)
                V.tensor_scalar(tile_exp[:], t_exp[:], float(NE - 1), None, ALU.min).then_inc(S["tiles_ready"], 1)
                V.tensor_copy(pad_row[:], base[:]).then_inc(S["tiles_ready"], 1)

                def combine(i, r, start, end):
                    dve.wait_ge(S["yt_done"], i + 1)
                    dve.wait_ge(rt_loaded[r], loads_of(i, r))
                    if not (start and r == 0):
                        dve.wait_ge(S["ge_ready"], i)
                    V.tensor_tensor(fe, ps[:, 6 + r % 2, 0:TILE].rearrange("p (h d) -> p h d", h=2),
                                    rt[r][:, :, D:2 * D], ALU.add).then_inc(S["fe_ready"], 1)
                    if not start:
                        dve.wait_ge(out_stored[r], 32 // BUFS * (i - r))
                    V.tensor_copy(out_no[r][:], rt[r][:, :, 4 * D]).then_inc(S["outno_ready"], 1)
                    dve.wait_ge(S["te_ready"], i + 1)
                    dve.wait_ge(S["fe_ready"], i + 1)
                    if not (start and r == 0):
                        dve.wait_ge(S["sg_ready"], i)
                    V.scalar_tensor_tensor(ge, te, 1.0, fe, ALU.add, ALU.mult).then_inc(S["ge_ready"], 1)
                    dve.wait_ge(S["sg_ready"], i + 1)
                    V.scalar_tensor_tensor(oo[r], sg, 0.5, rt[r][:, :, 3 * D:4 * D], ALU.mult,
                                           ALU.add).then_inc(S["oo_ready"], 1)

                expert_tiles(dve, combine)


def kernel(L0_attn_hidden_states, L0_attn_in_proj_w, L0_attn_conv_w, L0_attn_conv_b, L0_attn_ln_g, L0_attn_ln_b,
           L0_attn_fc_w, L0_attn_fc_b, L0_attn_cproj_w, L0_attn_cproj_b, L0_attn_out_w, L0_ffn_ln1_w, L0_ffn_ln1_b,
           L0_ffn_w_qkv, L0_ffn_w_proj, L0_ffn_ln2_w, L0_ffn_ln2_b, L0_ffn_gate_w, L0_ffn_gate_b, L0_ffn_w1,
           L0_ffn_w2):
    import concourse.bacc as bacc
    from concourse.bass_utils import run_bass_kernel_spmd

    def chunks(a):
        a = np.asarray(a)
        return np.ascontiguousarray(np.moveaxis(a.reshape(-1, P, *a.shape[1:]), 0, 1))

    in_proj = np.asarray(L0_attn_in_proj_w)
    conv_w = np.asarray(L0_attn_conv_w)
    per = conv_w.shape[1]
    blk = np.zeros((P, TAPS, NC, P), conv_w.dtype)
    for c in range(NC):
        for g in range(P // per):
            rows = slice(g * per, (g + 1) * per)
            blk[rows, :, c, rows] = conv_w[c * P + g * per:c * P + (g + 1) * per].transpose(1, 2, 0)
    col = lambda a: np.ascontiguousarray(np.asarray(a).reshape(-1, P).T)
    ones_pattern = np.zeros((P, HG), np.float32)
    for j in range(HG):
        ones_pattern[C_ROW + j, j] = 1.0
        ones_pattern[C_ROW + HG + j, j] = 1.0
    on_all = lambda a: np.ascontiguousarray(np.broadcast_to(np.asarray(a, np.float32), (P, len(a))))
    w1 = np.asarray(L0_ffn_w1)
    w2 = np.asarray(L0_ffn_w2)
    arrays = {
        "x": np.asarray(L0_attn_hidden_states),
        "w_h": chunks(in_proj[:CI]),
        "w_gT": np.ascontiguousarray(in_proj[CI:].T),
        "conv_blk": blk,
        "conv_b": col(L0_attn_conv_b),
        "ln_g": col(L0_attn_ln_g),
        "ln_b": col(L0_attn_ln_b),
        "fcT": chunks(np.asarray(L0_attn_fc_w).T),
        "fc_b": col(L0_attn_fc_b),
        "cproj": chunks(L0_attn_cproj_w),
        "cproj_b": col(L0_attn_cproj_b),
        "outT": chunks(np.asarray(L0_attn_out_w).T),
        "ln1_w": col(L0_ffn_ln1_w),
        "ln1_b": col(L0_ffn_ln1_b),
        "w_qkv": np.asarray(L0_ffn_w_qkv),
        "w_proj": np.asarray(L0_ffn_w_proj),
        "ln2_w": col(L0_ffn_ln2_w),
        "ln2_b": col(L0_ffn_ln2_b),
        "gate_w": np.asarray(L0_ffn_gate_w),
        "gate_b": np.ascontiguousarray(np.broadcast_to(np.asarray(L0_ffn_gate_b), (P, NE))),
        "w_exp": np.concatenate([w1, w2.reshape(NE, NHC, P, D).transpose(0, 2, 1, 3).reshape(NE, P, NHC * D)], 2),
        "ident": np.eye(P, dtype=np.float32),
        "ones_pattern": ones_pattern,
        "expert_rank": on_all(NE - np.arange(NE)),
        "segment_start": on_all(SEG * np.arange(NE)),
        "token_no": np.ascontiguousarray(np.arange(L, dtype=np.float32).reshape(NT, P).T),
        "before": np.triu(np.ones((P, P), np.float32), 1),
        "tile_no": on_all(np.arange(N_TILES)),
        "tile_edges": on_all(TILE * np.arange(N_TILES - NE)),
    }
    nc = bacc.Bacc("TRN2", target_bir_lowering=False, num_devices=1)
    ins = [nc.dram_tensor(f"{n}_dram", a.shape, mybir.dt.from_np(a.dtype), kind="ExternalInput").ap()
           for n, a in arrays.items()]
    out = nc.dram_tensor("out_dram", (NB, L, D), F32, kind="ExternalOutput").ap()
    fused_block(nc, ins, out)
    got = run_bass_kernel_spmd(nc, [{f"{n}_dram": a for n, a in arrays.items()}], core_ids=[0])
    return got.results[0]["out_dram"]
```

```python
from contextlib import ExitStack

import numpy as np

import concourse.bass as bass
from concourse import mybir

F32 = mybir.dt.float32
FR = mybir.dt.float32r
BF16 = mybir.dt.bfloat16
I32 = mybir.dt.int32
U32 = mybir.dt.uint32
ALU = mybir.AluOpType
ACT = mybir.ActivationFunctionType
AX = mybir.AxisListType

P = 128
EPS = 1e-5
NB, L, D = 8, 512, 128
NT = L // P
CI = 256
NC = CI // P
TAPS = 4
H = 16
DK = D // H
HG = 4
NG = H // HG
PADL = TAPS - 1
NE = 8
HID = 512
NHC = HID // P
SCALE = float(DK) ** -0.5
ROW = 4 * D + 1
SEG = NB * L + 2 * P
TILE = 2 * P
N_TILES = NB * L // TILE + NE
BUFS = 4
PASSES = N_TILES // BUFS
NO_TOKEN = 2.0 ** 20
LEAD = 11
N_PAIRS = H * NT // 2
N_E = H * NT
C_ROW = 96


def fused_block(nc, ins, out):
    (x, w_h, w_gT, conv_blk, conv_b, ln_g, ln_b, fcT, fc_b, cproj, cproj_b, outT,
     ln1_w, ln1_b, w_qkv, w_proj, ln2_w, ln2_b, gate_w, gate_b, w_exp,
     ident_in, ones_pattern, expert_rank, segment_start, token_no, before, tile_no, tile_edges) = ins

    x_v = x.rearrange("b (t p) d -> b p t d", p=P)
    out_v = out.rearrange("b (t p) d -> b p t d", p=P)
    qk_dram = nc.dram_tensor("qk_dram", [P, 4, L], F32, kind="Internal").ap()
    rows_dram = nc.dram_tensor("rows_dram", [NE * SEG + TILE, ROW], F32, kind="Internal").ap()
    out_rows = out.rearrange("b t d -> (b t) d")

    with ExitStack() as ctx:
        def sb(name, shape, dt=F32):
            return ctx.enter_context(nc.sbuf_tensor(name, shape, dt))

        def sem(name):
            return ctx.enter_context(nc.semaphore(name))

        ps = ctx.enter_context(nc.psum_tensor("ps", [P, 8, 512], F32))

        prob = sb("prob", [P, 2 * HG, NT, L])
        blk_sb = prob[:, 7, 0:2, :].rearrange("p a n -> p (a n)").rearrange("p (j c n) -> p j c n", j=TAPS, c=NC)
        w_h_sb = prob[:, 7, 2, 0:NC * D].rearrange("p (c d) -> p c d", c=NC)
        cproj_sb = prob[:, 7, 2, NC * D:2 * NC * D].rearrange("p (c d) -> p c d", c=NC)
        fcg = prob[:, 7, 3, 0:NC * D].rearrange("p (c d) -> p c d", c=NC)
        ident = sb("ident", [P, P])
        w_gT_sb = sb("w_gT_sb", [P, CI])
        cb_sb = sb("cb_sb", [P, NC])
        lng_sb = sb("lng_sb", [P, NC])
        lnb_sb = sb("lnb_sb", [P, NC])
        fcT_sb = sb("fcT_sb", [P, NC, D])
        fcb_sb = sb("fcb_sb", [P, 1])
        cpb_sb = sb("cpb_sb", [P, NC])
        outT_sb = sb("outT_sb", [P, NC, D])
        ln1w_sb = sb("ln1w_sb", [P, 1])
        ln1b_sb = sb("ln1b_sb", [P, 1])
        wqkv_sb = sb("wqkv_sb", [P, 3 * D])
        wproj_sb = sb("wproj_sb", [P, D])
        ln2w_sb = sb("ln2w_sb", [P, 1])
        ln2b_sb = sb("ln2b_sb", [P, 1])
        gw_sb = sb("gw_sb", [P, NE])
        gb_sb = sb("gb_sb", [P, NE])
        pat_sb = sb("pat_sb", [P, HG])
        erank_sb = sb("erank_sb", [P, NE])
        seg_sb = sb("seg_sb", [P, NE])
        tok_sb = sb("tok_sb", [P, NT])
        before_sb = sb("before_sb", [P, P])
        tno_sb = sb("tno_sb", [P, N_TILES])
        edge_sb = sb("edge_sb", [P, N_TILES - NE])
        before_bf = sb("before_bf", [P, P], BF16)
        ones_bf = sb("ones_bf", [P, P], BF16)
        ones = sb("ones", [P, P])
        mean_w = sb("mean_w", [P, P])
        neg_half = sb("neg_half", [P, NT])
        wc = sb("wc", [P, TAPS, CI])
        half_cb = sb("half_cb", [P, NC])
        fcc = sb("fcc", [P, NC, D])
        fc_bias = sb("fc_bias", [P, 1])
        w_so = sb("w_so", [P, D])
        s_bias = sb("s_bias", [P, 1])
        x_tok = sb("x_tok", [P, NT, D])
        x_st = sb("x_st", [P, NT, 6])
        x_mv = sb("x_mv", [P, NT, 2])
        x_ve = sb("x_ve", [P, NT])
        x_rs = sb("x_rs", [P, NT])
        x_tmp = sb("x_tmp", [P, 3, NT])
        x_r1 = sb("x_r1", [P, NT])
        xn = sb("xn", [P, NT, D])
        xn1 = sb("xn1", [P, NT, D])
        xnT = sb("xnT", [P, PADL + L])
        xn1T = sb("xn1T", [P, L])
        qk_hl = sb("qk_hl", [P, 4, L], FR)
        q_st = sb("q_st", [P, NG, L], FR)
        k_one = sb("k_one", [P, H, L], FR)
        v_sb = sb("v_sb", [P, NT, H, 32])
        th = sb("th", [P, NC, L])
        u = sb("u", [P, NC, L])
        hm = sb("hm", [P, NC, L])
        sq = sb("sq", [P, NC, L])
        srow = sb("srow", [64, L])
        h_mean = sb("h_mean", [P, NT])
        h_msq = sb("h_msq", [P, NT])
        h_var = sb("h_var", [P, NT])
        h_ve = sb("h_ve", [P, NT])
        h_rs = sb("h_rs", [P, NT])
        diag = sb("diag", [P, NT, P])
        rbc = sb("rbc", [P, L])
        zr = sb("zr", [P, L])
        zb = sb("zb", [P, L])
        tz = sb("tz", [P, L])
        s1 = sb("s1", [P, L])
        sT = sb("sT", [P, L])
        mx = sb("mx", [P, NG, NT, HG])
        negc = sb("negc", [P, NG, NT, 2 * HG], FR)
        crow = sb("crow", [2 * HG, L], FR)
        yraw = sb("yraw", [P, L])
        rden = sb("rden", [P, NT, HG])
        ytok = sb("ytok", [P, NT, NG, HG, DK])
        xres = sb("xres", [P, NT, D])
        yTs = sb("yTs", [P, L])
        row = sb("row", [P, NT, ROW])
        xn2 = row[:, :, 0:D]
        x2 = row[:, :, D:2 * D]
        s_tok = row[:, :, 2 * D:3 * D]
        x_row = row[:, :, 3 * D:4 * D]
        no_row = row[:, :, 4 * D]
        no_now = sb("no_now", [P, NT])
        f_st = sb("f_st", [P, NT, 6])
        f_mv = sb("f_mv", [P, NT, 2])
        f_ve = sb("f_ve", [P, NT])
        f_rs = sb("f_rs", [P, NT])
        x3T = sb("x3T", [P, L])
        lg = sb("lg", [P, NT, NE])
        lg_top = sb("lg_top", [P, NT])
        lg_eq = sb("lg_eq", [P, NT, NE])
        lg_sc = sb("lg_sc", [P, NT, NE])
        lg_first = sb("lg_first", [P, NT])
        hot = sb("hot", [P, NT, NE], BF16)
        base = sb("base", [P, NE])
        place = sb("place", [P, NT, NE])
        place_hot = sb("place_hot", [P, NT, NE])
        slot_f = sb("slot_f", [P, NT])
        slot = sb("slot", [P, NT], U32)
        count = sb("count", [P, NE])
        tiles = sb("tiles", [P, NE])
        upto = sb("upto", [P, NE])
        zeros8 = sb("zeros8", [P, NE])
        t_exp = sb("t_exp", [P, N_TILES])
        t_off = sb("t_off", [P, N_TILES])
        t_row = sb("t_row", [P, N_TILES])
        t_row2 = sb("t_row2", [P, N_TILES])
        tile_row = sb("tile_row", [P, N_TILES], I32)
        tile_exp = sb("tile_exp", [P, N_TILES], I32)
        pad_row = sb("pad_row", [P, NE], I32)
        room = prob[:].rearrange("p a t n -> p (a t n)")
        used = 0
        def carve(shape):
            nonlocal used
            size = int(np.prod(shape))
            got = room[:, used:used + size]
            used += size
            if len(shape) == 2:
                got = got.rearrange("p (a b) -> p a b", a=shape[0])
            if len(shape) == 3:
                got = got.rearrange("p (a b c) -> p a b c", a=shape[0], b=shape[1])
            return got
        rt = [carve([2, ROW]) for _ in range(BUFS)]
        wt = [carve([2 * HID]) for _ in range(BUFS)]
        x3s = [carve([TILE]) for _ in range(2)]
        hT = carve([NHC, TILE])
        yTe = carve([TILE])
        fe = carve([2, D])
        te = carve([2, D])
        ge = carve([2, D])
        sg = carve([2, D])
        oo = [carve([2, D]) for _ in range(BUFS)]
        pad = carve([2, ROW])
        over = carve([NE, N_TILES - NE])
        past = carve([N_TILES, NE])
        past_n = carve([N_TILES, NE])
        out_no = [sb(f"out_no{r}", [P, 2], U32) for r in range(BUFS)]

        names = """parted wts_loaded setup_dve setup_pe setup_act ones_set
            x_loaded x_aggr x_var xp_chain x_r1 xn_part xn_ready xT_done xnT_ready xn1T_ready qk_done qk_high qk_split qk_spilled
            v_done v_ready
            gate_done tanh_ready u_ready conv_done hm_ready sq_ready sums_done srow_ready statT_done h_chain h_var_ready
            h_rs_ready diag_ready rbc_done rbc_ready z_done zr_ready zb_ready tz_ready s1_ready sT_done sT_ready
            stok_done stok_ready xrow_loaded norow_ready no_next
            m_done max_done negh_ready negc_ready cT_done crow_ready e_done exp_done pv_done yraw_ready yT_done
            rden_ready ynorm_ready
            xres_ready ytT_done yTs_ready proj_done x2_ready f_chain f_var_ready f_rs_ready xn2_ready
            xn2T_done x3T_ready lg_done r_chain hot_ready rank_done slotf_ready slot_ready base_ready scattered
            pad_set tile_chain tiles_ready padded et_done x3s_ready hid_done hid_ready
            ye_done yTe_ready yt_done fe_ready te_ready ge_ready sg_ready oo_ready outno_ready""".split()
        S = {n: sem(n) for n in names}
        rt_loaded = [sem(f"rt_loaded{r}") for r in range(BUFS)]
        wt_loaded = [sem(f"wt_loaded{r}") for r in range(BUFS)]
        out_stored = [sem(f"out_stored{r}") for r in range(BUFS)]
        stacked = [sem(f"stacked{half}") for half in range(2)]
        c_placed = [sem(f"c_placed{g}") for g in range(NG)]

        weights = [(ident[:], ident_in), (w_h_sb, w_h), (w_gT_sb[:], w_gT), (blk_sb, conv_blk), (cb_sb[:], conv_b),
                   (lng_sb[:], ln_g), (lnb_sb[:], ln_b), (fcT_sb[:], fcT), (fcb_sb[:], fc_b), (cproj_sb, cproj),
                   (cpb_sb[:], cproj_b), (outT_sb[:], outT), (ln1w_sb[:], ln1_w), (ln1b_sb[:], ln1_b), (wqkv_sb[:], w_qkv),
                   (wproj_sb[:], w_proj), (ln2w_sb[:], ln2_w), (ln2b_sb[:], ln2_b), (gw_sb[:], gate_w), (gb_sb[:], gate_b),
                   (pat_sb[:], ones_pattern),
                   (erank_sb[:], expert_rank), (seg_sb[:], segment_start), (tok_sb[:], token_no),
                   (before_sb[:], before), (tno_sb[:], tile_no), (edge_sb[:], tile_edges)]

        def part(eng):
            eng.sem_inc(S["parted"])

        def expert_tiles(eng, step):
            for r in range(BUFS):
                step(r, r, True, False)
            with eng.Fori(1, PASSES - 1) as n:
                for r in range(BUFS):
                    step(n * BUFS + r, r, False, False)
            for r in range(BUFS):
                step((PASSES - 1) * BUFS + r, r, False, True)

        def loads_of(i, r):
            return 16 // BUFS * (i - r) + 16

        def e_bank(n):
            return 4 + n % 2 if n < N_E // 2 else (4, 5, 3)[(n - N_E // 2) % 3]

        def slot_of(n):
            return 0 if n < LEAD else n % 2

        def batches(eng, body):
            body(0, True, False, False)
            body(1, False, True, False)
            with eng.Fori(2, NB - 1) as b:
                body(b, False, False, False)
            body(NB - 1, False, False, True)

        with nc.Block() as block:

            @block.sync
            def _(sp):
                for dst, src in weights:
                    sp.dma_start(dst, src).then_inc(S["wts_loaded"], 16)

                def load_x(b, first):
                    if not first:
                        sp.wait_ge(S["xn_ready"], b)
                    sp.dma_start(x_tok[:], x_v[b]).then_inc(S["x_loaded"], 16)

                def spill_qk(b, first):
                    sp.wait_ge(S["qk_split"], 2 * b + 2)
                    sp.dma_start(qk_dram, qk_hl[:].bitcast(F32)).then_inc(S["qk_spilled"], 16)

                def stack_qk(b, first, half):
                    sp.wait_ge(S["qk_spilled"], 16 * b + 16)
                    if first:
                        sp.wait_ge(S["ones_set"], 6)
                    else:
                        part(sp)
                        sp.wait_ge(S["e_done"], H * NT * (b - 1) + H * NT // 2 * (half + 1))
                    groups = slice(half * NG // 2, (half + 1) * NG // 2)
                    for copy, (q_piece, k_piece) in enumerate(((0, 2), (1, 2), (0, 3))):
                        rows = slice(32 * copy, 32 * copy + 32)
                        src = qk_dram[:, q_piece, :].rearrange("(g r) n -> r g n", g=NG)[:, groups, :]
                        sp.dma_start(q_st[rows, groups, :].bitcast(F32), src).then_inc(stacked[half], 16)
                        for j in range(HG):
                            row = 32 * copy + DK * j
                            src = qk_dram[:, k_piece, :].rearrange("(g r) n -> r g n", g=NG)[DK * j:DK * j + DK, groups, :]
                            dst = k_one[row:row + DK].rearrange("p (g j) n -> p g j n", g=NG)[:, groups, j, :]
                            sp.dma_start(dst.bitcast(F32), src).then_inc(stacked[half], 16)

                load_x(0, True)
                spill_qk(0, True)
                stack_qk(0, True, 0)

                def body(b, first, second, last):
                    if not last:
                        load_x(b + 1, False)
                    stack_qk(b, first, 1)
                    for g in range(NG):
                        if g == 2:
                            if not first:
                                sp.wait_ge(S["scattered"], 64 * b)
                            sp.dma_start(x_row, x_v[b]).then_inc(S["xrow_loaded"], 16)
                        sp.wait_ge(S["crow_ready"], NG * b + g + 1)
                        sp.dma_start(q_st[C_ROW:C_ROW + 2 * HG, g, :].bitcast(F32),
                                     crow[:].bitcast(F32)).then_inc(c_placed[g], 16)
                    if not last:
                        for half in range(2):
                            sp.wait_ge(stacked[half], 240 * b + 240)
                        spill_qk(b + 1, False)
                        stack_qk(b + 1, False, 0)

                batches(sp, body)

                sp.wait_ge(S["scattered"], 64 * NB)
                sp.wait_ge(S["tiles_ready"], 3)
                sp.wait_ge(S["pad_set"], 2)
                for e in range(NE):
                    at = sp.value_load(pad_row[0:1, e:e + 1], min_val=0, max_val=NE * SEG - TILE)
                    sp.dma_start(rows_dram[bass.ds(at, TILE), :].rearrange("(h p) r -> p h r", p=P),
                                 pad).then_inc(S["padded"], 16)
                sp.dma_start(rows_dram[NE * SEG:NE * SEG + TILE, :].rearrange("(h p) r -> p h r", p=P),
                             pad).then_inc(S["padded"], 16)
                sp.wait_ge(S["padded"], 16 * (NE + 1))

                def load_tile(i, r, start, end):
                    row_at = sp.value_load(tile_row[0:1, bass.ds(i, 1)], min_val=0, max_val=NE * SEG)
                    exp_at = sp.value_load(tile_exp[0:1, bass.ds(i, 1)], min_val=0, max_val=NE - 1)
                    if not start:
                        sp.wait_ge(S["oo_ready"], i - BUFS + 1)
                    sp.dma_start(rt[r], rows_dram[bass.ds(row_at, TILE), :].rearrange("(h p) r -> p h r", p=P))\
                        .then_inc(rt_loaded[r], 16)
                    if not start:
                        sp.wait_ge(S["ye_done"], i - BUFS + 1)
                    sp.dma_start(wt[r], w_exp[exp_at]).then_inc(wt_loaded[r], 16)

                expert_tiles(sp, load_tile)

            @block.tensor
            def _(pe):
                mm = nc.tensor.matmul
                tr = nc.tensor.transpose
                pe.wait_ge(S["wts_loaded"], 16 * len(weights))
                pe.wait_ge(S["setup_dve"], 3)
                for j in range(TAPS):
                    for c in range(NC):
                        last = mm(ps[:, j // 2, (j % 2) * CI + c * P:(j % 2) * CI + (c + 1) * P], w_h_sb[:, c, :],
                                  blk_sb[:, j, c, :], start=True, stop=True, skip_group_check=True)
                last.then_inc(S["setup_pe"], 1)
                for c in range(NC):
                    last = mm(ps[:, 2, 0:D], mean_w[:], fcg[:, c, :], start=(c == 0), stop=(c == NC - 1))
                last.then_inc(S["setup_pe"], 1)
                for c in range(NC):
                    mm(ps[:, 3, 0:1], fcT_sb[:, c, :], lnb_sb[:, c:c + 1], start=(c == 0), stop=(c == NC - 1))
                for c in range(NC):
                    mm(ps[:, 4, 0:1], outT_sb[:, c, :], cpb_sb[:, c:c + 1], start=(c == 0), stop=(c == NC - 1))
                for c in range(NC):
                    last = mm(ps[:, 5, 0:D], cproj_sb[:, c, :], outT_sb[:, c, :], start=(c == 0), stop=(c == NC - 1))
                last.then_inc(S["setup_pe"], 1)

                def p_transpose(b):
                    pe.wait_ge(S["xn_ready"], b + 1)
                    for t in range(NT):
                        last = tr(ps[:, 0, t * P:(t + 1) * P], xn[:, t, :], ident[:])
                    last.then_inc(S["xT_done"], 1)
                    for t in range(NT):
                        last = tr(ps[:, 1, t * P:(t + 1) * P], xn1[:, t, :], ident[:])
                    last.then_inc(S["xT_done"], 1)

                def p_qk(b):
                    pe.wait_ge(S["xnT_ready"], b + 1)
                    pe.wait_ge(S["xn1T_ready"], b + 1)
                    mm(ps[:, 0, :], wqkv_sb[:, 0:D], xn1T[:], start=True, stop=True).then_inc(S["qk_done"], 1)
                    mm(ps[:, 1, :], wqkv_sb[:, D:2 * D], xn1T[:], start=True, stop=True).then_inc(S["qk_done"], 1)

                def p_v(b):
                    pe.wait_ge(S["xn1T_ready"], b + 1)
                    for t in range(NT):
                        last = mm(ps[:, 2, t * D:(t + 1) * D], xn1T[:, t * P:(t + 1) * P], wqkv_sb[:, 2 * D:3 * D],
                                  start=True, stop=True, skip_group_check=True)
                    last.then_inc(S["v_done"], 1)

                def a_gate(b, c):
                    pe.wait_ge(S["xnT_ready"], b + 1)
                    mm(ps[:, 4 + c, :], w_gT_sb[:, c * P:(c + 1) * P], xnT[:, PADL:PADL + L],
                       start=True, stop=True).then_inc(S["gate_done"], 1)

                def a_conv(b, c, half):
                    for j in (2 * half, 2 * half + 1):
                        last = mm(ps[:, 6 + c, :], wc[:, j, c * P:(c + 1) * P], xnT[:, j:j + L],
                                  start=(j == 0), stop=(j == TAPS - 1))
                    if half:
                        last.then_inc(S["conv_done"], 1)

                def a_sums(b):
                    pe.wait_ge(S["hm_ready"], 2 * b + 2)
                    pe.wait_ge(S["u_ready"], 2 * b + 2)
                    pe.wait_ge(S["sq_ready"], 2 * b + 2)
                    for c in range(NC):
                        mm(ps[0:32, 4, :], ones[:, 0:32], hm[:, c, :], start=(c == 0), stop=(c == NC - 1),
                           skip_group_check=True)
                        last = mm(ps[32:64, 4, :], ones[:, 0:32], sq[:, c, :], start=(c == 0), stop=(c == NC - 1),
                                  skip_group_check=True)
                    last.then_inc(S["sums_done"], 1)

                def a_stat_transpose(b):
                    pe.wait_ge(S["srow_ready"], b + 1)
                    part(pe)
                    for t in range(NT):
                        last = tr(ps[:, 5, t * 64:(t + 1) * 64], srow[:, t * P:(t + 1) * P], ident[0:64, 0:64])
                    last.then_inc(S["statT_done"], 1)

                def a_z(b):
                    for c in range(NC):
                        last = mm(ps[:, 6, :], fcc[:, c, :], hm[:, c, :], start=(c == 0), stop=(c == NC - 1))
                    last.then_inc(S["z_done"], 1)

                def a_rbc(b):
                    pe.wait_ge(S["diag_ready"], b + 1)
                    mm(ps[:, 7, :], ones[:], diag[:].rearrange("p t n -> p (t n)"), start=True,
                       stop=True).then_inc(S["rbc_done"], 1)

                def a_out(b):
                    for c in range(NC):
                        mm(ps[:, 7, :], outT_sb[:, c, :], hm[:, c, :], start=(c == 0), stop=False)
                    pe.wait_ge(S["s1_ready"], b + 1)
                    mm(ps[:, 7, :], w_so[:], s1[:], start=False, stop=True).then_inc(S["sT_done"], 1)

                def a_s_transpose(b):
                    pe.wait_ge(S["sT_ready"], b + 1)
                    pe.wait_ge(S["zr_ready"], b + 1)
                    for t in range(NT):
                        last = tr(ps[:, 6, t * P:(t + 1) * P], sT[:, t * P:(t + 1) * P], ident[:])
                    last.then_inc(S["stok_done"], 1)

                def m_pair(b, n):
                    head, pair = n // 2, n % 2
                    if 0 < n < LEAD:
                        pe.wait_ge(S["max_done"], N_PAIRS * b + n)
                    if n > LEAD:
                        pe.wait_ge(S["max_done"], N_PAIRS * b + n - 1)
                    for i in range(2):
                        t = 2 * pair + i
                        last = mm(ps[:, 2 * slot_of(n) + i, :], q_st[0:C_ROW, head // HG, t * P:(t + 1) * P],
                                  k_one[0:C_ROW, head, :], start=True, stop=True)
                    last.then_inc(S["m_done"], 1)

                def c_transpose(b, g):
                    pe.wait_ge(S["negc_ready"], NG * b + g + 1)
                    for t in range(NT):
                        last = tr(ps[0:2 * HG, 7, t * P:(t + 1) * P], negc[:, g, t, :].bitcast(F32), ident[:])
                    last.then_inc(S["cT_done"], 1)

                def e_step(b, first, g, k):
                    n = g * HG * NT + k
                    if n == N_E // 2 + 2:
                        pe.wait_ge(S["max_done"], N_PAIRS * (b + 1))
                    elif n > N_E // 2 + 2:
                        pe.wait_ge(S["exp_done"], N_E * b + n - 2)
                    elif not (first and n < 2):
                        pe.wait_ge(S["exp_done"], N_E * b + n - 1)
                    mt = k % NT
                    mm(ps[:, e_bank(n), :], k_one[:, g * HG + k // NT, mt * P:(mt + 1) * P], q_st[:, g, :],
                       start=True, stop=True).then_inc(S["e_done"], 1)

                def pv(b, g, mt):
                    if mt == 0:
                        pe.wait_ge(S["exp_done"], H * NT * b + HG * NT * (g + 1))
                        if g > 0:
                            pe.wait_ge(S["yraw_ready"], NG * b + g)
                    for j in range(HG):
                        last = mm(ps[32 * j:32 * j + 32, 6, :], v_sb[:, mt, g * HG + j, :],
                                  prob[:, (g % 2) * HG + j, mt, :], start=(mt == 0), stop=(mt == NT - 1),
                                  skip_group_check=True)
                    if mt == NT - 1:
                        last.then_inc(S["pv_done"], 1)

                def y_transpose(b, g):
                    pe.wait_ge(S["yraw_ready"], NG * b + g + 1)
                    if g > 0:
                        pe.wait_ge(S["ynorm_ready"], NG * b + g)
                    for t in range(NT):
                        last = tr(ps[:, 7, t * P:(t + 1) * P], yraw[:, t * P:(t + 1) * P], ident[:])
                    last.then_inc(S["yT_done"], 1)

                def f_y(b):
                    pe.wait_ge(S["ynorm_ready"], NG * b + NG)
                    for t in range(NT):
                        last = tr(ps[:, 2, t * P:(t + 1) * P], ytok[:, t].rearrange("p g j d -> p (g j d)"), ident[:])
                    last.then_inc(S["ytT_done"], 1)

                def f_proj(b):
                    pe.wait_ge(S["yTs_ready"], b + 1)
                    for t in range(NT):
                        last = mm(ps[:, 3, t * D:(t + 1) * D], yTs[:, t * P:(t + 1) * P], wproj_sb[:], start=True,
                                  stop=True, skip_group_check=True)
                    last.then_inc(S["proj_done"], 1)

                def f_xn2(b):
                    pe.wait_ge(S["xn2_ready"], b + 1)
                    for t in range(NT):
                        last = tr(ps[:, 2, t * P:(t + 1) * P], xn2[:, t, :], ident[:])
                    last.then_inc(S["xn2T_done"], 1)

                def r_logits(b):
                    pe.wait_ge(S["x3T_ready"], b + 1)
                    for t in range(NT):
                        last = mm(ps[:, 3, t * NE:(t + 1) * NE], x3T[:, t * P:(t + 1) * P], gw_sb[:],
                                  start=True, stop=True, skip_group_check=True)
                    last.then_inc(S["lg_done"], 1)

                def r_ranks(b):
                    pe.wait_ge(S["hot_ready"], b + 1)
                    for t in range(NT):
                        at = (NT + t) * NE
                        for earlier in range(t):
                            mm(ps[:, 3, at:at + NE], ones_bf[:], hot[:, earlier, :], start=(earlier == 0),
                               stop=False, skip_group_check=True)
                        mm(ps[:, 3, at:at + NE], before_bf[:], hot[:, t, :], start=(t == 0), stop=True,
                           skip_group_check=True)
                    at = 2 * NT * NE
                    for t in range(NT):
                        last = mm(ps[:, 3, at:at + NE], ones_bf[:], hot[:, t, :], start=(t == 0), stop=(t == NT - 1),
                                  skip_group_check=True)
                    last.then_inc(S["rank_done"], 1)

                pe.wait_ge(S["setup_dve"], 8)
                pe.wait_ge(S["setup_act"], 2)
                p_transpose(0)
                p_qk(0)
                p_v(0)

                def body(b, first, second, last):
                    pe.wait_ge(S["qk_split"], 2 * b + 2)
                    pe.wait_ge(stacked[0], 240 * b + 240)
                    if not first:
                        y_transpose(b - 1, NG - 2)
                    m_pair(b, 0)
                    if not first:
                        pe.wait_ge(S["exp_done"], H * NT * b)
                    a_gate(b, 0)
                    if not first:
                        y_transpose(b - 1, NG - 1)
                    a_gate(b, 1)
                    m_pair(b, 1)
                    a_conv(b, 0, 0)
                    m_pair(b, 2)
                    a_conv(b, 0, 1)
                    m_pair(b, 3)
                    pe.wait_ge(S["v_ready"], b + 1)
                    if not first:
                        f_y(b - 1)
                    a_conv(b, 1, 0)
                    m_pair(b, 4)
                    a_conv(b, 1, 1)
                    m_pair(b, 5)
                    if not first:
                        f_proj(b - 1)
                    m_pair(b, 6)
                    a_sums(b)
                    m_pair(b, 7)
                    a_stat_transpose(b)
                    a_z(b)
                    m_pair(b, 8)
                    if not first:
                        f_xn2(b - 1)
                    c_transpose(b, 0)
                    m_pair(b, 9)
                    if not first:
                        pe.wait_ge(S["x2_ready"], b)
                        r_logits(b - 1)
                    m_pair(b, 10)
                    if not first:
                        r_ranks(b - 1)
                    pe.wait_ge(S["crow_ready"], NG * b + 1)
                    a_rbc(b)
                    pe.wait_ge(S["h_var_ready"], b + 1)
                    pe.wait_ge(S["srow_ready"], b + 1)
                    pe.wait_ge(stacked[1], 240 * b + 240)
                    for g in range(NG):
                        pe.wait_ge(c_placed[g], 16 * b + 16)
                        for k in range(HG * NT):
                            e_step(b, first, g, k)
                            n = LEAD + 11 * g + k - (k + 1) // 3
                            if g < 2 and k % 3 != 2 and n < N_PAIRS:
                                if n == LEAD and not first:
                                    pe.wait_ge(S["x3T_ready"], b)
                                    pe.wait_ge(S["base_ready"], b + 1)
                                m_pair(b, n)
                            if (g, k) == (1, 3):
                                pe.wait_ge(S["stok_ready"], b + 1)
                            if g > 0 and k % 4 == 3:
                                pv(b, g - 1, k // 4)
                            if (g, k) == (0, 9):
                                pe.wait_ge(S["rbc_ready"], b + 1)
                                c_transpose(b, 1)
                            if (g, k) == (0, 12):
                                pe.wait_ge(S["crow_ready"], NG * b + 2)
                                a_out(b)
                            if (g, k) == (1, 1):
                                a_s_transpose(b)
                            if (g, k) == (1, 5):
                                c_transpose(b, 2)
                            if (g, k) == (2, 3):
                                c_transpose(b, 3)
                            if g == 2 and k == 2 and not last:
                                pe.wait_ge(S["max_done"], N_PAIRS * (b + 1))
                                p_transpose(b + 1)
                            if g == 2 and k == 8 and not last:
                                p_qk(b + 1)
                            if g == 2 and k == 13 and not last:
                                p_v(b + 1)
                            if g > 1 and k == 8:
                                if g == 2:
                                    pe.wait_ge(S["crow_ready"], NG * b + NG)
                                y_transpose(b, g - 2)
                    for mt in range(NT):
                        pv(b, NG - 1, mt)

                batches(pe, body)
                y_transpose(NB - 1, NG - 2)
                y_transpose(NB - 1, NG - 1)
                f_y(NB - 1)
                f_proj(NB - 1)
                f_xn2(NB - 1)
                r_logits(NB - 1)
                r_ranks(NB - 1)

                def e_transpose(i, r, start):
                    q = r % 2
                    pe.wait_ge(rt_loaded[r], loads_of(i, r))
                    if not (start and r < 2):
                        pe.wait_ge(S["x3s_ready"], i - 1)
                    for h in range(2):
                        last = tr(ps[:, q, h * P:(h + 1) * P], rt[r][:, h, 0:D], ident[:])
                    last.then_inc(S["et_done"], 1)

                def e_hidden(i, r, start):
                    pe.wait_ge(wt_loaded[r], loads_of(i, r))
                    pe.wait_ge(S["x3s_ready"], i + 1)
                    for k in range(NHC):
                        if k % 2 == 0 and not (start and r == 0):
                            pe.wait_ge(S["hid_ready"], 2 * i + k // 2 - 1)
                        last = mm(ps[:, 2 + k // 2, (k % 2) * TILE:(k % 2 + 1) * TILE], wt[r][:, k * P:(k + 1) * P],
                                  x3s[r % 2], start=True, stop=True, skip_group_check=True)
                        if k % 2:
                            last.then_inc(S["hid_done"], 1)

                def e_second(i, r, start):
                    if not (start and r < 2):
                        pe.wait_ge(S["yTe_ready"], i - 1)
                    for k in range(NHC):
                        if k % 2 == 0:
                            pe.wait_ge(S["hid_ready"], 2 * i + k // 2 + 1)
                        last = mm(ps[:, 4 + r % 2, 0:TILE], wt[r][:, HID + k * D:HID + (k + 1) * D], hT[:, k, :],
                                  start=(k == 0), stop=(k == NHC - 1))
                    last.then_inc(S["ye_done"], 1)

                def e_back(i, r, start):
                    pe.wait_ge(S["yTe_ready"], i + 1)
                    if not (start and r < 2):
                        pe.wait_ge(S["fe_ready"], i - 1)
                    part(pe)
                    for h in range(2):
                        last = tr(ps[:, 6 + r % 2, h * P:(h + 1) * P], yTe[:, h * P:(h + 1) * P], ident[:])
                    last.then_inc(S["yt_done"], 1)

                def tile(i, r, start, end):
                    e_hidden(i, r, start)
                    if not (start and r == 0):
                        e_back(i - 1, (r - 1) % BUFS, start)
                    if not (end and r == BUFS - 1):
                        e_transpose(i + 1, (r + 1) % BUFS, start and r + 1 < BUFS)
                    e_second(i, r, start)

                pe.wait_ge(S["base_ready"], NB + 1)
                e_transpose(0, 0, True)
                expert_tiles(pe, tile)
                e_back(N_TILES - 1, BUFS - 1, False)

            @block.scalar
            def _(act):
                A = nc.scalar.activation
                act.preload_act_table(ACT.Exp)
                act.wait_ge(S["setup_pe"], 1)
                A(wc[:].rearrange("p j c -> p (j c)"), ps[:, 0:2, :].rearrange("p k n -> p (k n)"), ACT.Copy,
                  scale=0.5).then_inc(S["setup_act"], 1)
                act.wait_ge(S["setup_pe"], 3)
                A(w_so[:], ps[:, 5, 0:D], ACT.Copy, scale=0.5).then_inc(S["setup_act"], 1)

                def p_xT(b, first):
                    act.wait_ge(S["xT_done"], 2 * b + 1)
                    if not first:
                        act.wait_ge(S["conv_done"], 2 * b)
                    A(xnT[:, PADL:PADL + L], ps[:, 0, :], ACT.Copy).then_inc(S["xnT_ready"], 1)
                    act.wait_ge(S["xT_done"], 2 * b + 2)
                    if not first:
                        act.wait_ge(S["v_done"], b)
                    A(xn1T[:], ps[:, 1, :], ACT.Identity, bias=ln1b_sb[:], scale=ln1w_sb[:]).then_inc(S["xn1T_ready"], 1)

                def p_v(b, first):
                    act.wait_ge(S["v_done"], b + 1)
                    if first:
                        act.wait_ge(S["ones_set"], 6)
                    else:
                        act.wait_ge(S["pv_done"], NG * b)
                    for t in range(NT):
                        last = A(v_sb[:, t, :, 0:DK], ps[:, 2, t * D:(t + 1) * D].rearrange("p (h d) -> p h d", h=H),
                                 ACT.Copy)
                    last.then_inc(S["v_ready"], 1)

                p_xT(0, True)
                p_v(0, True)

                def exp_step(b, first, g, k):
                    n = g * HG * NT + k
                    act.wait_ge(S["e_done"], H * NT * b + n + 1)
                    if k == 0:
                        if g >= 2:
                            act.wait_ge(S["pv_done"], NG * b + g - 1)
                        elif not first:
                            act.wait_ge(S["pv_done"], NG * b + g - 1)
                    A(prob[:, (g % 2) * HG + k // NT, k % NT, :], ps[:, e_bank(n), :], ACT.Exp,
                      scale=SCALE).then_inc(S["exp_done"], 1)

                def y_copy(b, g, first):
                    act.wait_ge(S["pv_done"], NG * b + g + 1)
                    if not (first and g == 0):
                        act.wait_ge(S["yT_done"], NG * b + g)
                    A(yraw[:], ps[:, 6, :], ACT.Copy).then_inc(S["yraw_ready"], 1)

                def s_tanh(b, first):
                    act.wait_ge(S["zb_ready"], b + 1)
                    if not first:
                        act.wait_ge(S["s1_ready"], b)
                    A(tz[:], zb[:], ACT.Tanh, scale=0.5).then_inc(S["tz_ready"], 1)

                def s_bias_add(b, first):
                    act.wait_ge(S["sT_done"], b + 1)
                    act.wait_ge(S["setup_dve"], 8)
                    if not first:
                        act.wait_ge(S["stok_done"], b)
                    A(sT[:], ps[:, 7, :], ACT.Identity, bias=s_bias[:]).then_inc(S["sT_ready"], 1)

                def s_copy(b, first):
                    act.wait_ge(S["stok_done"], b + 1)
                    if not first:
                        act.wait_ge(S["scattered"], 64 * b)
                    A(s_tok, ps[:, 6, :].rearrange("p (t d) -> p t d", t=NT), ACT.Copy).then_inc(S["stok_ready"], 1)

                def f_yTs(b, first):
                    act.wait_ge(S["ytT_done"], b + 1)
                    if not first:
                        act.wait_ge(S["proj_done"], b)
                    A(yTs[:], ps[:, 2, :], ACT.Copy).then_inc(S["yTs_ready"], 1)

                def f_x3T(b, first):
                    act.wait_ge(S["xn2T_done"], b + 1)
                    if not first:
                        act.wait_ge(S["lg_done"], b)
                    A(x3T[:], ps[:, 2, :], ACT.Identity, bias=ln2b_sb[:], scale=ln2w_sb[:]).then_inc(S["x3T_ready"], 1)

                def body(b, first, second, last):
                    for c in range(NC):
                        act.wait_ge(S["gate_done"], 2 * b + c + 1)
                        if not first:
                            act.wait_ge(S["u_ready"], 2 * b)
                        A(th[:, c, :], ps[:, 4 + c, :], ACT.Tanh, scale=0.5).then_inc(S["tanh_ready"], 1)
                    if not first:
                        p_v(b, False)
                        f_yTs(b - 1, second)
                    for c in range(NC):
                        act.wait_ge(S["hm_ready"], 2 * b + c + 1)
                        if not first:
                            act.wait_ge(S["sums_done"], b)
                        A(sq[:, c, :], hm[:, c, :], ACT.Square).then_inc(S["sq_ready"], 1)
                    act.wait_ge(S["sums_done"], b + 1)
                    if not first:
                        act.wait_ge(S["statT_done"], b)
                    A(srow[:], ps[0:64, 4, :], ACT.Copy).then_inc(S["srow_ready"], 1)
                    if not first:
                        f_x3T(b - 1, second)
                    act.wait_ge(S["rbc_done"], b + 1)
                    if not first:
                        act.wait_ge(S["zr_ready"], b)
                    A(rbc[:], ps[:, 7, :], ACT.Copy).then_inc(S["rbc_ready"], 1)
                    for g in range(NG):
                        for k in range(HG * NT):
                            exp_step(b, first, g, k)
                            if (g, k) == (0, 5):
                                s_tanh(b, first)
                            if (g, k) == (0, 14):
                                s_bias_add(b, first)
                            if (g, k) == (1, 2):
                                s_copy(b, first)
                            if g > 0 and k == HG * NT - 1:
                                y_copy(b, g - 1, first)
                            if g == 2 and k == 4 and not last:
                                p_xT(b + 1, False)
                    y_copy(b, NG - 1, first)

                batches(act, body)
                f_yTs(NB - 1, False)
                f_x3T(NB - 1, False)

                act.preload_act_table(ACT.Gelu_apprx_tanh)

                def x3_scale(i, r, start):
                    act.wait_ge(S["et_done"], i + 1)
                    if not (start and r < 2):
                        act.wait_ge(S["hid_done"], 2 * (i - 1))
                    A(x3s[r % 2], ps[:, r % 2, 0:TILE], ACT.Identity, bias=ln2b_sb[:], scale=ln2w_sb[:])\
                        .then_inc(S["x3s_ready"], 1)

                def gelu(i, r, start):
                    for half in range(2):
                        act.wait_ge(S["hid_done"], 2 * i + half + 1)
                        if half == 0 and not (start and r == 0):
                            act.wait_ge(S["ye_done"], i)
                        A(hT[:, 2 * half:2 * half + 2, :], ps[:, 2 + half, :].rearrange("p (k n) -> p k n", k=2),
                          ACT.Gelu_apprx_tanh).then_inc(S["hid_ready"], 1)

                def y_out(i, r, start):
                    act.wait_ge(S["ye_done"], i + 1)
                    if not (start and r == 0):
                        act.wait_ge(S["yt_done"], i)
                    A(yTe, ps[:, 4 + r % 2, 0:TILE], ACT.Copy).then_inc(S["yTe_ready"], 1)

                def tanh_half(i, r, start):
                    act.wait_ge(S["fe_ready"], i + 1)
                    if not (start and r == 0):
                        act.wait_ge(S["ge_ready"], i)
                    A(te, fe, ACT.Tanh, scale=0.5).then_inc(S["te_ready"], 1)

                def tile(i, r, start, end):
                    gelu(i, r, start)
                    if not (end and r == BUFS - 1):
                        x3_scale(i + 1, (r + 1) % BUFS, start and r + 1 < BUFS)
                    if not (start and r == 0):
                        tanh_half(i - 1, (r - 1) % BUFS, start and r > 0)
                    y_out(i, r, start)

                x3_scale(0, 0, True)
                expert_tiles(act, tile)
                tanh_half(N_TILES - 1, BUFS - 1, False)

            @block.gpsimd
            def _(pool):
                G = nc.gpsimd

                def p_norm(b, first):
                    chain = 4 * b
                    pool.wait_ge(S["x_var"], b + 1)
                    if not first:
                        pool.wait_ge(S["xT_done"], 2 * b)
                        pool.wait_ge(S["xn_ready"], b)
                        pool.wait_ge(S["xres_ready"], b)
                    G.tensor_tensor(x_rs[:], x_ve[:], neg_half[:], ALU.pow).then_inc(S["xp_chain"], 1)
                    pool.wait_ge(S["xp_chain"], chain + 1)
                    G.tensor_tensor(x_tmp[:, 0, :], x_mv[:, :, 1], x_rs[:], ALU.mult).then_inc(S["xp_chain"], 1)
                    pool.wait_ge(S["xp_chain"], chain + 2)
                    G.tensor_tensor(x_tmp[:, 1, :], x_tmp[:, 0, :], x_rs[:], ALU.mult).then_inc(S["xp_chain"], 1)
                    pool.wait_ge(S["xp_chain"], chain + 3)
                    part(pool)
                    G.tensor_scalar(x_tmp[:, 2, :], x_tmp[:, 1, :], EPS, None, ALU.add).then_inc(S["xp_chain"], 1)
                    pool.wait_ge(S["xp_chain"], chain + 4)
                    G.tensor_tensor(x_r1[:], x_tmp[:, 2, :], neg_half[:], ALU.pow).then_inc(S["x_r1"], 1)
                    for t in range(NT):
                        G.tensor_scalar(xn[:, t, :], x_tok[:, t, :], x_mv[:, t, 0:1], x_rs[:, t:t + 1],
                                        ALU.subtract, ALU.mult).then_inc(S["xn_part"], 1)
                    pool.wait_ge(S["x_r1"], b + 1)
                    pool.wait_ge(S["xn_part"], NT * b + NT)
                    part(pool)
                    for t in range(NT):
                        last = G.tensor_scalar(xn1[:, t, :], xn[:, t, :], x_r1[:, t:t + 1], None, ALU.mult)
                    last.then_inc(S["xn_ready"], 1)

                def scatter_rows(b):
                    pool.wait_ge(S["slot_ready"], b + 1)
                    pool.wait_ge(S["stok_ready"], b + 1)
                    pool.wait_ge(S["xrow_loaded"], 16 * b + 16)
                    pool.wait_ge(S["xn2_ready"], b + 1)
                    pool.wait_ge(S["norow_ready"], b + 1)
                    part(pool)
                    for t in range(NT):
                        G.indirect_dma_start(rows_dram, bass.IndirectOffsetOnAxis(slot[:, t:t + 1], 0), row[:, t, :],
                                             None, bounds_check=NE * SEG - 1, oob_is_err=False)\
                            .then_inc(S["scattered"], 16)

                pool.wait_ge(S["ones_set"], 8)
                p_norm(0, True)

                def f_norm(b, first):
                    pool.wait_ge(S["f_var_ready"], b + 1)
                    if not first:
                        pool.wait_ge(S["xn2_ready"], b)
                        pool.wait_ge(S["xn2T_done"], b)
                    G.tensor_tensor(f_rs[:], f_ve[:], neg_half[:], ALU.pow).then_inc(S["f_rs_ready"], 1)
                    if not first:
                        pool.wait_ge(S["scattered"], 64 * b)
                        pool.wait_ge(S["no_next"], b + 1)
                    pool.wait_ge(S["f_rs_ready"], b + 1)
                    part(pool)
                    for t in range(NT):
                        last = G.tensor_scalar(xn2[:, t, :], x2[:, t, :], f_mv[:, t, 0:1], f_rs[:, t:t + 1],
                                               ALU.subtract, ALU.mult)
                    last.then_inc(S["xn2_ready"], 1)

                def number_rows(b):
                    G.tensor_scalar(no_row, no_now[:], 1.0, None, ALU.mult).then_inc(S["norow_ready"], 1)
                    pool.wait_ge(S["norow_ready"], b + 1)
                    part(pool)
                    G.tensor_scalar(no_now[:], no_now[:], float(L), None, ALU.add).then_inc(S["no_next"], 1)

                def body(b, first, second, last):
                    if not first:
                        f_norm(b - 1, second)
                    pool.wait_ge(S["xn_ready"], b + 1)
                    if not first:
                        pool.wait_ge(S["x2_ready"], b)
                        part(pool)
                    G.tensor_scalar(xres[:].rearrange("p t d -> p (t d)"), xn[:].rearrange("p t d -> p (t d)"), 1.0,
                                    None, ALU.mult).then_inc(S["xres_ready"], 1)
                    if not first:
                        number_rows(b - 1)
                    pool.wait_ge(S["h_var_ready"], b + 1)
                    if not first:
                        pool.wait_ge(S["diag_ready"], b)
                    G.tensor_tensor(h_rs[:], h_ve[:], neg_half[:], ALU.pow).then_inc(S["h_rs_ready"], 1)
                    pool.wait_ge(S["h_rs_ready"], b + 1)
                    if not first:
                        pool.wait_ge(S["rbc_done"], b)
                    G.tensor_tensor(diag[:], ident[:].rearrange("p (o n) -> p o n", o=1).to_broadcast([P, NT, P]),
                                    h_rs[:].rearrange("p (t o) -> p t o", o=1).to_broadcast([P, NT, P]),
                                    ALU.mult).then_inc(S["diag_ready"], 1)
                    if not first:
                        scatter_rows(b - 1)
                    pool.wait_ge(S["zr_ready"], b + 1)
                    if not first:
                        pool.wait_ge(S["s1_ready"], b)
                        part(pool)
                    G.tensor_scalar(zb[:], zr[:], fc_bias[:, 0:1], None, ALU.add).then_inc(S["zb_ready"], 1)
                    if not last:
                        p_norm(b + 1, False)

                G.tensor_scalar(no_now[:], tok_sb[:], 1.0, None, ALU.mult).then_inc(S["no_next"], 1)
                batches(pool, body)
                f_norm(NB - 1, False)
                number_rows(NB - 1)
                scatter_rows(NB - 1)

                G.memset(pad.rearrange("p h r -> p (h r)"), 0.0).then_inc(S["pad_set"], 1)
                pool.wait_ge(S["pad_set"], 1)
                G.memset(pad[:, :, 4 * D:4 * D + 1], NO_TOKEN).then_inc(S["pad_set"], 1)

                def weigh_store(i, r, start, end):
                    pool.wait_ge(S["ge_ready"], i + 1)
                    if not (start and r == 0):
                        pool.wait_ge(S["oo_ready"], i)
                    G.tensor_tensor(sg, rt[r][:, :, 2 * D:3 * D], ge, ALU.mult).then_inc(S["sg_ready"], 1)
                    pool.wait_ge(S["oo_ready"], i + 1)
                    pool.wait_ge(S["outno_ready"], i + 1)
                    part(pool)
                    for h in range(2):
                        G.indirect_dma_start(out_rows, bass.IndirectOffsetOnAxis(out_no[r][:, h:h + 1], 0), oo[r][:, h, :],
                                             None, bounds_check=NB * L - 1, oob_is_err=False)\
                            .then_inc(out_stored[r], 16)

                expert_tiles(pool, weigh_store)
                for r in range(BUFS):
                    pool.wait_ge(out_stored[r], 32 * PASSES)

            @block.vector
            def _(dve):
                V = nc.vector
                V.memset(ones[:], 1.0).then_inc(S["ones_set"], 1)
                V.memset(neg_half[:], -0.5).then_inc(S["ones_set"], 1)
                V.memset(mean_w[:], 1.0 / CI).then_inc(S["setup_dve"], 1)
                V.memset(xnT[:, 0:PADL], 0.0).then_inc(S["setup_dve"], 1)
                V.memset(v_sb[:].rearrange("p t h d -> p (t h d)"), 0.0).then_inc(S["ones_set"], 1)
                dve.wait_ge(S["wts_loaded"], 16 * len(weights))
                dve.wait_ge(S["ones_set"], 3)
                V.memset(v_sb[:, :, :, DK:DK + 1], 1.0).then_inc(S["ones_set"], 1)
                V.tensor_tensor(fcg, fcT_sb[:], lng_sb[:].rearrange("p (c o) -> p c o", o=1).to_broadcast([P, NC, D]),
                                ALU.mult).then_inc(S["setup_dve"], 1)
                for g in range(NG):
                    ins = V.tensor_copy(k_one[:, g * HG:(g + 1) * HG, :],
                                        pat_sb[:].rearrange("p (j o) -> p j o", o=1).to_broadcast([P, HG, L]))
                ins.then_inc(S["ones_set"], 1)
                zero = prob[:, 0, :, :]
                V.memset(zero, 0.0).then_inc(S["h_chain"], 1)
                dve.wait_ge(S["h_chain"], 1)
                V.tensor_copy(q_st[:], zero).then_inc(S["ones_set"], 1)
                V.tensor_copy(before_bf[:], before_sb[:])
                V.tensor_copy(ones_bf[:], ones[:]).then_inc(S["ones_set"], 1)
                V.tensor_copy(base[:], seg_sb[:]).then_inc(S["base_ready"], 1)
                V.memset(zeros8[:], 0.0).then_inc(S["ones_set"], 1)
                V.tensor_scalar(half_cb[:], cb_sb[:], 0.5, None, ALU.mult).then_inc(S["setup_dve"], 1)

                def p_stats(b, first):
                    dve.wait_ge(S["x_loaded"], 16 * b + 16)
                    if not first:
                        dve.wait_ge(S["xn_ready"], b)
                    for t in range(NT):
                        last = V.bn_stats(x_st[:, t, :], x_tok[:, t, :])
                    last.then_inc(S["x_aggr"], 1)
                    dve.wait_ge(S["x_aggr"], 2 * b + 1)
                    part(dve)
                    for t in range(NT):
                        last = V.bn_aggr(x_mv[:, t, :], x_st[:, t, :])
                    last.then_inc(S["x_aggr"], 1)
                    dve.wait_ge(S["x_aggr"], 2 * b + 2)
                    V.tensor_scalar(x_ve[:], x_mv[:, :, 1], EPS, None, ALU.add).then_inc(S["x_var"], 1)

                def p_split(b, first):
                    for i in range(2):
                        dve.wait_ge(S["qk_done"], 2 * b + i + 1)
                        if not first:
                            dve.wait_ge(S["qk_spilled"], 16 * b)
                        V.tensor_copy(qk_hl[:, 2 * i, :], ps[:, i, :]).then_inc(S["qk_high"], 1)
                        dve.wait_ge(S["qk_high"], 2 * b + i + 1)
                        V.tensor_tensor(qk_hl[:, 2 * i + 1, :], ps[:, i, :], qk_hl[:, 2 * i, :].bitcast(F32),
                                        ALU.subtract).then_inc(S["qk_split"], 1)

                p_stats(0, True)
                dve.wait_ge(S["setup_pe"], 3)
                V.tensor_tensor(fcc[:], fcg, ps[:, 2, 0:D].rearrange("p (o d) -> p o d", o=1).to_broadcast([P, NC, D]),
                                ALU.subtract).then_inc(S["setup_dve"], 1)
                V.tensor_tensor(fc_bias[:], ps[:, 3, 0:1], fcb_sb[:], ALU.add).then_inc(S["setup_dve"], 1)
                V.tensor_copy(s_bias[:], ps[:, 4, 0:1]).then_inc(S["setup_dve"], 1)
                V.tensor_scalar(h_mean[:], ones[:, 0:NT], 0.0, None, ALU.mult).then_inc(S["setup_dve"], 1)
                dve.wait_ge(S["setup_dve"], 8)
                p_split(0, True)

                def reduce_max(b, first, n):
                    head, pair = n // 2, n % 2
                    g, j = head // HG, head % HG
                    dve.wait_ge(S["m_done"], H * 2 * b + n + 1)
                    if n % 8 == 0 and not first:
                        dve.wait_ge(S["negc_ready"], NG * b)
                    V.tensor_reduce(mx[:, g, 2 * pair:2 * pair + 2, j], ps[:, 2 * slot_of(n):2 * slot_of(n) + 2, :], AX.X,
                                    ALU.max).then_inc(S["max_done"], 1)

                def split_max(b, first, g):
                    dve.wait_ge(S["max_done"], H * 2 * b + 8 * (g + 1))
                    if not first:
                        dve.wait_ge(S["cT_done"], NG * b)
                    V.tensor_scalar(negc[:, g, :, 0:HG], mx[:, g, :, :], -1.0, None, ALU.mult).then_inc(S["negh_ready"], 1)
                    dve.wait_ge(S["negh_ready"], NG * b + g + 1)
                    V.scalar_tensor_tensor(negc[:, g, :, HG:2 * HG], mx[:, g, :, :], -1.0,
                                           negc[:, g, :, 0:HG].bitcast(F32), ALU.mult, ALU.subtract)\
                        .then_inc(S["negc_ready"], 1)

                def c_row(b, first, g):
                    dve.wait_ge(S["cT_done"], NG * b + g + 1)
                    if g > 0:
                        dve.wait_ge(c_placed[g - 1], 16 * b + 16)
                    elif not first:
                        dve.wait_ge(c_placed[NG - 1], 16 * b)
                    V.tensor_copy(crow[:], ps[0:2 * HG, 7, :]).then_inc(S["crow_ready"], 1)

                def y_norm(b, first, g):
                    dve.wait_ge(S["yT_done"], NG * b + g + 1)
                    if not (first and g == 0):
                        dve.wait_ge(S["ynorm_ready"], NG * b + g)
                    if g == 0 and not first:
                        dve.wait_ge(S["ytT_done"], b)
                    yv = ps[:, 7, :].rearrange("p (t j r) -> p t j r", t=NT, j=HG)
                    V.reciprocal(rden[:], yv[:, :, :, DK]).then_inc(S["rden_ready"], 1)
                    dve.wait_ge(S["rden_ready"], NG * b + g + 1)
                    V.tensor_tensor(ytok[:, :, g, :, :], yv[:, :, :, 0:DK],
                                    rden[:].rearrange("p t (j o) -> p t j o", o=1).to_broadcast([P, NT, HG, DK]),
                                    ALU.mult).then_inc(S["ynorm_ready"], 1)

                def f_stats(b, first):
                    dve.wait_ge(S["proj_done"], b + 1)
                    dve.wait_ge(S["xres_ready"], b + 1)
                    if not first:
                        dve.wait_ge(S["scattered"], 64 * b)
                    V.tensor_tensor(x2, ps[:, 3, :].rearrange("p (t d) -> p t d", t=NT), xres[:],
                                    ALU.add).then_inc(S["x2_ready"], 1)
                    dve.wait_ge(S["x2_ready"], b + 1)
                    for t in range(NT):
                        ins = V.bn_stats(f_st[:, t, :], x2[:, t, :])
                    ins.then_inc(S["f_chain"], 1)
                    dve.wait_ge(S["f_chain"], 2 * b + 1)
                    part(dve)
                    for t in range(NT):
                        ins = V.bn_aggr(f_mv[:, t, :], f_st[:, t, :])
                    ins.then_inc(S["f_chain"], 1)
                    dve.wait_ge(S["f_chain"], 2 * b + 2)
                    V.tensor_scalar(f_ve[:], f_mv[:, :, 1], EPS, None, ALU.add).then_inc(S["f_var_ready"], 1)

                def a_u(b, first, c):
                    dve.wait_ge(S["tanh_ready"], 2 * b + c + 1)
                    if not first:
                        dve.wait_ge(S["hm_ready"], 2 * b)
                    V.scalar_tensor_tensor(u[:, c, :], th[:, c, :], 1.0, ps[:, 4 + c, :], ALU.add,
                                           ALU.mult).then_inc(S["u_ready"], 1)

                def a_hm(b, first, c):
                    dve.wait_ge(S["conv_done"], 2 * b + c + 1)
                    dve.wait_ge(S["u_ready"], 2 * b + c + 1)
                    if not first:
                        dve.wait_ge(S["sT_done"], b)
                        dve.wait_ge(S["sq_ready"], 2 * b)
                    V.scalar_tensor_tensor(hm[:, c, :], ps[:, 6 + c, :], half_cb[:, c:c + 1], u[:, c, :], ALU.add,
                                           ALU.mult).then_inc(S["hm_ready"], 1)

                def body(b, first, second, last):
                    chain = 3 * b + 1
                    if not first:
                        y_norm(b - 1, second, NG - 2)
                    reduce_max(b, first, 0)
                    a_u(b, first, 0)
                    if not first:
                        y_norm(b - 1, second, NG - 1)
                    a_u(b, first, 1)
                    reduce_max(b, first, 1)
                    reduce_max(b, first, 2)
                    a_hm(b, first, 0)
                    reduce_max(b, first, 3)
                    reduce_max(b, first, 4)
                    a_hm(b, first, 1)
                    reduce_max(b, first, 5)
                    if not first:
                        f_stats(b - 1, second)
                    reduce_max(b, first, 6)
                    dve.wait_ge(S["statT_done"], b + 1)
                    if not first:
                        dve.wait_ge(S["h_rs_ready"], b)
                    sums = ps[:, 5, 0:4 * 64].rearrange("p (t r) -> p t r", t=NT)
                    V.tensor_scalar(h_mean[:], sums[:, :, 0], 1.0 / CI, None, ALU.mult).then_inc(S["h_chain"], 1)
                    dve.wait_ge(S["h_chain"], chain + 1)
                    V.tensor_tensor(h_msq[:], h_mean[:], h_mean[:], ALU.mult).then_inc(S["h_chain"], 1)
                    dve.wait_ge(S["h_chain"], chain + 2)
                    V.scalar_tensor_tensor(h_var[:], sums[:, :, 32], 1.0 / CI, h_msq[:], ALU.mult,
                                           ALU.subtract).then_inc(S["h_chain"], 1)
                    dve.wait_ge(S["h_chain"], chain + 3)
                    V.tensor_scalar(h_ve[:], h_var[:], 0.0, EPS, ALU.max, ALU.add).then_inc(S["h_var_ready"], 1)
                    reduce_max(b, first, 7)
                    split_max(b, first, 0)
                    reduce_max(b, first, 8)
                    c_row(b, first, 0)
                    reduce_max(b, first, 9)
                    if not first:
                        r_first(b - 1, second)
                    reduce_max(b, first, 10)
                    if not first:
                        r_place(b - 1, second)
                    reduce_max(b, first, 11)
                    dve.wait_ge(S["z_done"], b + 1)
                    dve.wait_ge(S["rbc_ready"], b + 1)
                    if not first:
                        dve.wait_ge(S["zb_ready"], b)
                    V.tensor_tensor(zr[:], ps[:, 6, :], rbc[:], ALU.mult).then_inc(S["zr_ready"], 1)
                    for n in range(12, 15):
                        reduce_max(b, first, n)
                    dve.wait_ge(S["tz_ready"], b + 1)
                    if not first:
                        dve.wait_ge(S["sT_done"], b)
                    V.scalar_tensor_tensor(s1[:], tz[:], 1.0, zb[:], ALU.add, ALU.mult).then_inc(S["s1_ready"], 1)
                    reduce_max(b, first, 15)
                    split_max(b, first, 1)
                    reduce_max(b, first, 16)
                    reduce_max(b, first, 17)
                    c_row(b, first, 1)
                    if not last:
                        p_stats(b + 1, False)
                    for n in range(18, 24):
                        reduce_max(b, first, n)
                    split_max(b, first, 2)
                    reduce_max(b, first, 24)
                    c_row(b, first, 2)
                    for n in range(25, 32):
                        reduce_max(b, first, n)
                    split_max(b, first, 3)
                    c_row(b, first, 3)
                    if not last:
                        p_split(b + 1, False)
                    for g in range(NG - 2):
                        y_norm(b, first, g)

                def step(ins, name, count):
                    ins.then_inc(S[name], 1)
                    dve.wait_ge(S[name], count)

                def wide(a):
                    return a.rearrange("p (t o) -> p t o", o=1).to_broadcast([P, NT, NE])

                def over_tiles(a):
                    return a.rearrange("p (o e) -> p o e", o=1).to_broadcast([P, NT, NE])

                def r_first(b, first):
                    c = 7 * b
                    dve.wait_ge(S["lg_done"], b + 1)
                    step(V.tensor_tensor(lg[:], ps[:, 3, 0:NT * NE].rearrange("p (t e) -> p t e", t=NT),
                                         over_tiles(gb_sb[:]), ALU.add), "r_chain", c + 1)
                    step(V.tensor_reduce(lg_top[:], lg[:], AX.X, ALU.max), "r_chain", c + 2)
                    step(V.tensor_tensor(lg_eq[:], lg[:], wide(lg_top[:]), ALU.is_equal), "r_chain", c + 3)
                    step(V.tensor_tensor(lg_sc[:], lg_eq[:], over_tiles(erank_sb[:]), ALU.mult), "r_chain", c + 4)
                    step(V.tensor_reduce(lg_first[:], lg_sc[:], AX.X, ALU.max), "r_chain", c + 5)
                    if not first:
                        dve.wait_ge(S["rank_done"], b)
                    V.tensor_tensor(hot[:], lg_sc[:], wide(lg_first[:]), ALU.is_equal).then_inc(S["hot_ready"], 1)

                def r_place(b, first):
                    c = 7 * b
                    ranks = ps[:, 3, NT * NE:2 * NT * NE]
                    totals = ps[:, 3, 2 * NT * NE:(2 * NT + 1) * NE]
                    dve.wait_ge(S["hot_ready"], b + 1)
                    dve.wait_ge(S["rank_done"], b + 1)
                    dve.wait_ge(S["base_ready"], b + 1)
                    V.tensor_tensor(place[:], ranks.rearrange("p (t e) -> p t e", t=NT),
                                    over_tiles(base[:]), ALU.add).then_inc(S["r_chain"], 1)
                    dve.wait_ge(S["r_chain"], c + 6)
                    V.tensor_tensor(base[:], base[:], totals, ALU.add).then_inc(S["base_ready"], 1)
                    dve.wait_ge(S["base_ready"], b + 2)
                    V.tensor_tensor(place_hot[:], place[:], hot[:], ALU.mult).then_inc(S["r_chain"], 1)
                    dve.wait_ge(S["r_chain"], c + 7)
                    V.tensor_reduce(slot_f[:], place_hot[:], AX.X, ALU.add).then_inc(S["slotf_ready"], 1)
                    dve.wait_ge(S["slotf_ready"], b + 1)
                    if not first:
                        dve.wait_ge(S["scattered"], 64 * b)
                    V.tensor_copy(slot[:], slot_f[:]).then_inc(S["slot_ready"], 1)

                batches(dve, body)
                y_norm(NB - 1, False, NG - 2)
                y_norm(NB - 1, False, NG - 1)
                f_stats(NB - 1, False)
                r_first(NB - 1, False)
                r_place(NB - 1, False)

                dve.wait_ge(S["base_ready"], NB + 1)
                step(V.tensor_tensor(count[:], base[:], seg_sb[:], ALU.subtract), "tile_chain", 1)
                step(V.tensor_tensor(over, count[:].rearrange("p (e o) -> p e o", o=1).to_broadcast([P, NE, N_TILES - NE]),
                                     edge_sb[:].rearrange("p (o k) -> p o k", o=1).to_broadcast([P, NE, N_TILES - NE]),
                                     ALU.is_gt), "tile_chain", 2)
                step(V.tensor_reduce(tiles[:], over, AX.X, ALU.add), "tile_chain", 3)
                step(V.tensor_tensor_scan(upto[:], tiles[:], zeros8[:], 0.0, ALU.add, ALU.add), "tile_chain", 4)
                step(V.tensor_tensor(past, tno_sb[:].rearrange("p (i o) -> p i o", o=1).to_broadcast([P, N_TILES, NE]),
                                     upto[:].rearrange("p (o e) -> p o e", o=1).to_broadcast([P, N_TILES, NE]), ALU.is_ge), "tile_chain", 5)
                step(V.tensor_reduce(t_exp[:], past, AX.X, ALU.add), "tile_chain", 6)
                step(V.tensor_tensor(past_n, past,
                                     tiles[:].rearrange("p (o e) -> p o e", o=1).to_broadcast([P, N_TILES, NE]), ALU.mult), "tile_chain", 7)
                step(V.tensor_reduce(t_off[:], past_n, AX.X, ALU.add), "tile_chain", 8)
                step(V.tensor_tensor(t_row[:], tno_sb[:], t_off[:], ALU.subtract), "tile_chain", 9)
                step(V.tensor_scalar(t_row2[:], t_row[:], float(TILE), None, ALU.mult), "tile_chain", 10)
                step(V.scalar_tensor_tensor(t_row[:], t_exp[:], float(SEG), t_row2[:], ALU.mult, ALU.add), "tile_chain", 11)
                V.tensor_scalar(tile_row[:], t_row[:], float(NE * SEG), None, ALU.min).then_inc(S["tiles_ready"], 1)
                V.tensor_scalar(tile_exp[:], t_exp[:], float(NE - 1), None, ALU.min).then_inc(S["tiles_ready"], 1)
                V.tensor_copy(pad_row[:], base[:]).then_inc(S["tiles_ready"], 1)

                def combine(i, r, start, end):
                    dve.wait_ge(S["yt_done"], i + 1)
                    dve.wait_ge(rt_loaded[r], loads_of(i, r))
                    if not (start and r == 0):
                        dve.wait_ge(S["ge_ready"], i)
                    V.tensor_tensor(fe, ps[:, 6 + r % 2, 0:TILE].rearrange("p (h d) -> p h d", h=2),
                                    rt[r][:, :, D:2 * D], ALU.add).then_inc(S["fe_ready"], 1)
                    if not start:
                        dve.wait_ge(out_stored[r], 32 // BUFS * (i - r))
                    V.tensor_copy(out_no[r][:], rt[r][:, :, 4 * D]).then_inc(S["outno_ready"], 1)
                    dve.wait_ge(S["te_ready"], i + 1)
                    dve.wait_ge(S["fe_ready"], i + 1)
                    if not (start and r == 0):
                        dve.wait_ge(S["sg_ready"], i)
                    V.scalar_tensor_tensor(ge, te, 1.0, fe, ALU.add, ALU.mult).then_inc(S["ge_ready"], 1)
                    dve.wait_ge(S["sg_ready"], i + 1)
                    V.scalar_tensor_tensor(oo[r], sg, 0.5, rt[r][:, :, 3 * D:4 * D], ALU.mult,
                                           ALU.add).then_inc(S["oo_ready"], 1)

                expert_tiles(dve, combine)


def kernel(L0_attn_hidden_states, L0_attn_in_proj_w, L0_attn_conv_w, L0_attn_conv_b, L0_attn_ln_g, L0_attn_ln_b,
           L0_attn_fc_w, L0_attn_fc_b, L0_attn_cproj_w, L0_attn_cproj_b, L0_attn_out_w, L0_ffn_ln1_w, L0_ffn_ln1_b,
           L0_ffn_w_qkv, L0_ffn_w_proj, L0_ffn_ln2_w, L0_ffn_ln2_b, L0_ffn_gate_w, L0_ffn_gate_b, L0_ffn_w1,
           L0_ffn_w2):
    import concourse.bacc as bacc
    from concourse.bass_utils import run_bass_kernel_spmd

    def chunks(a):
        a = np.asarray(a)
        return np.ascontiguousarray(np.moveaxis(a.reshape(-1, P, *a.shape[1:]), 0, 1))

    in_proj = np.asarray(L0_attn_in_proj_w)
    conv_w = np.asarray(L0_attn_conv_w)
    per = conv_w.shape[1]
    blk = np.zeros((P, TAPS, NC, P), conv_w.dtype)
    for c in range(NC):
        for g in range(P // per):
            rows = slice(g * per, (g + 1) * per)
            blk[rows, :, c, rows] = conv_w[c * P + g * per:c * P + (g + 1) * per].transpose(1, 2, 0)
    col = lambda a: np.ascontiguousarray(np.asarray(a).reshape(-1, P).T)
    ones_pattern = np.zeros((P, HG), np.float32)
    for j in range(HG):
        ones_pattern[C_ROW + j, j] = 1.0
        ones_pattern[C_ROW + HG + j, j] = 1.0
    on_all = lambda a: np.ascontiguousarray(np.broadcast_to(np.asarray(a, np.float32), (P, len(a))))
    w1 = np.asarray(L0_ffn_w1)
    w2 = np.asarray(L0_ffn_w2)
    arrays = {
        "x": np.asarray(L0_attn_hidden_states),
        "w_h": chunks(in_proj[:CI]),
        "w_gT": np.ascontiguousarray(in_proj[CI:].T),
        "conv_blk": blk,
        "conv_b": col(L0_attn_conv_b),
        "ln_g": col(L0_attn_ln_g),
        "ln_b": col(L0_attn_ln_b),
        "fcT": chunks(np.asarray(L0_attn_fc_w).T),
        "fc_b": col(L0_attn_fc_b),
        "cproj": chunks(L0_attn_cproj_w),
        "cproj_b": col(L0_attn_cproj_b),
        "outT": chunks(np.asarray(L0_attn_out_w).T),
        "ln1_w": col(L0_ffn_ln1_w),
        "ln1_b": col(L0_ffn_ln1_b),
        "w_qkv": np.asarray(L0_ffn_w_qkv),
        "w_proj": np.asarray(L0_ffn_w_proj),
        "ln2_w": col(L0_ffn_ln2_w),
        "ln2_b": col(L0_ffn_ln2_b),
        "gate_w": np.asarray(L0_ffn_gate_w),
        "gate_b": np.ascontiguousarray(np.broadcast_to(np.asarray(L0_ffn_gate_b), (P, NE))),
        "w_exp": np.concatenate([w1, w2.reshape(NE, NHC, P, D).transpose(0, 2, 1, 3).reshape(NE, P, NHC * D)], 2),
        "ident": np.eye(P, dtype=np.float32),
        "ones_pattern": ones_pattern,
        "expert_rank": on_all(NE - np.arange(NE)),
        "segment_start": on_all(SEG * np.arange(NE)),
        "token_no": np.ascontiguousarray(np.arange(L, dtype=np.float32).reshape(NT, P).T),
        "before": np.triu(np.ones((P, P), np.float32), 1),
        "tile_no": on_all(np.arange(N_TILES)),
        "tile_edges": on_all(TILE * np.arange(N_TILES - NE)),
    }
    nc = bacc.Bacc("TRN2", target_bir_lowering=False, num_devices=1)
    ins = [nc.dram_tensor(f"{n}_dram", a.shape, mybir.dt.from_np(a.dtype), kind="ExternalInput").ap()
           for n, a in arrays.items()]
    out = nc.dram_tensor("out_dram", (NB, L, D), F32, kind="ExternalOutput").ap()
    fused_block(nc, ins, out)
    got = run_bass_kernel_spmd(nc, [{f"{n}_dram": a for n, a in arrays.items()}], core_ids=[0])
    return got.results[0]["out_dram"]
```

```python
from contextlib import ExitStack

import numpy as np

import concourse.bass as bass
from concourse import mybir

F32 = mybir.dt.float32
FR = mybir.dt.float32r
BF16 = mybir.dt.bfloat16
I32 = mybir.dt.int32
U32 = mybir.dt.uint32
ALU = mybir.AluOpType
ACT = mybir.ActivationFunctionType
AX = mybir.AxisListType

P = 128
EPS = 1e-5
NB, L, D = 8, 512, 128
NT = L // P
CI = 256
NC = CI // P
TAPS = 4
H = 16
DK = D // H
HG = 4
NG = H // HG
PADL = TAPS - 1
NE = 8
HID = 512
NHC = HID // P
SCALE = float(DK) ** -0.5
ROW = 4 * D + 1
SEG = NB * L + 2 * P
TILE = 2 * P
N_TILES = NB * L // TILE + NE
BUFS = 4
PASSES = N_TILES // BUFS
NO_TOKEN = 2.0 ** 20
N_ST = H * NT
EARLY = 24
NEXT_AT = 0
AHEAD = 38
M_TWO_BANKS = 48
C_END = 104
C_ROW = 96

FIRST = {"ident": P, "ones_pattern": HG, "ln1_w": 1, "ln1_b": 1, "w_qkv": 3 * D}
SETUP = {"conv_blk": TAPS * NC * P, "w_h": NC * D, "cproj": NC * D}
MAIN = {"w_gT": CI, "conv_b": NC, "ln_g": NC, "ln_b": NC, "fcT": NC * D, "fc_b": 1, "cproj_b": NC, "outT": NC * D,
        "w_proj": D, "ln2_w": 1, "ln2_b": 1, "gate_w": NE, "gate_b": NE, "expert_rank": NE, "segment_start": NE,
        "token_no": NT, "before": P, "tile_no": N_TILES, "tile_edges": N_TILES - NE}

HL_PRODUCTS = ((0, 0), (1, 0), (0, 1))


def fused_block(nc, ins, out):
    x, first_pack, setup_pack, main_pack, w_exp = ins

    x_v = x.rearrange("b (t p) d -> b p t d", p=P)
    out_v = out.rearrange("b (t p) d -> b p t d", p=P)
    qk_dram = nc.dram_tensor("qk_dram", [P, 4, L], F32, kind="Internal").ap()
    rows_dram = nc.dram_tensor("rows_dram", [NE * SEG + TILE, ROW], F32, kind="Internal").ap()
    out_rows = out.rearrange("b t d -> (b t) d")

    with ExitStack() as ctx:
        def sb(name, shape, dt=F32):
            return ctx.enter_context(nc.sbuf_tensor(name, shape, dt))

        def sem(name):
            return ctx.enter_context(nc.semaphore(name))

        ps = ctx.enter_context(nc.psum_tensor("ps", [P, 8, 512], F32))

        prob = sb("prob", [P, 2 * HG, NT, L])
        room = prob[:].rearrange("p a t n -> p (a t n)")
        n_setup = sum(SETUP.values())
        setup_sb = room[:, NG * HG * L:NG * HG * L + n_setup]
        fcg = room[:, NG * HG * L + n_setup:NG * HG * L + n_setup + NC * D].rearrange("p (c d) -> p c d", c=NC)
        first_sb = sb("first_sb", [P, sum(FIRST.values())])
        main_sb = sb("main_sb", [P, sum(MAIN.values())])
        loaded = {}
        for tile, pack in ((first_sb, FIRST), (setup_sb, SETUP), (main_sb, MAIN)):
            at = 0
            for name, width in pack.items():
                loaded[name] = tile[:, at:at + width]
                at += width

        def chunked(name):
            return loaded[name].rearrange("p (c d) -> p c d", c=NC)

        blk_sb = loaded["conv_blk"].rearrange("p (j c n) -> p j c n", j=TAPS, c=NC)
        w_h_sb, cproj_sb, fcT_sb, outT_sb = chunked("w_h"), chunked("cproj"), chunked("fcT"), chunked("outT")
        ident, pat_sb, wqkv_sb = loaded["ident"], loaded["ones_pattern"], loaded["w_qkv"]
        ln1w_sb, ln1b_sb, ln2w_sb, ln2b_sb = loaded["ln1_w"], loaded["ln1_b"], loaded["ln2_w"], loaded["ln2_b"]
        w_gT_sb, cb_sb, lng_sb, lnb_sb = loaded["w_gT"], loaded["conv_b"], loaded["ln_g"], loaded["ln_b"]
        fcb_sb, cpb_sb, wproj_sb = loaded["fc_b"], loaded["cproj_b"], loaded["w_proj"]
        gw_sb, gb_sb = loaded["gate_w"], loaded["gate_b"]
        erank_sb = loaded["expert_rank"]
        seg_sb, tok_sb, before_sb = loaded["segment_start"], loaded["token_no"], loaded["before"]
        tno_sb, edge_sb = loaded["tile_no"], loaded["tile_edges"]
        before_bf = sb("before_bf", [P, P], BF16)
        ones_bf = sb("ones_bf", [P, P], BF16)
        ones = sb("ones", [P, P])
        mean_w = sb("mean_w", [P, P])
        neg_half = sb("neg_half", [P, NT])
        wc = room[:, NG * HG * L + n_setup + NC * D:NG * HG * L + n_setup + NC * D + TAPS * CI]
        wc_hl = sb("wc_hl", [P, 2, TAPS, CI], FR)
        wg_hl = sb("wg_hl", [P, 2, CI], FR)
        half_cb = sb("half_cb", [P, NC])
        fcc = sb("fcc", [P, NC, D])
        fc_bias = sb("fc_bias", [P, 1])
        half_fcb = sb("half_fcb", [P, 1])
        w_so = sb("w_so", [P, D])
        s_bias = sb("s_bias", [P, 1])
        x_tok = sb("x_tok", [P, NT, D])
        x_st = sb("x_st", [P, NT, 6])
        x_mv = sb("x_mv", [P, NT, 2])
        x_ve = sb("x_ve", [P, NT])
        x_rs = sb("x_rs", [P, NT])
        x_tmp = sb("x_tmp", [P, 3, NT])
        x_r1 = sb("x_r1", [P, NT])
        xn = sb("xn", [P, NT, D])
        xn1 = sb("xn1", [P, NT, D])
        xnT_hl = sb("xnT_hl", [P, 2, PADL + L], FR)
        xn1T = sb("xn1T", [P, L])
        qk_hl = sb("qk_hl", [P, 4, L], FR)
        q_st = sb("q_st", [P, NG, L], FR)
        k_one = sb("k_one", [P, H, L], FR)
        v_sb = sb("v_sb", [P, NT, H, 32])
        th = sb("th", [P, NC, L])
        u = sb("u", [P, NC, L])
        hm = sb("hm", [P, NC, L])
        sq = th
        srow = sb("srow", [64, L])
        h_mean = sb("h_mean", [P, NT])
        h_msq = sb("h_msq", [P, NT])
        h_var = sb("h_var", [P, NT])
        h_ve = sb("h_ve", [P, NT])
        h_rs = sb("h_rs", [P, NT])
        diag = sb("diag", [P, NT, P])
        rbc = sb("rbc", [P, L])
        zr = sb("zr", [P, L])
        zb = sb("zb", [P, L])
        tz = sb("tz", [P, L])
        s1 = sb("s1", [P, L])
        sT = sb("sT", [P, L])
        mx = sb("mx", [P, NG, NT, HG])
        negc = sb("negc", [P, NG, NT, 2 * HG], FR)
        crow = sb("crow", [2 * HG, L], FR)
        yraw = sb("yraw", [P, L])
        rden = sb("rden", [P, NT, HG])
        ytok = sb("ytok", [P, NT, NG, HG, DK])
        xres = sb("xres", [P, NT, D])
        yTs = sb("yTs", [P, L])
        row = sb("row", [P, NT, ROW])
        xn2 = row[:, :, 0:D]
        x2 = row[:, :, D:2 * D]
        s_tok = row[:, :, 2 * D:3 * D]
        x_row = row[:, :, 3 * D:4 * D]
        no_row = row[:, :, 4 * D]
        no_now = sb("no_now", [P, NT])
        f_st = sb("f_st", [P, NT, 6])
        f_mv = sb("f_mv", [P, NT, 2])
        f_ve = sb("f_ve", [P, NT])
        f_rs = sb("f_rs", [P, NT])
        x3T = sb("x3T", [P, L])
        lg = sb("lg", [P, NT, NE])
        lg_top = sb("lg_top", [P, NT])
        lg_eq = sb("lg_eq", [P, NT, NE])
        lg_sc = sb("lg_sc", [P, NT, NE])
        lg_first = sb("lg_first", [P, NT])
        hot = sb("hot", [P, NT, NE], BF16)
        base = sb("base", [P, NE])
        place = sb("place", [P, NT, NE])
        place_hot = sb("place_hot", [P, NT, NE])
        slot_f = sb("slot_f", [P, NT])
        slot = sb("slot", [P, NT], U32)
        count = sb("count", [P, NE])
        tiles = sb("tiles", [P, NE])
        upto = sb("upto", [P, NE])
        zeros8 = sb("zeros8", [P, NE])
        t_exp = sb("t_exp", [P, N_TILES])
        t_off = sb("t_off", [P, N_TILES])
        t_row = sb("t_row", [P, N_TILES])
        t_row2 = sb("t_row2", [P, N_TILES])
        tile_row = sb("tile_row", [P, N_TILES], I32)
        tile_exp = sb("tile_exp", [P, N_TILES], I32)
        pad = sb("pad", [P, 2, ROW])
        pad_row = sb("pad_row", [P, NE], I32)
        used = 0
        def carve(shape):
            nonlocal used
            size = int(np.prod(shape))
            got = room[:, used:used + size]
            used += size
            if len(shape) == 2:
                got = got.rearrange("p (a b) -> p a b", a=shape[0])
            if len(shape) == 3:
                got = got.rearrange("p (a b c) -> p a b c", a=shape[0], b=shape[1])
            return got
        rt = [carve([2, ROW]) for _ in range(BUFS)]
        wt = [carve([2 * HID]) for _ in range(BUFS)]
        x3s = [carve([TILE]) for _ in range(2)]
        hT = carve([NHC, TILE])
        yTe = carve([TILE])
        fe = carve([2, D])
        te = carve([2, D])
        ge = carve([2, D])
        sg = carve([2, D])
        oo = [carve([2, D]) for _ in range(BUFS)]
        over = carve([NE, N_TILES - NE])
        past = carve([N_TILES, NE])
        past_n = carve([N_TILES, NE])
        out_no = [sb(f"out_no{r}", [P, 2], U32) for r in range(BUFS)]

        names = """
            parted first_loaded setup_loaded main_loaded setup_dve setup_pe setup_act w_high zeros_set ones_set
            x_loaded x_aggr x_var xp_chain x_r1 xn_part xn_ready xT_done xnT_high xnT_split xn1T_ready
            qk_done qk_high qk_split qk_spilled v_done v_ready
            gate_done tanh_ready u_ready conv_done hm_ready sq_ready sums_done srow_ready statT_done h_chain
            h_var_ready h_rs_ready diag_ready rbc_done rbc_ready z_done zr_ready zb_ready tz_ready s1_ready
            sT_done sT_ready stok_done stok_ready xrow_loaded norow_ready no_next
            m_done max_done negh_ready negc_ready cT_done crow_ready e_done exp_done pv_done yraw_ready yT_done
            rden_ready ynorm_ready
            xres_ready ytT_done yTs_ready proj_done x2_ready f_chain f_var_ready f_rs_ready xn2_ready
            xn2T_done x3T_ready lg_done r_chain hot_ready rank_done slotf_ready slot_ready base_ready scattered
            pad_set pad_row_ready tile_chain tiles_ready padded
            et_done x3s_ready hid_done hid_ready ye_done yTe_ready yt_done fe_ready te_ready ge_ready sg_ready
            oo_ready outno_ready""".split()
        S = {n: sem(n) for n in names}
        rt_loaded = [sem(f"rt_loaded{r}") for r in range(BUFS)]
        wt_loaded = [sem(f"wt_loaded{r}") for r in range(BUFS)]
        out_stored = [sem(f"out_stored{r}") for r in range(BUFS)]
        stacked = [sem(f"stacked{half}") for half in range(2)]
        c_placed = [sem(f"c_placed{g}") for g in range(NG)]

        def part(eng):
            eng.sem_inc(S["parted"])

        def expert_tiles(eng, step):
            for r in range(BUFS):
                step(r, r, True, False)
            with eng.Fori(1, PASSES - 1) as n:
                for r in range(BUFS):
                    step(n * BUFS + r, r, False, False)
            for r in range(BUFS):
                step((PASSES - 1) * BUFS + r, r, False, True)

        def loads_of(i, r):
            return 16 // BUFS * (i - r) + 16

        def m_bank(i):
            if i < EARLY:
                return i % 3
            return i % 2 if i < M_TWO_BANKS else (3, 0, 1)[(i - M_TWO_BANKS) % 3]

        def e_bank(n):
            return 4 + n % 2 if n < N_ST // 2 else (4, 5, 3)[(n - N_ST // 2) % 3]

        def early(step):
            return (EARLY - NT) * (step - NEXT_AT) // (HG * NT - NEXT_AT)

        def started(step):
            return EARLY + (N_ST // 2 - EARLY) * step // 8

        def scored(step):
            return AHEAD + (N_ST - AHEAD) * step // (2 * HG * NT)

        def batches(eng, body):
            body(0, True, False, False, 2)
            body(1, False, True, False, 2)
            with eng.Fori(2, NB - 2) as b:
                body(b, False, False, False, 2)
            body(NB - 2, False, False, False, 1)
            body(NB - 1, False, False, True, 0)

        with nc.Block() as block:

            @block.sync
            def _(sp):
                def load_x(b, first):
                    if not first:
                        sp.wait_ge(S["xn_ready"], b)
                    sp.dma_start(x_tok[:], x_v[b]).then_inc(S["x_loaded"], 16)

                def spill_qk(b, first):
                    sp.wait_ge(S["qk_split"], 2 * b + 2)
                    sp.dma_start(qk_dram, qk_hl[:].bitcast(F32)).then_inc(S["qk_spilled"], 16)

                def stack_qk(b, half, copies):
                    groups = slice(half * NG // 2, (half + 1) * NG // 2)
                    for copy in copies:
                        q_piece, k_piece = ((0, 2), (1, 2), (0, 3))[copy]
                        rows = slice(32 * copy, 32 * copy + 32)
                        src = qk_dram[:, q_piece, :].rearrange("(g r) n -> r g n", g=NG)[:, groups, :]
                        sp.dma_start(q_st[rows, groups, :].bitcast(F32), src).then_inc(stacked[half], 16)
                        for j in range(HG):
                            row = 32 * copy + DK * j
                            head_j = slice(DK * j, DK * j + DK)
                            src = qk_dram[:, k_piece, :].rearrange("(g r) n -> r g n", g=NG)[head_j, groups, :]
                            dst = k_one[row:row + DK].rearrange("p (g j) n -> p g j n", g=NG)[:, groups, j, :]
                            sp.dma_start(dst.bitcast(F32), src).then_inc(stacked[half], 16)

                def place_c(b, g):
                    sp.wait_ge(S["crow_ready"], NG * b + g + 1)
                    sp.dma_start(q_st[C_ROW:C_ROW + 2 * HG, g, :].bitcast(F32),
                                 crow[:].bitcast(F32)).then_inc(c_placed[g], 16)

                load_x(0, True)
                sp.dma_start(first_sb[:], first_pack).then_inc(S["first_loaded"], 16)
                sp.dma_start(setup_sb, setup_pack).then_inc(S["setup_loaded"], 16)
                sp.dma_start(main_sb[:], main_pack).then_inc(S["main_loaded"], 16)
                load_x(1, False)
                sp.wait_ge(S["pad_set"], 2)
                sp.dma_start(rows_dram[NE * SEG:NE * SEG + TILE, :].rearrange("(h p) r -> p h r", p=P),
                             pad[:]).then_inc(S["padded"], 16)
                spill_qk(0, True)
                sp.wait_ge(S["qk_spilled"], 16)
                sp.wait_ge(S["ones_set"], 5)
                stack_qk(0, 0, range(3))

                def body(b, first, second, last, left):
                    if not first:
                        part(sp)
                        sp.wait_ge(S["e_done"], N_ST * b)
                    stack_qk(b, 1, range(3))
                    place_c(b, 0)
                    place_c(b, 1)
                    if left == 2:
                        load_x(b + 2, False)
                    place_c(b, 2)
                    if not first:
                        sp.wait_ge(S["scattered"], 64 * b)
                    sp.dma_start(x_row, x_v[b]).then_inc(S["xrow_loaded"], 16)
                    if not last:
                        for half in range(2):
                            sp.wait_ge(stacked[half], 240 * b + 240)
                        spill_qk(b + 1, False)
                        sp.wait_ge(S["qk_spilled"], 16 * b + 32)
                        part(sp)
                        sp.wait_ge(S["e_done"], N_ST * b + N_ST // 2)
                        stack_qk(b + 1, 0, range(2))
                    place_c(b, 3)
                    if not last:
                        stack_qk(b + 1, 0, range(2, 3))

                batches(sp, body)

                sp.wait_ge(S["pad_row_ready"], 1)
                for e in range(NE):
                    at = sp.value_load(pad_row[0:1, e:e + 1], min_val=0, max_val=NE * SEG - TILE)
                    sp.dma_start(rows_dram[bass.ds(at, TILE), :].rearrange("(h p) r -> p h r", p=P),
                                 pad[:]).then_inc(S["padded"], 16)
                sp.wait_ge(S["padded"], 16 * (NE + 1))
                sp.wait_ge(S["scattered"], 64 * NB)
                sp.wait_ge(S["tiles_ready"], 2)

                def load_tile(i, r, start, end):
                    row_at = sp.value_load(tile_row[0:1, bass.ds(i, 1)], min_val=0, max_val=NE * SEG)
                    exp_at = sp.value_load(tile_exp[0:1, bass.ds(i, 1)], min_val=0, max_val=NE - 1)
                    if not start:
                        sp.wait_ge(S["oo_ready"], i - BUFS + 1)
                    sp.dma_start(rt[r], rows_dram[bass.ds(row_at, TILE), :].rearrange("(h p) r -> p h r", p=P))\
                        .then_inc(rt_loaded[r], 16)
                    if not start:
                        sp.wait_ge(S["ye_done"], i - BUFS + 1)
                    sp.dma_start(wt[r], w_exp[exp_at]).then_inc(wt_loaded[r], 16)

                expert_tiles(sp, load_tile)

            @block.tensor
            def _(pe):
                mm = nc.tensor.matmul
                tr = nc.tensor.transpose
                pe.wait_ge(S["setup_loaded"], 16)
                for j in range(TAPS):
                    for c in range(NC):
                        last = mm(ps[:, j // 2, (j % 2) * CI + c * P:(j % 2) * CI + (c + 1) * P], w_h_sb[:, c, :],
                                  blk_sb[:, j, c, :], start=True, stop=True, skip_group_check=True)
                last.then_inc(S["setup_pe"], 1)

                def p_xn(b):
                    pe.wait_ge(S["xn_part"], b + 1)
                    for t in range(NT):
                        last = tr(ps[:, 2, t * P:(t + 1) * P], xn[:, t, :], ident[:])
                    last.then_inc(S["xT_done"], 1)

                def p_xn1(b):
                    pe.wait_ge(S["xn_ready"], b + 1)
                    pe.wait_ge(S["xnT_split"], b + 1)
                    for t in range(NT):
                        last = tr(ps[:, 2, t * P:(t + 1) * P], xn1[:, t, :], ident[:])
                    last.then_inc(S["xT_done"], 1)

                def p_q(b):
                    pe.wait_ge(S["xn1T_ready"], b + 1)
                    mm(ps[:, 2, :], wqkv_sb[:, 0:D], xn1T[:], start=True, stop=True).then_inc(S["qk_done"], 1)

                def p_k(b):
                    pe.wait_ge(S["qk_split"], 2 * b + 1)
                    mm(ps[:, 2, :], wqkv_sb[:, D:2 * D], xn1T[:], start=True, stop=True).then_inc(S["qk_done"], 1)

                def p_v(b):
                    pe.wait_ge(S["max_done"], N_ST * b + EARLY)
                    for t in range(NT):
                        last = mm(ps[:, 2, t * D:(t + 1) * D], xn1T[:, t * P:(t + 1) * P], wqkv_sb[:, 2 * D:3 * D],
                                  start=True, stop=True, skip_group_check=True)
                    last.then_inc(S["v_done"], 1)

                def a_gate(b, c):
                    pe.wait_ge(S["xnT_split"], b + 1)
                    for n, (w, x_part) in enumerate(HL_PRODUCTS):
                        last = mm(ps[:, 4 + c, :], wg_hl[:, w, c * P:(c + 1) * P], xnT_hl[:, x_part, PADL:PADL + L],
                                  start=(n == 0), stop=(n == 2))
                    last.then_inc(S["gate_done"], 1)

                def a_tap(b, c, j):
                    for n, (w, x_part) in enumerate(HL_PRODUCTS):
                        last = mm(ps[:, 6 + c, :], wc_hl[:, w, j, c * P:(c + 1) * P], xnT_hl[:, x_part, j:j + L],
                                  start=(j == 0 and n == 0), stop=(j == TAPS - 1 and n == 2))
                    if j == TAPS - 1:
                        last.then_inc(S["conv_done"], 1)

                def a_sums(b, c):
                    if c == 0:
                        pe.wait_ge(S["hm_ready"], 2 * b + 2)
                        pe.wait_ge(S["u_ready"], 2 * b + 2)
                        pe.wait_ge(S["sq_ready"], 2 * b + 2)
                    mm(ps[0:32, 4, :], ones[:, 0:32], hm[:, c, :], start=(c == 0), stop=(c == NC - 1),
                       skip_group_check=True)
                    last = mm(ps[32:64, 4, :], ones[:, 0:32], sq[:, c, :], start=(c == 0), stop=(c == NC - 1),
                              skip_group_check=True)
                    if c == NC - 1:
                        last.then_inc(S["sums_done"], 1)

                def a_stat_transpose(b):
                    pe.wait_ge(S["srow_ready"], b + 1)
                    part(pe)
                    for t in range(NT):
                        last = tr(ps[:, 5, t * 64:(t + 1) * 64], srow[:, t * P:(t + 1) * P], ident[0:64, 0:64])
                    last.then_inc(S["statT_done"], 1)

                def a_z(b, c):
                    last = mm(ps[:, 6, :], fcc[:, c, :], hm[:, c, :], start=(c == 0), stop=(c == NC - 1))
                    if c == NC - 1:
                        last.then_inc(S["z_done"], 1)

                def a_rbc(b):
                    pe.wait_ge(S["diag_ready"], b + 1)
                    mm(ps[:, 7, :], ones[:], diag[:].rearrange("p t n -> p (t n)"), start=True,
                       stop=True).then_inc(S["rbc_done"], 1)

                def a_out(b, c):
                    if c < NC:
                        mm(ps[:, 7, :], outT_sb[:, c, :], hm[:, c, :], start=(c == 0), stop=False)
                    else:
                        pe.wait_ge(S["s1_ready"], b + 1)
                        mm(ps[:, 7, :], w_so[:], s1[:], start=False, stop=True).then_inc(S["sT_done"], 1)

                def a_s_transpose(b):
                    pe.wait_ge(S["sT_ready"], b + 1)
                    pe.wait_ge(S["zr_ready"], b + 1)
                    for t in range(NT):
                        last = tr(ps[:, 6, t * P:(t + 1) * P], sT[:, t * P:(t + 1) * P], ident[:])
                    last.then_inc(S["stok_done"], 1)

                def m_tiles(b, begin, end, first=False):
                    for i in range(begin, end):
                        head, t = i // NT, i % NT
                        if i == 2:
                            pe.wait_ge(S["qk_split"], 2 * b + 2)
                        elif i > M_TWO_BANKS or (i < EARLY and not (first and i < 2)):
                            pe.wait_ge(S["max_done"], N_ST * b + i - 2)
                        elif EARLY <= i < M_TWO_BANKS:
                            pe.wait_ge(S["max_done"], N_ST * b + i - 1)
                        mm(ps[:, m_bank(i), :], q_st[0:C_ROW, head // HG, t * P:(t + 1) * P], k_one[0:C_ROW, head, :],
                           start=True, stop=True).then_inc(S["m_done"], 1)

                def c_transpose(b, g):
                    pe.wait_ge(S["negc_ready"], NG * b + g + 1)
                    for t in range(NT):
                        last = tr(ps[0:2 * HG, 7, t * P:(t + 1) * P], negc[:, g, t, :].bitcast(F32), ident[:])
                    last.then_inc(S["cT_done"], 1)

                def e_step(b, first, g, k):
                    n = g * HG * NT + k
                    if n == N_ST // 2 + 2:
                        pe.wait_ge(S["max_done"], N_ST * (b + 1))
                    elif n > N_ST // 2 + 2:
                        pe.wait_ge(S["exp_done"], N_ST * b + n - 2)
                    elif not (first and n < 2):
                        pe.wait_ge(S["exp_done"], N_ST * b + n - 1)
                    mt = k % NT
                    mm(ps[:, e_bank(n), :], k_one[0:C_END, g * HG + k // NT, mt * P:(mt + 1) * P],
                       q_st[0:C_END, g, :], start=True, stop=True).then_inc(S["e_done"], 1)

                def pv(b, g, mt):
                    if mt == 0:
                        pe.wait_ge(S["exp_done"], H * NT * b + HG * NT * (g + 1))
                        if g > 0:
                            pe.wait_ge(S["yraw_ready"], NG * b + g)
                    for j in range(HG):
                        last = mm(ps[32 * j:32 * j + 32, 6, :], v_sb[:, mt, g * HG + j, :],
                                  prob[:, (g % 2) * HG + j, mt, :], start=(mt == 0), stop=(mt == NT - 1),
                                  skip_group_check=True)
                    if mt == NT - 1:
                        last.then_inc(S["pv_done"], 1)

                def y_transpose(b, g):
                    pe.wait_ge(S["yraw_ready"], NG * b + g + 1)
                    if g > 0:
                        pe.wait_ge(S["ynorm_ready"], NG * b + g)
                    for t in range(NT):
                        last = tr(ps[:, 7, t * P:(t + 1) * P], yraw[:, t * P:(t + 1) * P], ident[:])
                    last.then_inc(S["yT_done"], 1)

                def f_y(b):
                    pe.wait_ge(S["ynorm_ready"], NG * b + NG)
                    for t in range(NT):
                        last = tr(ps[:, 2, t * P:(t + 1) * P], ytok[:, t].rearrange("p g j d -> p (g j d)"), ident[:])
                    last.then_inc(S["ytT_done"], 1)

                def f_proj(b):
                    pe.wait_ge(S["yTs_ready"], b + 1)
                    for t in range(NT):
                        last = mm(ps[:, 3, t * D:(t + 1) * D], yTs[:, t * P:(t + 1) * P], wproj_sb[:], start=True,
                                  stop=True, skip_group_check=True)
                    last.then_inc(S["proj_done"], 1)

                def f_xn2(b):
                    pe.wait_ge(S["xn2_ready"], b + 1)
                    for t in range(NT):
                        last = tr(ps[:, 2, t * P:(t + 1) * P], xn2[:, t, :], ident[:])
                    last.then_inc(S["xn2T_done"], 1)

                def r_logits(b):
                    pe.wait_ge(S["x3T_ready"], b + 1)
                    for t in range(NT):
                        last = mm(ps[:, 3, t * NE:(t + 1) * NE], x3T[:, t * P:(t + 1) * P], gw_sb[:],
                                  start=True, stop=True, skip_group_check=True)
                    last.then_inc(S["lg_done"], 1)

                def r_ranks(b):
                    pe.wait_ge(S["hot_ready"], b + 1)
                    for t in range(NT):
                        at = (NT + t) * NE
                        for earlier in range(t):
                            mm(ps[:, 3, at:at + NE], ones_bf[:], hot[:, earlier, :], start=(earlier == 0),
                               stop=False, skip_group_check=True)
                        mm(ps[:, 3, at:at + NE], before_bf[:], hot[:, t, :], start=(t == 0), stop=True,
                           skip_group_check=True)
                    at = 2 * NT * NE
                    for t in range(NT):
                        last = mm(ps[:, 3, at:at + NE], ones_bf[:], hot[:, t, :], start=(t == 0), stop=(t == NT - 1),
                                  skip_group_check=True)
                    last.then_inc(S["rank_done"], 1)

                pe.wait_ge(S["first_loaded"], 16)
                p_xn(0)
                p_xn1(0)
                p_q(0)
                p_k(0)
                pe.wait_ge(S["main_loaded"], 16)
                pe.wait_ge(S["setup_dve"], 3)
                for c in range(NC):
                    last = mm(ps[:, 6, 0:D], mean_w[:], fcg[:, c, :], start=(c == 0), stop=(c == NC - 1))
                last.then_inc(S["setup_pe"], 1)
                for c in range(NC):
                    mm(ps[:, 3, 0:1], fcT_sb[:, c, :], lnb_sb[:, c:c + 1], start=(c == 0), stop=(c == NC - 1))
                for c in range(NC):
                    mm(ps[:, 4, 0:1], outT_sb[:, c, :], cpb_sb[:, c:c + 1], start=(c == 0), stop=(c == NC - 1))
                for c in range(NC):
                    last = mm(ps[:, 5, 0:D], cproj_sb[:, c, :], outT_sb[:, c, :], start=(c == 0), stop=(c == NC - 1))
                last.then_inc(S["setup_pe"], 1)
                pe.wait_ge(S["setup_dve"], 10)
                pe.wait_ge(S["setup_act"], 2)

                def a_start(b):
                    def scores(begin, end):
                        m_tiles(b, started(begin), started(end))

                    scores(0, 1)
                    a_gate(b, 0)
                    p_v(b)
                    scores(1, 2)
                    y_transpose(b - 1, NG - 1)
                    a_gate(b, 1)
                    scores(2, 3)
                    for j, begin, end in ((0, 3, 4), (1, 4, 4), (2, 4, 5), (3, 5, 6)):
                        a_tap(b, 0, j)
                        scores(begin, end)
                    pe.wait_ge(S["v_ready"], b + 1)
                    f_y(b - 1)
                    for j, begin, end in ((0, 6, 7), (1, 7, 7), (2, 7, 8), (3, 8, 8)):
                        a_tap(b, 1, j)
                        scores(begin, end)

                def body(b, first, second, last, left):
                    if not first:
                        y_transpose(b - 1, NG - 2)
                        pe.wait_ge(S["exp_done"], N_ST * b)
                    if first:
                        for c in range(NC):
                            a_gate(b, c)
                        for c in range(NC):
                            for j in range(TAPS):
                                a_tap(b, c, j)
                        pe.wait_ge(stacked[0], 240)
                        m_tiles(b, 0, 32, True)
                        p_v(b)
                    else:
                        a_start(b)
                    if not first:
                        f_proj(b - 1)
                    pe.wait_ge(stacked[1], 240 * b + 240)
                    m_tiles(b, 32, 33)
                    pe.wait_ge(S["hm_ready"], 2 * b + 2)
                    c_transpose(b, 0)
                    a_sums(b, 0)
                    m_tiles(b, 33, 34)
                    a_sums(b, 1)
                    m_tiles(b, 34, 35)
                    a_z(b, 0)
                    a_stat_transpose(b)
                    m_tiles(b, 35, 36)
                    a_z(b, 1)
                    m_tiles(b, 36, AHEAD)
                    pe.wait_ge(S["h_var_ready"], b + 1)
                    pe.wait_ge(S["srow_ready"], b + 1)
                    for g in range(NG):
                        pe.wait_ge(c_placed[g], 16 * b + 16)
                        for k in range(HG * NT):
                            e_step(b, first, g, k)
                            if g < 2:
                                begin, end = scored(g * HG * NT + k), scored(g * HG * NT + k + 1)
                                if begin <= M_TWO_BANKS < end and not first:
                                    pe.wait_ge(S["base_ready"], b + 1)
                                m_tiles(b, begin, end)
                            if g == 1 and k == 9:
                                pe.wait_ge(S["stok_ready"], b + 1)
                            if g == 1 and k > 8 and k % 2:
                                pv(b, 0, (k - 9) // 2)
                            if g > 1 and k % 4 == 3:
                                pv(b, g - 1, k // 4)
                            if (g, k) == (0, 2):
                                pe.wait_ge(S["crow_ready"], NG * b + 1)
                                a_rbc(b)
                            if (g, k) == (0, 1) and not first:
                                f_xn2(b - 1)
                            if (g, k) == (0, 4) and not first:
                                pe.wait_ge(S["x2_ready"], b)
                                r_logits(b - 1)
                            if (g, k) == (0, 9) and not first:
                                r_ranks(b - 1)
                            if (g, k) == (0, 6):
                                pe.wait_ge(S["rbc_ready"], b + 1)
                                c_transpose(b, 1)
                            if (g, k) == (0, 10):
                                pe.wait_ge(S["crow_ready"], NG * b + 2)
                            if (g, k) in ((0, 10), (0, 11), (0, 12)):
                                a_out(b, k - 10)
                            if (g, k) == (0, 15):
                                a_s_transpose(b)
                            if (g, k) == (1, 4):
                                c_transpose(b, 2)
                            if (g, k) == (2, 3):
                                pe.wait_ge(S["crow_ready"], NG * b + 3)
                                c_transpose(b, 3)
                            if not last:
                                if (g, k) == (0, 13):
                                    if not first:
                                        pe.wait_ge(S["x3T_ready"], b)
                                    p_xn(b + 1)
                                if (g, k) == (1, 2):
                                    p_xn1(b + 1)
                                if (g, k) == (1, 4):
                                    p_q(b + 1)
                                if (g, k) == (1, 8):
                                    p_k(b + 1)
                            if g > 1 and k == 8:
                                if g == 2:
                                    pe.wait_ge(S["crow_ready"], NG * b + NG)
                                y_transpose(b, g - 2)
                            if g == 3 and k >= NEXT_AT and not last:
                                if k == NEXT_AT:
                                    pe.wait_ge(stacked[0], 240 * b + 480)
                                m_tiles(b + 1, early(k), early(k + 1))
                    for mt in range(NT):
                        pv(b, NG - 1, mt)
                        if not last:
                            m_tiles(b + 1, EARLY - NT + mt, EARLY - NT + mt + 1)

                batches(pe, body)
                y_transpose(NB - 1, NG - 2)
                y_transpose(NB - 1, NG - 1)
                f_y(NB - 1)
                f_proj(NB - 1)
                f_xn2(NB - 1)
                r_logits(NB - 1)
                r_ranks(NB - 1)

                def e_transpose(i, r, start):
                    q = r % 2
                    pe.wait_ge(rt_loaded[r], loads_of(i, r))
                    if not (start and r < 2):
                        pe.wait_ge(S["x3s_ready"], i - 1)
                    for h in range(2):
                        last = tr(ps[:, q, h * P:(h + 1) * P], rt[r][:, h, 0:D], ident[:])
                    last.then_inc(S["et_done"], 1)

                def e_hidden(i, r, start):
                    pe.wait_ge(wt_loaded[r], loads_of(i, r))
                    pe.wait_ge(S["x3s_ready"], i + 1)
                    for k in range(NHC):
                        if k % 2 == 0 and not (start and r == 0):
                            pe.wait_ge(S["hid_ready"], 2 * i + k // 2 - 1)
                        last = mm(ps[:, 2 + k // 2, (k % 2) * TILE:(k % 2 + 1) * TILE], wt[r][:, k * P:(k + 1) * P],
                                  x3s[r % 2], start=True, stop=True, skip_group_check=True)
                        if k % 2:
                            last.then_inc(S["hid_done"], 1)

                def e_second(i, r, start):
                    if not (start and r < 2):
                        pe.wait_ge(S["yTe_ready"], i - 1)
                    for k in range(NHC):
                        if k % 2 == 0:
                            pe.wait_ge(S["hid_ready"], 2 * i + k // 2 + 1)
                        last = mm(ps[:, 4 + r % 2, 0:TILE], wt[r][:, HID + k * D:HID + (k + 1) * D], hT[:, k, :],
                                  start=(k == 0), stop=(k == NHC - 1))
                    last.then_inc(S["ye_done"], 1)

                def e_back(i, r, start):
                    pe.wait_ge(S["yTe_ready"], i + 1)
                    if not (start and r < 2):
                        pe.wait_ge(S["fe_ready"], i - 1)
                    part(pe)
                    for h in range(2):
                        last = tr(ps[:, 6 + r % 2, h * P:(h + 1) * P], yTe[:, h * P:(h + 1) * P], ident[:])
                    last.then_inc(S["yt_done"], 1)

                def tile(i, r, start, end):
                    e_hidden(i, r, start)
                    if not (start and r == 0):
                        e_back(i - 1, (r - 1) % BUFS, start)
                    if not (end and r == BUFS - 1):
                        e_transpose(i + 1, (r + 1) % BUFS, start and r + 1 < BUFS)
                    e_second(i, r, start)

                pe.wait_ge(S["base_ready"], NB + 1)
                e_transpose(0, 0, True)
                expert_tiles(pe, tile)
                e_back(N_TILES - 1, BUFS - 1, False)

            @block.scalar
            def _(act):
                A = nc.scalar.activation
                act.preload_act_table(ACT.Exp)
                act.wait_ge(S["setup_pe"], 1)
                A(wc, ps[:, 0:2, :].rearrange("p k n -> p (k n)"), ACT.Copy,
                  scale=0.5).then_inc(S["setup_act"], 1)

                def p_xT(b, first):
                    act.wait_ge(S["xT_done"], 2 * b + 1)
                    if not first:
                        act.wait_ge(S["conv_done"], 2 * b)
                    A(xnT_hl[:, 0, PADL:PADL + L], ps[:, 2, :], ACT.Copy).then_inc(S["xnT_high"], 1)

                def p_x1T(b, first):
                    act.wait_ge(S["xT_done"], 2 * b + 2)
                    if not first:
                        act.wait_ge(S["v_done"], b)
                    A(xn1T[:], ps[:, 2, :], ACT.Identity, bias=ln1b_sb[:], scale=ln1w_sb[:])\
                        .then_inc(S["xn1T_ready"], 1)

                def p_v(b, first):
                    act.wait_ge(S["v_done"], b + 1)
                    if first:
                        act.wait_ge(S["ones_set"], 4)
                    else:
                        act.wait_ge(S["pv_done"], NG * b)
                    for t in range(NT):
                        last = A(v_sb[:, t, :, 0:DK], ps[:, 2, t * D:(t + 1) * D].rearrange("p (h d) -> p h d", h=H),
                                 ACT.Copy)
                    last.then_inc(S["v_ready"], 1)

                p_xT(0, True)
                p_x1T(0, True)
                act.wait_ge(S["setup_pe"], 3)
                A(w_so[:], ps[:, 5, 0:D], ACT.Copy, scale=0.5).then_inc(S["setup_act"], 1)

                def exp_step(b, first, g, k):
                    n = g * HG * NT + k
                    act.wait_ge(S["e_done"], H * NT * b + n + 1)
                    if k == 0:
                        if g >= 2:
                            act.wait_ge(S["pv_done"], NG * b + g - 1)
                        elif not first:
                            act.wait_ge(S["pv_done"], NG * b + g - 1)
                    A(prob[:, (g % 2) * HG + k // NT, k % NT, :], ps[:, e_bank(n), :], ACT.Exp,
                      scale=SCALE).then_inc(S["exp_done"], 1)

                def y_copy(b, g, first):
                    act.wait_ge(S["pv_done"], NG * b + g + 1)
                    if not (first and g == 0):
                        act.wait_ge(S["yT_done"], NG * b + g)
                    A(yraw[:], ps[:, 6, :], ACT.Copy).then_inc(S["yraw_ready"], 1)

                def c_row(b, first, g):
                    act.wait_ge(S["cT_done"], NG * b + g + 1)
                    if g > 0:
                        act.wait_ge(c_placed[g - 1], 16 * b + 16)
                    elif not first:
                        act.wait_ge(c_placed[NG - 1], 16 * b)
                    A(crow[:], ps[0:2 * HG, 7, :], ACT.Copy).then_inc(S["crow_ready"], 1)

                def s_tanh(b, first):
                    act.wait_ge(S["zr_ready"], b + 1)
                    act.wait_ge(S["setup_dve"], 10)
                    if not first:
                        act.wait_ge(S["s1_ready"], b)
                    A(tz[:], zr[:], ACT.Tanh, bias=half_fcb[:], scale=0.5).then_inc(S["tz_ready"], 1)

                def s_bias_add(b, first):
                    act.wait_ge(S["sT_done"], b + 1)
                    act.wait_ge(S["setup_dve"], 10)
                    if not first:
                        act.wait_ge(S["stok_done"], b)
                    A(sT[:], ps[:, 7, :], ACT.Identity, bias=s_bias[:]).then_inc(S["sT_ready"], 1)

                def s_copy(b, first):
                    act.wait_ge(S["stok_done"], b + 1)
                    if not first:
                        act.wait_ge(S["scattered"], 64 * b)
                    A(s_tok, ps[:, 6, :].rearrange("p (t d) -> p t d", t=NT), ACT.Copy).then_inc(S["stok_ready"], 1)

                def f_yTs(b, first):
                    act.wait_ge(S["ytT_done"], b + 1)
                    if not first:
                        act.wait_ge(S["proj_done"], b)
                    A(yTs[:], ps[:, 2, :], ACT.Copy).then_inc(S["yTs_ready"], 1)

                def f_x3T(b, first):
                    act.wait_ge(S["xn2T_done"], b + 1)
                    if not first:
                        act.wait_ge(S["lg_done"], b)
                    A(x3T[:], ps[:, 2, :], ACT.Identity, bias=ln2b_sb[:], scale=ln2w_sb[:])\
                        .then_inc(S["x3T_ready"], 1)

                def body(b, first, second, last, left):
                    for c in range(NC):
                        act.wait_ge(S["gate_done"], 2 * b + c + 1)
                        if not first:
                            act.wait_ge(S["u_ready"], 2 * b)
                            act.wait_ge(S["sums_done"], b)
                        A(th[:, c, :], ps[:, 4 + c, :], ACT.Tanh, scale=0.5).then_inc(S["tanh_ready"], 1)
                    p_v(b, first)
                    if not first:
                        f_yTs(b - 1, second)
                    for c in range(NC):
                        act.wait_ge(S["hm_ready"], 2 * b + c + 1)
                        act.wait_ge(S["u_ready"], 2 * b + 2)
                        if not first:
                            act.wait_ge(S["sums_done"], b)
                        A(sq[:, c, :], hm[:, c, :], ACT.Square).then_inc(S["sq_ready"], 1)
                    c_row(b, first, 0)
                    act.wait_ge(S["sums_done"], b + 1)
                    if not first:
                        act.wait_ge(S["statT_done"], b)
                    A(srow[:], ps[0:64, 4, :], ACT.Copy).then_inc(S["srow_ready"], 1)
                    act.wait_ge(S["xn_ready"], b + 1)
                    if not first:
                        act.wait_ge(S["x2_ready"], b)
                    A(xres[:].rearrange("p t d -> p (t d)"), xn[:].rearrange("p t d -> p (t d)"),
                      ACT.Copy).then_inc(S["xres_ready"], 1)
                    for g in range(NG):
                        for k in range(HG * NT):
                            exp_step(b, first, g, k)
                            if (g, k) == (0, 1) and not first:
                                f_x3T(b - 1, second)
                            if (g, k) == (0, 2):
                                act.wait_ge(S["rbc_done"], b + 1)
                                if not first:
                                    act.wait_ge(S["zr_ready"], b)
                                A(rbc[:], ps[:, 7, :], ACT.Copy).then_inc(S["rbc_ready"], 1)
                            if (g, k) == (0, 6):
                                s_tanh(b, first)
                            if (g, k) in ((0, 7), (1, 5), (2, 4)):
                                c_row(b, first, g + 1)
                            if (g, k) == (0, 13):
                                s_bias_add(b, first)
                            if (g, k) == (0, 14) and not last:
                                p_xT(b + 1, False)
                            if (g, k) == (1, 3) and not last:
                                p_x1T(b + 1, False)
                            if (g, k) == (1, 7):
                                s_copy(b, first)
                            if g > 0 and k == HG * NT - 1:
                                y_copy(b, g - 1, first)
                    y_copy(b, NG - 1, first)

                batches(act, body)
                f_yTs(NB - 1, False)
                f_x3T(NB - 1, False)

                act.preload_act_table(ACT.Gelu_apprx_tanh)

                def x3_scale(i, r, start):
                    act.wait_ge(S["et_done"], i + 1)
                    if not (start and r < 2):
                        act.wait_ge(S["hid_done"], 2 * (i - 1))
                    A(x3s[r % 2], ps[:, r % 2, 0:TILE], ACT.Identity, bias=ln2b_sb[:], scale=ln2w_sb[:])\
                        .then_inc(S["x3s_ready"], 1)

                def gelu(i, r, start):
                    for half in range(2):
                        act.wait_ge(S["hid_done"], 2 * i + half + 1)
                        if half == 0 and not (start and r == 0):
                            act.wait_ge(S["ye_done"], i)
                        A(hT[:, 2 * half:2 * half + 2, :], ps[:, 2 + half, :].rearrange("p (k n) -> p k n", k=2),
                          ACT.Gelu_apprx_tanh).then_inc(S["hid_ready"], 1)

                def y_out(i, r, start):
                    act.wait_ge(S["ye_done"], i + 1)
                    if not (start and r == 0):
                        act.wait_ge(S["yt_done"], i)
                    A(yTe, ps[:, 4 + r % 2, 0:TILE], ACT.Copy).then_inc(S["yTe_ready"], 1)

                def tanh_half(i, r, start):
                    act.wait_ge(S["fe_ready"], i + 1)
                    if not (start and r == 0):
                        act.wait_ge(S["ge_ready"], i)
                    A(te, fe, ACT.Tanh, scale=0.5).then_inc(S["te_ready"], 1)

                def tile(i, r, start, end):
                    gelu(i, r, start)
                    if not (end and r == BUFS - 1):
                        x3_scale(i + 1, (r + 1) % BUFS, start and r + 1 < BUFS)
                    if not (start and r == 0):
                        tanh_half(i - 1, (r - 1) % BUFS, start and r > 0)
                    y_out(i, r, start)

                x3_scale(0, 0, True)
                expert_tiles(act, tile)
                tanh_half(N_TILES - 1, BUFS - 1, False)

            @block.gpsimd
            def _(pool):
                G = nc.gpsimd

                def p_rstd(b, first):
                    chain = 4 * b
                    pool.wait_ge(S["x_var"], b + 1)
                    if not first:
                        pool.wait_ge(S["xn_ready"], b)
                    G.tensor_tensor(x_rs[:], x_ve[:], neg_half[:], ALU.pow).then_inc(S["xp_chain"], 1)
                    pool.wait_ge(S["xp_chain"], chain + 1)
                    G.tensor_tensor(x_tmp[:, 0, :], x_mv[:, :, 1], x_rs[:], ALU.mult).then_inc(S["xp_chain"], 1)
                    pool.wait_ge(S["xp_chain"], chain + 2)
                    G.tensor_tensor(x_tmp[:, 1, :], x_tmp[:, 0, :], x_rs[:], ALU.mult).then_inc(S["xp_chain"], 1)
                    pool.wait_ge(S["xp_chain"], chain + 3)
                    part(pool)
                    G.tensor_scalar(x_tmp[:, 2, :], x_tmp[:, 1, :], EPS, None, ALU.add).then_inc(S["xp_chain"], 1)
                    pool.wait_ge(S["xp_chain"], chain + 4)
                    G.tensor_tensor(x_r1[:], x_tmp[:, 2, :], neg_half[:], ALU.pow).then_inc(S["x_r1"], 1)

                def scatter_rows(b):
                    pool.wait_ge(S["slot_ready"], b + 1)
                    pool.wait_ge(S["stok_ready"], b + 1)
                    pool.wait_ge(S["xrow_loaded"], 16 * b + 16)
                    pool.wait_ge(S["xn2_ready"], b + 1)
                    pool.wait_ge(S["norow_ready"], b + 1)
                    part(pool)
                    for t in range(NT):
                        G.indirect_dma_start(rows_dram, bass.IndirectOffsetOnAxis(slot[:, t:t + 1], 0), row[:, t, :],
                                             None, bounds_check=NE * SEG - 1, oob_is_err=False)\
                            .then_inc(S["scattered"], 16)

                G.memset(pad[:].rearrange("p h r -> p (h r)"), 0.0).then_inc(S["pad_set"], 1)
                pool.wait_ge(S["pad_set"], 1)
                G.memset(pad[:, :, 4 * D:4 * D + 1], NO_TOKEN).then_inc(S["pad_set"], 1)
                pool.wait_ge(S["ones_set"], 2)
                p_rstd(0, True)
                p_rstd(1, False)

                def f_rstd(b, first):
                    pool.wait_ge(S["f_var_ready"], b + 1)
                    if not first:
                        pool.wait_ge(S["xn2_ready"], b)
                    G.tensor_tensor(f_rs[:], f_ve[:], neg_half[:], ALU.pow).then_inc(S["f_rs_ready"], 1)

                def number_rows(b, first):
                    pool.wait_ge(S["no_next"], b + 1)
                    if not first:
                        pool.wait_ge(S["scattered"], 64 * b)
                    part(pool)
                    G.tensor_scalar(no_row, no_now[:], 1.0, None, ALU.mult).then_inc(S["norow_ready"], 1)
                    pool.wait_ge(S["norow_ready"], b + 1)
                    part(pool)
                    G.tensor_scalar(no_now[:], no_now[:], float(L), None, ALU.add).then_inc(S["no_next"], 1)

                def body(b, first, second, last, left):
                    if not first:
                        f_rstd(b - 1, second)
                    pool.wait_ge(S["h_var_ready"], b + 1)
                    if not first:
                        pool.wait_ge(S["diag_ready"], b)
                    G.tensor_tensor(h_rs[:], h_ve[:], neg_half[:], ALU.pow).then_inc(S["h_rs_ready"], 1)
                    pool.wait_ge(S["h_rs_ready"], b + 1)
                    if not first:
                        pool.wait_ge(S["rbc_done"], b)
                    G.tensor_tensor(diag[:], ident[:].rearrange("p (o n) -> p o n", o=1).to_broadcast([P, NT, P]),
                                    h_rs[:].rearrange("p (t o) -> p t o", o=1).to_broadcast([P, NT, P]),
                                    ALU.mult).then_inc(S["diag_ready"], 1)
                    pool.wait_ge(S["zr_ready"], b + 1)
                    if not first:
                        pool.wait_ge(S["s1_ready"], b)
                        part(pool)
                    G.tensor_scalar(zb[:], zr[:], fc_bias[:, 0:1], None, ALU.add).then_inc(S["zb_ready"], 1)
                    if not first:
                        number_rows(b - 1, second)
                        scatter_rows(b - 1)
                    if left == 2:
                        p_rstd(b + 2, False)

                pool.wait_ge(S["main_loaded"], 16)
                G.tensor_scalar(no_now[:], tok_sb[:], 1.0, None, ALU.mult).then_inc(S["no_next"], 1)
                batches(pool, body)
                f_rstd(NB - 1, False)
                number_rows(NB - 1, False)
                scatter_rows(NB - 1)

                def weigh_store(i, r, start, end):
                    pool.wait_ge(S["ge_ready"], i + 1)
                    if not (start and r == 0):
                        pool.wait_ge(S["oo_ready"], i)
                    G.tensor_tensor(sg, rt[r][:, :, 2 * D:3 * D], ge, ALU.mult).then_inc(S["sg_ready"], 1)
                    pool.wait_ge(S["oo_ready"], i + 1)
                    pool.wait_ge(S["outno_ready"], i + 1)
                    part(pool)
                    for h in range(2):
                        G.indirect_dma_start(out_rows, bass.IndirectOffsetOnAxis(out_no[r][:, h:h + 1], 0),
                                             oo[r][:, h, :], None, bounds_check=NB * L - 1, oob_is_err=False)\
                            .then_inc(out_stored[r], 16)

                expert_tiles(pool, weigh_store)
                for r in range(BUFS):
                    pool.wait_ge(out_stored[r], 32 * PASSES)

            @block.vector
            def _(dve):
                V = nc.vector

                def rows_alike(a, rows, cols):
                    return a.rearrange("p (o c) -> p o c", o=1).to_broadcast([P, rows, cols])

                def cols_alike(a, rows, cols):
                    return a.rearrange("p (r o) -> p r o", o=1).to_broadcast([P, rows, cols])

                V.memset(ones[:], 1.0).then_inc(S["ones_set"], 1)
                V.memset(neg_half[:], -0.5).then_inc(S["ones_set"], 1)
                V.memset(mean_w[:], 1.0 / CI).then_inc(S["setup_dve"], 1)
                V.memset(zeros8[:], 0.0).then_inc(S["zeros_set"], 1)
                dve.wait_ge(S["zeros_set"], 1)
                for high_low in range(2):
                    ins = V.tensor_copy(xnT_hl[:, high_low, 0:PADL], zeros8[:, 0:PADL])
                ins.then_inc(S["setup_dve"], 1)
                V.memset(v_sb[:].rearrange("p t h d -> p (t h d)"), 0.0).then_inc(S["ones_set"], 1)
                dve.wait_ge(S["ones_set"], 3)
                V.memset(v_sb[:, :, :, DK:DK + 1], 1.0).then_inc(S["ones_set"], 1)

                def k_patterns(g):
                    return V.tensor_copy(k_one[:, g * HG:(g + 1) * HG, :],
                                         pat_sb[:].rearrange("p (j o) -> p j o", o=1).to_broadcast([P, HG, L]))

                def p_stats(b, first):
                    dve.wait_ge(S["x_loaded"], 16 * b + 16)
                    if not first:
                        dve.wait_ge(S["xn_ready"], b)
                    for t in range(NT):
                        last = V.bn_stats(x_st[:, t, :], x_tok[:, t, :])
                    last.then_inc(S["x_aggr"], 1)
                    dve.wait_ge(S["x_aggr"], 2 * b + 1)
                    part(dve)
                    for t in range(NT):
                        last = V.bn_aggr(x_mv[:, t, :], x_st[:, t, :])
                    last.then_inc(S["x_aggr"], 1)
                    dve.wait_ge(S["x_aggr"], 2 * b + 2)
                    V.tensor_scalar(x_ve[:], x_mv[:, :, 1], EPS, None, ALU.add).then_inc(S["x_var"], 1)

                def x_split(b, first):
                    dve.wait_ge(S["xnT_high"], b + 1)
                    if not first:
                        dve.wait_ge(S["conv_done"], 2 * b)
                    V.tensor_tensor(xnT_hl[:, 1, PADL:PADL + L], ps[:, 2, :],
                                    xnT_hl[:, 0, PADL:PADL + L].bitcast(F32), ALU.subtract).then_inc(S["xnT_split"], 1)

                def p_split(b, first, i):
                    dve.wait_ge(S["qk_done"], 2 * b + i + 1)
                    if not first:
                        dve.wait_ge(S["qk_spilled"], 16 * b)
                    V.tensor_copy(qk_hl[:, 2 * i, :], ps[:, 2, :]).then_inc(S["qk_high"], 1)
                    dve.wait_ge(S["qk_high"], 2 * b + i + 1)
                    V.tensor_tensor(qk_hl[:, 2 * i + 1, :], ps[:, 2, :], qk_hl[:, 2 * i, :].bitcast(F32),
                                    ALU.subtract).then_inc(S["qk_split"], 1)

                def p_xn(b, first):
                    dve.wait_ge(S["x_r1"], b + 1)
                    if not first:
                        dve.wait_ge(S["xT_done"], 2 * b)
                        dve.wait_ge(S["xres_ready"], b)
                        dve.wait_ge(S["xn_ready"], b)
                        part(dve)
                    for t in range(NT):
                        last = V.tensor_scalar(xn[:, t, :], x_tok[:, t, :], x_mv[:, t, 0:1], x_rs[:, t:t + 1],
                                               ALU.subtract, ALU.mult)
                    last.then_inc(S["xn_part"], 1)

                def p_xn1(b):
                    dve.wait_ge(S["xn_part"], b + 1)
                    part(dve)
                    for t in range(NT):
                        last = V.tensor_scalar(xn1[:, t, :], xn[:, t, :], x_r1[:, t:t + 1], None, ALU.mult)
                    last.then_inc(S["xn_ready"], 1)

                p_stats(0, True)
                dve.wait_ge(S["first_loaded"], 16)
                for g in range(2):
                    k_patterns(g)
                p_xn(0, True)
                p_xn1(0)
                k_patterns(2)
                x_split(0, True)
                k_patterns(3).then_inc(S["ones_set"], 1)
                dve.wait_ge(S["main_loaded"], 16)
                V.tensor_tensor(fcg, fcT_sb[:], lng_sb[:].rearrange("p (c o) -> p c o", o=1).to_broadcast([P, NC, D]),
                                ALU.mult).then_inc(S["setup_dve"], 1)
                p_split(0, True, 0)
                p_split(0, True, 1)
                V.tensor_copy(before_bf[:], before_sb[:])
                V.tensor_copy(ones_bf[:], ones[:]).then_inc(S["ones_set"], 1)
                V.tensor_copy(base[:], seg_sb[:]).then_inc(S["base_ready"], 1)
                V.tensor_scalar(half_cb[:], cb_sb[:], 0.5, None, ALU.mult).then_inc(S["setup_dve"], 1)
                dve.wait_ge(S["setup_act"], 1)
                V.tensor_copy(wc_hl[:, 0].rearrange("p j c -> p (j c)"), wc)
                V.tensor_copy(wg_hl[:, 0], w_gT_sb[:]).then_inc(S["w_high"], 1)
                dve.wait_ge(S["w_high"], 1)
                V.tensor_tensor(wc_hl[:, 1].rearrange("p j c -> p (j c)"), wc,
                                wc_hl[:, 0].rearrange("p j c -> p (j c)").bitcast(F32), ALU.subtract)
                V.tensor_tensor(wg_hl[:, 1], w_gT_sb[:], wg_hl[:, 0].bitcast(F32),
                                ALU.subtract).then_inc(S["setup_dve"], 1)
                dve.wait_ge(S["setup_pe"], 3)
                V.tensor_tensor(fcc[:], fcg, rows_alike(ps[:, 6, 0:D], NC, D), ALU.subtract).then_inc(S["setup_dve"], 1)
                V.tensor_tensor(fc_bias[:], ps[:, 3, 0:1], fcb_sb[:], ALU.add).then_inc(S["setup_dve"], 1)
                V.tensor_copy(s_bias[:], ps[:, 4, 0:1]).then_inc(S["setup_dve"], 1)
                dve.wait_ge(S["setup_dve"], 8)
                V.tensor_scalar(half_fcb[:], fc_bias[:], 0.5, None, ALU.mult).then_inc(S["setup_dve"], 1)
                V.tensor_scalar(h_mean[:], ones[:, 0:NT], 0.0, None, ALU.mult).then_inc(S["setup_dve"], 1)
                dve.wait_ge(S["setup_dve"], 10)
                p_stats(1, False)

                def reduce_max(b, first, begin, end):
                    for i in range(begin, end):
                        head, t = i // NT, i % NT
                        dve.wait_ge(S["m_done"], N_ST * b + i + 1)
                        if i == 0 and not first:
                            dve.wait_ge(S["negc_ready"], NG * b)
                        V.tensor_reduce(mx[:, head // HG, t, head % HG:head % HG + 1], ps[:, m_bank(i), :], AX.X,
                                        ALU.max).then_inc(S["max_done"], 1)

                def split_max(b, first, g):
                    dve.wait_ge(S["max_done"], N_ST * b + 16 * (g + 1))
                    if not first:
                        dve.wait_ge(S["cT_done"], NG * b)
                    V.tensor_scalar(negc[:, g, :, 0:HG], mx[:, g, :, :], -1.0, None, ALU.mult)\
                        .then_inc(S["negh_ready"], 1)
                    dve.wait_ge(S["negh_ready"], NG * b + g + 1)
                    V.scalar_tensor_tensor(negc[:, g, :, HG:2 * HG], mx[:, g, :, :], -1.0,
                                           negc[:, g, :, 0:HG].bitcast(F32), ALU.mult, ALU.subtract)\
                        .then_inc(S["negc_ready"], 1)

                def y_norm(b, first, g):
                    dve.wait_ge(S["yT_done"], NG * b + g + 1)
                    if not (first and g == 0):
                        dve.wait_ge(S["ynorm_ready"], NG * b + g)
                    if g == 0 and not first:
                        dve.wait_ge(S["ytT_done"], b)
                    yv = ps[:, 7, :].rearrange("p (t j r) -> p t j r", t=NT, j=HG)
                    V.reciprocal(rden[:], yv[:, :, :, DK]).then_inc(S["rden_ready"], 1)
                    dve.wait_ge(S["rden_ready"], NG * b + g + 1)
                    V.tensor_tensor(ytok[:, :, g, :, :], yv[:, :, :, 0:DK],
                                    rden[:].rearrange("p t (j o) -> p t j o", o=1).to_broadcast([P, NT, HG, DK]),
                                    ALU.mult).then_inc(S["ynorm_ready"], 1)

                def f_stats(b, first):
                    dve.wait_ge(S["proj_done"], b + 1)
                    dve.wait_ge(S["xres_ready"], b + 1)
                    if not first:
                        dve.wait_ge(S["scattered"], 64 * b)
                        dve.wait_ge(S["xn2_ready"], b)
                    V.tensor_tensor(x2, ps[:, 3, :].rearrange("p (t d) -> p t d", t=NT), xres[:],
                                    ALU.add).then_inc(S["x2_ready"], 1)
                    dve.wait_ge(S["x2_ready"], b + 1)
                    for t in range(NT):
                        ins = V.bn_stats(f_st[:, t, :], x2[:, t, :])
                    ins.then_inc(S["f_chain"], 1)
                    dve.wait_ge(S["f_chain"], 2 * b + 1)
                    part(dve)
                    for t in range(NT):
                        ins = V.bn_aggr(f_mv[:, t, :], f_st[:, t, :])
                    ins.then_inc(S["f_chain"], 1)
                    dve.wait_ge(S["f_chain"], 2 * b + 2)
                    V.tensor_scalar(f_ve[:], f_mv[:, :, 1], EPS, None, ALU.add).then_inc(S["f_var_ready"], 1)

                def f_xn2(b, first):
                    dve.wait_ge(S["f_rs_ready"], b + 1)
                    if not first:
                        dve.wait_ge(S["xn2T_done"], b)
                    part(dve)
                    for t in range(NT):
                        ins = V.tensor_scalar(xn2[:, t, :], x2[:, t, :], f_mv[:, t, 0:1], f_rs[:, t:t + 1],
                                              ALU.subtract, ALU.mult)
                    ins.then_inc(S["xn2_ready"], 1)

                def a_u(b, first, c):
                    dve.wait_ge(S["tanh_ready"], 2 * b + c + 1)
                    if not first:
                        dve.wait_ge(S["hm_ready"], 2 * b)
                    V.scalar_tensor_tensor(u[:, c, :], th[:, c, :], 1.0, ps[:, 4 + c, :], ALU.add,
                                           ALU.mult).then_inc(S["u_ready"], 1)

                def a_hm(b, first, c):
                    dve.wait_ge(S["conv_done"], 2 * b + c + 1)
                    dve.wait_ge(S["u_ready"], 2 * b + c + 1)
                    if not first:
                        dve.wait_ge(S["sT_done"], b)
                        dve.wait_ge(S["sq_ready"], 2 * b)
                    V.scalar_tensor_tensor(hm[:, c, :], ps[:, 6 + c, :], half_cb[:, c:c + 1], u[:, c, :], ALU.add,
                                           ALU.mult).then_inc(S["hm_ready"], 1)

                def body(b, first, second, last, left):
                    chain = 3 * b
                    if first:
                        for c in range(NC):
                            a_u(b, first, c)
                        for c in range(NC):
                            a_hm(b, first, c)
                        reduce_max(b, first, 0, 16)
                        split_max(b, first, 0)
                        reduce_max(b, first, 16, 32)
                    else:
                        split_max(b, first, 0)
                        y_norm(b - 1, second, NG - 2)
                        reduce_max(b, first, EARLY, started(1))
                        a_u(b, first, 0)
                        reduce_max(b, first, started(1), started(2))
                        y_norm(b - 1, second, NG - 1)
                        a_u(b, first, 1)
                        reduce_max(b, first, started(2), started(5))
                        a_hm(b, first, 0)
                        reduce_max(b, first, started(5), started(8))
                        a_hm(b, first, 1)
                    split_max(b, first, 1)
                    reduce_max(b, first, 32, 33)
                    if not first:
                        f_stats(b - 1, second)
                    reduce_max(b, first, 33, 35)
                    dve.wait_ge(S["statT_done"], b + 1)
                    if not first:
                        dve.wait_ge(S["h_rs_ready"], b)
                    sums = ps[:, 5, 0:4 * 64].rearrange("p (t r) -> p t r", t=NT)
                    V.tensor_scalar(h_mean[:], sums[:, :, 0], 1.0 / CI, None, ALU.mult).then_inc(S["h_chain"], 1)
                    dve.wait_ge(S["h_chain"], chain + 1)
                    V.tensor_tensor(h_msq[:], h_mean[:], h_mean[:], ALU.mult).then_inc(S["h_chain"], 1)
                    dve.wait_ge(S["h_chain"], chain + 2)
                    V.scalar_tensor_tensor(h_var[:], sums[:, :, 32], 1.0 / CI, h_msq[:], ALU.mult,
                                           ALU.subtract).then_inc(S["h_chain"], 1)
                    dve.wait_ge(S["h_chain"], chain + 3)
                    V.tensor_scalar(h_ve[:], h_var[:], 0.0, EPS, ALU.max, ALU.add).then_inc(S["h_var_ready"], 1)
                    reduce_max(b, first, 35, 36)
                    if not first:
                        f_xn2(b - 1, second)
                    reduce_max(b, first, 36, 41)
                    dve.wait_ge(S["z_done"], b + 1)
                    dve.wait_ge(S["rbc_ready"], b + 1)
                    if not first:
                        dve.wait_ge(S["zb_ready"], b)
                    V.tensor_tensor(zr[:], ps[:, 6, :], rbc[:], ALU.mult).then_inc(S["zr_ready"], 1)
                    reduce_max(b, first, 41, 43)
                    if not first:
                        r_first(b - 1, second)
                    reduce_max(b, first, 43, 45)
                    dve.wait_ge(S["tz_ready"], b + 1)
                    dve.wait_ge(S["zb_ready"], b + 1)
                    if not first:
                        dve.wait_ge(S["sT_done"], b)
                    V.scalar_tensor_tensor(s1[:], tz[:], 1.0, zb[:], ALU.add, ALU.mult).then_inc(S["s1_ready"], 1)
                    reduce_max(b, first, 45, 46)
                    if not first:
                        r_place(b - 1, second)
                    reduce_max(b, first, 46, 47)
                    if not last:
                        p_xn(b + 1, False)
                    reduce_max(b, first, 47, 48)
                    split_max(b, first, 2)
                    if not last:
                        p_xn1(b + 1)
                    reduce_max(b, first, 48, 51)
                    if not last:
                        x_split(b + 1, False)
                    reduce_max(b, first, 51, 55)
                    if not last:
                        p_split(b + 1, False, 0)
                    reduce_max(b, first, 55, 59)
                    if not last:
                        p_split(b + 1, False, 1)
                    reduce_max(b, first, 59, N_ST)
                    split_max(b, first, 3)
                    if left == 2:
                        p_stats(b + 2, False)
                    y_norm(b, first, 0)
                    if not last:
                        reduce_max(b + 1, False, 0, early(8))
                    y_norm(b, first, 1)
                    if not last:
                        reduce_max(b + 1, False, early(8), EARLY)

                def step(ins, name, count):
                    ins.then_inc(S[name], 1)
                    dve.wait_ge(S[name], count)

                def r_first(b, first):
                    c = 7 * b
                    dve.wait_ge(S["lg_done"], b + 1)
                    step(V.tensor_tensor(lg[:], ps[:, 3, 0:NT * NE].rearrange("p (t e) -> p t e", t=NT),
                                         rows_alike(gb_sb[:], NT, NE), ALU.add), "r_chain", c + 1)
                    step(V.tensor_reduce(lg_top[:], lg[:], AX.X, ALU.max), "r_chain", c + 2)
                    step(V.tensor_tensor(lg_eq[:], lg[:], cols_alike(lg_top[:], NT, NE), ALU.is_equal),
                         "r_chain", c + 3)
                    step(V.tensor_tensor(lg_sc[:], lg_eq[:], rows_alike(erank_sb[:], NT, NE), ALU.mult),
                         "r_chain", c + 4)
                    step(V.tensor_reduce(lg_first[:], lg_sc[:], AX.X, ALU.max), "r_chain", c + 5)
                    if not first:
                        dve.wait_ge(S["rank_done"], b)
                    V.tensor_tensor(hot[:], lg_sc[:], cols_alike(lg_first[:], NT, NE), ALU.is_equal)\
                        .then_inc(S["hot_ready"], 1)

                def r_place(b, first):
                    c = 7 * b
                    ranks = ps[:, 3, NT * NE:2 * NT * NE]
                    totals = ps[:, 3, 2 * NT * NE:(2 * NT + 1) * NE]
                    dve.wait_ge(S["hot_ready"], b + 1)
                    dve.wait_ge(S["rank_done"], b + 1)
                    dve.wait_ge(S["base_ready"], b + 1)
                    V.tensor_tensor(place[:], ranks.rearrange("p (t e) -> p t e", t=NT),
                                    rows_alike(base[:], NT, NE), ALU.add).then_inc(S["r_chain"], 1)
                    dve.wait_ge(S["r_chain"], c + 6)
                    V.tensor_tensor(base[:], base[:], totals, ALU.add).then_inc(S["base_ready"], 1)
                    dve.wait_ge(S["base_ready"], b + 2)
                    V.tensor_tensor(place_hot[:], place[:], hot[:], ALU.mult).then_inc(S["r_chain"], 1)
                    dve.wait_ge(S["r_chain"], c + 7)
                    V.tensor_reduce(slot_f[:], place_hot[:], AX.X, ALU.add).then_inc(S["slotf_ready"], 1)
                    dve.wait_ge(S["slotf_ready"], b + 1)
                    if not first:
                        dve.wait_ge(S["scattered"], 64 * b)
                    V.tensor_copy(slot[:], slot_f[:]).then_inc(S["slot_ready"], 1)

                batches(dve, body)
                y_norm(NB - 1, False, NG - 2)
                y_norm(NB - 1, False, NG - 1)
                f_stats(NB - 1, False)
                f_xn2(NB - 1, False)
                r_first(NB - 1, False)
                r_place(NB - 1, False)

                dve.wait_ge(S["base_ready"], NB + 1)
                V.tensor_copy(pad_row[:], base[:]).then_inc(S["pad_row_ready"], 1)
                step(V.tensor_tensor(count[:], base[:], seg_sb[:], ALU.subtract), "tile_chain", 1)
                step(V.tensor_tensor(over, cols_alike(count[:], NE, N_TILES - NE),
                                     rows_alike(edge_sb[:], NE, N_TILES - NE), ALU.is_gt), "tile_chain", 2)
                step(V.tensor_reduce(tiles[:], over, AX.X, ALU.add), "tile_chain", 3)
                step(V.tensor_tensor_scan(upto[:], tiles[:], zeros8[:], 0.0, ALU.add, ALU.add), "tile_chain", 4)
                step(V.tensor_tensor(past, cols_alike(tno_sb[:], N_TILES, NE), rows_alike(upto[:], N_TILES, NE),
                                     ALU.is_ge), "tile_chain", 5)
                step(V.tensor_reduce(t_exp[:], past, AX.X, ALU.add), "tile_chain", 6)
                step(V.tensor_tensor(past_n, past, rows_alike(tiles[:], N_TILES, NE), ALU.mult), "tile_chain", 7)
                step(V.tensor_reduce(t_off[:], past_n, AX.X, ALU.add), "tile_chain", 8)
                step(V.tensor_tensor(t_row[:], tno_sb[:], t_off[:], ALU.subtract), "tile_chain", 9)
                step(V.tensor_scalar(t_row2[:], t_row[:], float(TILE), None, ALU.mult), "tile_chain", 10)
                step(V.scalar_tensor_tensor(t_row[:], t_exp[:], float(SEG), t_row2[:], ALU.mult, ALU.add),
                     "tile_chain", 11)
                V.tensor_scalar(tile_row[:], t_row[:], float(NE * SEG), None, ALU.min).then_inc(S["tiles_ready"], 1)
                V.tensor_scalar(tile_exp[:], t_exp[:], float(NE - 1), None, ALU.min).then_inc(S["tiles_ready"], 1)

                def combine(i, r, start, end):
                    dve.wait_ge(S["yt_done"], i + 1)
                    dve.wait_ge(rt_loaded[r], loads_of(i, r))
                    if not (start and r == 0):
                        dve.wait_ge(S["ge_ready"], i)
                    V.tensor_tensor(fe, ps[:, 6 + r % 2, 0:TILE].rearrange("p (h d) -> p h d", h=2),
                                    rt[r][:, :, D:2 * D], ALU.add).then_inc(S["fe_ready"], 1)
                    if not start:
                        dve.wait_ge(out_stored[r], 32 // BUFS * (i - r))
                    V.tensor_copy(out_no[r][:], rt[r][:, :, 4 * D]).then_inc(S["outno_ready"], 1)
                    dve.wait_ge(S["te_ready"], i + 1)
                    dve.wait_ge(S["fe_ready"], i + 1)
                    if not (start and r == 0):
                        dve.wait_ge(S["sg_ready"], i)
                    V.scalar_tensor_tensor(ge, te, 1.0, fe, ALU.add, ALU.mult).then_inc(S["ge_ready"], 1)
                    dve.wait_ge(S["sg_ready"], i + 1)
                    V.scalar_tensor_tensor(oo[r], sg, 0.5, rt[r][:, :, 3 * D:4 * D], ALU.mult,
                                           ALU.add).then_inc(S["oo_ready"], 1)

                expert_tiles(dve, combine)


def kernel(L0_attn_hidden_states, L0_attn_in_proj_w, L0_attn_conv_w, L0_attn_conv_b, L0_attn_ln_g, L0_attn_ln_b,
           L0_attn_fc_w, L0_attn_fc_b, L0_attn_cproj_w, L0_attn_cproj_b, L0_attn_out_w, L0_ffn_ln1_w, L0_ffn_ln1_b,
           L0_ffn_w_qkv, L0_ffn_w_proj, L0_ffn_ln2_w, L0_ffn_ln2_b, L0_ffn_gate_w, L0_ffn_gate_b, L0_ffn_w1,
           L0_ffn_w2):
    import concourse.bacc as bacc
    from concourse.bass_utils import run_bass_kernel_spmd

    def chunks(a):
        a = np.asarray(a)
        return np.ascontiguousarray(np.moveaxis(a.reshape(-1, P, *a.shape[1:]), 0, 1))

    in_proj = np.asarray(L0_attn_in_proj_w)
    conv_w = np.asarray(L0_attn_conv_w)
    per = conv_w.shape[1]
    blk = np.zeros((P, TAPS, NC, P), conv_w.dtype)
    for c in range(NC):
        for g in range(P // per):
            rows = slice(g * per, (g + 1) * per)
            blk[rows, :, c, rows] = conv_w[c * P + g * per:c * P + (g + 1) * per].transpose(1, 2, 0)
    col = lambda a: np.ascontiguousarray(np.asarray(a).reshape(-1, P).T)
    ones_pattern = np.zeros((P, HG), np.float32)
    for j in range(HG):
        ones_pattern[C_ROW + j, j] = 1.0
        ones_pattern[C_ROW + HG + j, j] = 1.0
    on_all = lambda a: np.ascontiguousarray(np.broadcast_to(np.asarray(a, np.float32), (P, len(a))))
    w1 = np.asarray(L0_ffn_w1)
    w2 = np.asarray(L0_ffn_w2)
    parts = {
        "w_h": chunks(in_proj[:CI]),
        "w_gT": np.ascontiguousarray(in_proj[CI:].T),
        "conv_blk": blk,
        "conv_b": col(L0_attn_conv_b),
        "ln_g": col(L0_attn_ln_g),
        "ln_b": col(L0_attn_ln_b),
        "fcT": chunks(np.asarray(L0_attn_fc_w).T),
        "fc_b": col(L0_attn_fc_b),
        "cproj": chunks(L0_attn_cproj_w),
        "cproj_b": col(L0_attn_cproj_b),
        "outT": chunks(np.asarray(L0_attn_out_w).T),
        "ln1_w": col(L0_ffn_ln1_w),
        "ln1_b": col(L0_ffn_ln1_b),
        "w_qkv": np.asarray(L0_ffn_w_qkv),
        "w_proj": np.asarray(L0_ffn_w_proj),
        "ln2_w": col(L0_ffn_ln2_w),
        "ln2_b": col(L0_ffn_ln2_b),
        "gate_w": np.asarray(L0_ffn_gate_w),
        "gate_b": np.ascontiguousarray(np.broadcast_to(np.asarray(L0_ffn_gate_b), (P, NE))),
        "ident": np.eye(P, dtype=np.float32),
        "ones_pattern": ones_pattern,
        "expert_rank": on_all(NE - np.arange(NE)),
        "segment_start": on_all(SEG * np.arange(NE)),
        "token_no": np.ascontiguousarray(np.arange(L, dtype=np.float32).reshape(NT, P).T),
        "before": np.triu(np.ones((P, P), np.float32), 1),
        "tile_no": on_all(np.arange(N_TILES)),
        "tile_edges": on_all(TILE * np.arange(N_TILES - NE)),
    }
    side_by_side = lambda names: np.concatenate([parts[n].reshape(P, -1) for n in names], 1)
    arrays = {
        "x": np.asarray(L0_attn_hidden_states),
        "first_pack": side_by_side(FIRST),
        "setup_pack": side_by_side(SETUP),
        "main_pack": side_by_side(MAIN),
        "w_exp": np.concatenate([w1, w2.reshape(NE, NHC, P, D).transpose(0, 2, 1, 3).reshape(NE, P, NHC * D)], 2),
    }
    nc = bacc.Bacc("TRN2", target_bir_lowering=False, num_devices=1)
    ins = [nc.dram_tensor(f"{n}_dram", a.shape, mybir.dt.from_np(a.dtype), kind="ExternalInput").ap()
           for n, a in arrays.items()]
    out = nc.dram_tensor("out_dram", (NB, L, D), F32, kind="ExternalOutput").ap()
    fused_block(nc, ins, out)
    got = run_bass_kernel_spmd(nc, [{f"{n}_dram": a for n, a in arrays.items()}], core_ids=[0])
    return got.results[0]["out_dram"]
```
